# Optimizing a Trainium2 kernel written in Bass

```python
import numpy as np
import jax
import jax.numpy as jnp

def _softmax(x, axis=-1):
    return jax.nn.softmax(x, axis=axis)

def _gelu(x):
    return jax.nn.gelu(x, approximate=True)

def _silu(x):
    return jax.nn.silu(x)

def _sigmoid(x):
    return jax.nn.sigmoid(x)

def _layernorm(x, axis=-1, eps=1e-05):
    m = jnp.mean(x, axis=axis, keepdims=True)
    v = jnp.var(x, axis=axis, keepdims=True)
    return (x - m) / jnp.sqrt(v + eps)

def _scatter_add(tgt, idx, src, axis=0):
    return tgt.at[idx].add(src)

def _segment_sum(src, seg, n):
    return jax.ops.segment_sum(src, seg, n)
kernel_name = 'mk_gps_d1_gnn_r8_5b1157'

def setup_inputs(seed: int=0):
    np.random.seed(seed)
    _w = jnp.asarray

    def _rec_inputs():
        import jax
        import jax.numpy as jnp
        _gk = jax.random.key(seed)
        x = -0.0002221 + 1 * jax.random.normal(jax.random.fold_in(_gk, 1), (1250, 768), jnp.float32)
        src = jax.random.randint(jax.random.fold_in(_gk, 2), (40000,), 0, 1250, jnp.int32)
        dst = jax.random.randint(jax.random.fold_in(_gk, 3), (40000,), 0, 1250, jnp.int32)
        _o = jnp.argsort(dst, stable=True)
        src = src[_o]
        dst = dst[_o]
        edge_type_3 = jax.random.randint(jax.random.fold_in(_gk, 12), (40000,), 0, 3, jnp.int32)
        return (x, src, dst, edge_type_3)
    x, src, dst, edge_type_3 = _rec_inputs()

    def _L0_gnn_setup():
        import jax, jax.numpy as jnp
        import numpy as np
        NEG_SLOPE = 0.2
        EPS = 1e-16
        N_NODES = 4096
        N_EDGES = 20000
        DIM = 768
        HEADS1 = 4
        OUT1 = DIM // HEADS1
        HEADS2 = 1
        OUT2 = DIM
        N_REL = 3

        def rgat_conv(x, W, q, k, b, src, dst, etype, heads, out_ch, n_nodes):
            xr = jnp.einsum('nd,rdf->rnf', x, W)
            oi = xr[etype, dst]
            oj = xr[etype, src]
            qi = oi @ q
            kj = oj @ k
            alpha = jax.nn.leaky_relu(qi + kj, NEG_SLOPE)
            m = jax.ops.segment_max(alpha, dst, num_segments=n_nodes)
            e = jnp.exp(alpha - m[dst])
            z = jax.ops.segment_sum(e, dst, num_segments=n_nodes)
            a = e / (z[dst] + EPS)
            msg = (a[:, :, None] * oj.reshape(-1, heads, out_ch)).reshape(-1, heads * out_ch)
            out = jax.ops.segment_sum(msg, dst, num_segments=n_nodes)
            return out + b
        key = jax.random.key(seed)
        ks = jax.random.split(key, 12)
        s = 0.02
        return {'x': jax.random.normal(ks[0], (N_NODES, DIM), dtype=jnp.float32), 'edge_index': jax.random.randint(ks[1], (2, N_EDGES), 0, N_NODES, dtype=jnp.int64), 'edge_type': jax.random.randint(ks[2], (N_EDGES,), 0, N_REL, dtype=jnp.int64), 'W1': jax.random.normal(ks[3], (N_REL, DIM, HEADS1 * OUT1), dtype=jnp.float32) * s, 'q1': jax.random.normal(ks[4], (HEADS1 * OUT1, HEADS1), dtype=jnp.float32) * s, 'k1': jax.random.normal(ks[5], (HEADS1 * OUT1, HEADS1), dtype=jnp.float32) * s, 'b1': jnp.zeros((HEADS1 * OUT1,), dtype=jnp.float32), 'W2': jax.random.normal(ks[6], (N_REL, DIM, HEADS2 * OUT2), dtype=jnp.float32) * s, 'q2': jax.random.normal(ks[7], (HEADS2 * OUT2, HEADS2), dtype=jnp.float32) * s, 'k2': jax.random.normal(ks[8], (HEADS2 * OUT2, HEADS2), dtype=jnp.float32) * s, 'b2': jnp.zeros((HEADS2 * OUT2,), dtype=jnp.float32)}
    _L0_gnn_all = _L0_gnn_setup()
    _L0_gnn_in = {k: v for k, v in _L0_gnn_all.items() if k in ('W1', 'q1', 'k1', 'b1', 'W2', 'q2', 'k2', 'b2')}
    del _L0_gnn_all

    def _L0_mix_setup():
        import jax, jax.numpy as jnp
        import numpy as np
        H = 12
        D = 64
        EPS = 1e-06

        def _phi(x):
            return jnp.where(x > 0, x + 1.0, jnp.exp(x))
        key = jax.random.key(seed)
        k1, k2, k3 = jax.random.split(key, 3)
        B, N, C = (4, 1024, 768)
        x = jax.random.normal(k1, (B, N, C), dtype=jnp.float32)
        W_qkv = jax.random.normal(k2, (C, 3 * C), dtype=jnp.float32) * C ** (-0.5)
        b_qkv = jnp.zeros((3 * C,), dtype=jnp.float32)
        W_out = jax.random.normal(k3, (C, C), dtype=jnp.float32) * C ** (-0.5)
        b_out = jnp.zeros((C,), dtype=jnp.float32)
        return {'x': x, 'W_qkv': W_qkv, 'b_qkv': b_qkv, 'W_out': W_out, 'b_out': b_out}
    _L0_mix_all = _L0_mix_setup()
    _L0_mix_in = {k: v for k, v in _L0_mix_all.items() if k in ('W_qkv', 'b_qkv', 'W_out', 'b_out')}
    del _L0_mix_all

    def _L0_ffn_setup():
        import jax, jax.numpy as jnp
        import numpy as np
        ACT_SCALE = 0.02
        W_SCALE = 0.01
        EFF_SCALE = ACT_SCALE * W_SCALE
        B, S, D, M = (8, 512, 768, 768)
        key = jax.random.key(seed)
        kx, kw, kb = jax.random.split(key, 3)
        x = jax.random.normal(kx, (B, S, D), dtype=jnp.float32)
        weight_t = jax.random.randint(kw, (D, M), -128, 128, dtype=jnp.int32).astype(jnp.int8)
        bias = jax.random.normal(kb, (M,), dtype=jnp.float32)
        return {'x': x, 'weight_t': weight_t, 'bias': bias}
    _L0_ffn_all = _L0_ffn_setup()
    _L0_ffn_in = {k: v for k, v in _L0_ffn_all.items() if k in ('weight_t', 'bias')}
    del _L0_ffn_all
    return {'x': x, 'src': src, 'dst': dst, 'edge_type_3': edge_type_3, 'L0_gnn_W1': _L0_gnn_in['W1'], 'L0_gnn_q1': _L0_gnn_in['q1'], 'L0_gnn_k1': _L0_gnn_in['k1'], 'L0_gnn_b1': _L0_gnn_in['b1'], 'L0_gnn_W2': _L0_gnn_in['W2'], 'L0_gnn_q2': _L0_gnn_in['q2'], 'L0_gnn_k2': _L0_gnn_in['k2'], 'L0_gnn_b2': _L0_gnn_in['b2'], 'L0_mix_W_qkv': _L0_mix_in['W_qkv'], 'L0_mix_b_qkv': _L0_mix_in['b_qkv'], 'L0_mix_W_out': _L0_mix_in['W_out'], 'L0_mix_b_out': _L0_mix_in['b_out'], 'L0_ffn_weight_t': _L0_ffn_in['weight_t'], 'L0_ffn_bias': _L0_ffn_in['bias']}

def reference(x, src, dst, edge_type_3, L0_gnn_W1, L0_gnn_q1, L0_gnn_k1, L0_gnn_b1, L0_gnn_W2, L0_gnn_q2, L0_gnn_k2, L0_gnn_b2, L0_mix_W_qkv, L0_mix_b_qkv, L0_mix_W_out, L0_mix_b_out, L0_ffn_weight_t, L0_ffn_bias):
    import jax
    import jax.numpy as jnp

    def _L0_gnn_ref(x, edge_index, edge_type, W1, q1, k1, b1, W2, q2, k2, b2):
        import jax, jax.numpy as jnp
        import numpy as np
        NEG_SLOPE = 0.2
        EPS = 1e-16
        N_NODES = 4096
        N_EDGES = 20000
        DIM = 768
        HEADS1 = 4
        OUT1 = DIM // HEADS1
        HEADS2 = 1
        OUT2 = DIM
        N_REL = 3

        def rgat_conv(x, W, q, k, b, src, dst, etype, heads, out_ch, n_nodes):
            xr = jnp.einsum('nd,rdf->rnf', x, W)
            oi = xr[etype, dst]
            oj = xr[etype, src]
            qi = oi @ q
            kj = oj @ k
            alpha = jax.nn.leaky_relu(qi + kj, NEG_SLOPE)
            m = jax.ops.segment_max(alpha, dst, num_segments=n_nodes)
            e = jnp.exp(alpha - m[dst])
            z = jax.ops.segment_sum(e, dst, num_segments=n_nodes)
            a = e / (z[dst] + EPS)
            msg = (a[:, :, None] * oj.reshape(-1, heads, out_ch)).reshape(-1, heads * out_ch)
            out = jax.ops.segment_sum(msg, dst, num_segments=n_nodes)
            return out + b
        src, dst = (edge_index[0], edge_index[1])
        n = x.shape[0]
        h = rgat_conv(x, W1, q1, k1, b1, src, dst, edge_type, HEADS1, OUT1, n)
        h = jax.nn.elu(h)
        out = rgat_conv(h, W2, q2, k2, b2, src, dst, edge_type, HEADS2, OUT2, n)
        return out

    def _L0_mix_ref(x, W_qkv, b_qkv, W_out, b_out):
        import jax, jax.numpy as jnp
        import numpy as np
        H = 12
        D = 64
        EPS = 1e-06

        def _phi(x):
            return jnp.where(x > 0, x + 1.0, jnp.exp(x))
        B, N, C = x.shape
        qkv = x @ W_qkv + b_qkv
        qkv = qkv.reshape(B, N, 3, H, D).transpose(2, 0, 3, 1, 4)
        q, k, v = (qkv[0], qkv[1], qkv[2])
        qf = _phi(q)
        kf = _phi(k)
        kv = jnp.einsum('bhnd,bhne->bhde', kf.astype(jnp.float32), v.astype(jnp.float32)).astype(v.dtype)
        y_num = jnp.einsum('bhnd,bhde->bhne', qf, kv)
        z = kf.astype(jnp.float32).sum(axis=2)
        y_den = jnp.einsum('bhnd,bhd->bhn', qf, z.astype(qf.dtype))
        y_den = jnp.maximum(y_den[..., None], EPS)
        y = (y_num / y_den).transpose(0, 2, 1, 3).reshape(B, N, C)
        return y @ W_out + b_out

    def _L0_ffn_ref(x, weight_t, bias):
        import jax, jax.numpy as jnp
        import numpy as np
        ACT_SCALE = 0.02
        W_SCALE = 0.01
        EFF_SCALE = ACT_SCALE * W_SCALE
        B, S, D, M = (8, 512, 768, 768)
        orig_shape = x.shape
        x_flat = x.reshape(-1, orig_shape[-1])
        x_int8 = jnp.clip(jnp.round(x_flat / ACT_SCALE), -128, 127).astype(jnp.int8)
        acc_i32 = jnp.matmul(x_int8, weight_t, preferred_element_type=jnp.int32)
        out = acc_i32.astype(jnp.float32) * jnp.float32(EFF_SCALE) + bias
        return out.reshape(orig_shape[:-1] + (M,))
    edge_index = jnp.stack([src, dst])
    xn = _layernorm(x, axis=-1)
    x = x + _L0_gnn_ref(xn, edge_index, edge_type_3, L0_gnn_W1, L0_gnn_q1, L0_gnn_k1, L0_gnn_b1, L0_gnn_W2, L0_gnn_q2, L0_gnn_k2, L0_gnn_b2) + _L0_mix_ref(xn[None], L0_mix_W_qkv, L0_mix_b_qkv, L0_mix_W_out, L0_mix_b_out)[0]
    x = x + _L0_ffn_ref(_layernorm(x, axis=-1)[None], L0_ffn_weight_t, L0_ffn_bias)[0]
    return x

_drawn_inputs = setup_inputs


def setup_inputs(seed=0):
    import zlib

    import numpy as np

    out = dict(_drawn_inputs(seed))
    spreads = {'L0_gnn_b1': (0.0, 0.1),
     'L0_gnn_b2': (0.0, 0.1),
     'L0_mix_b_qkv': (0.0, 0.1),
     'L0_mix_b_out': (0.0, 0.1)}
    factors = {'L0_gnn_W1': 4.827, 'L0_gnn_q1': 8.0, 'L0_gnn_k1': 8.0, 'L0_gnn_q2': 8.0, 'L0_gnn_k2': 8.0}
    for name, (base, spread) in spreads.items():
        noise = np.random.default_rng([zlib.crc32(name.encode()), seed]).standard_normal(out[name].shape)
        drawn = base * np.exp(spread * noise) if base else spread * noise
        out[name] = jnp.asarray(drawn.astype(out[name].dtype))
    for name, factor in factors.items():
        out[name] = (out[name] * factor).astype(out[name].dtype)
    return out
```

```python
from contextlib import ExitStack

import concourse.bass as bass
from concourse import mybir

F32 = mybir.dt.float32
F16 = mybir.dt.float16
BF16 = mybir.dt.bfloat16
I32 = mybir.dt.int32
I8 = mybir.dt.int8
U16 = mybir.dt.uint16
ALU = mybir.AluOpType
ACT = mybir.ActivationFunctionType
AX = mybir.AxisListType
ds = bass.ds

P = 128
N = 1250
D = 768
E = 40000
R = 3
H = 4
HD = D // H
K6 = D // P
NB = -(-N // P)
NPAD = NB * P
TAIL = N - (NB - 1) * P
WD = 42
WK = WD * R
NW = -(-N // WD)
ND = NW * WD
DB = 3 * WD
NDB = ND // DB
DTAIL = N - (NDB - 1) * DB
ET = 125
NT = E // ET
CW = 384
XH = 2 * HD + 2
XR2 = 2 * D + 2
DOTS2 = 2 * K6
V2_0 = 2 * H * R * NB
NRG = 4
RG = NPAD // NRG
BIG = -1e30
GW = 2 * DB
NG = ND // GW
DOTS = 2 * H * K6
OHS = 4
MAGIC = 12582912.0


def build(nc, x, src, dst, et, W1, q1, k1, b1, W2, q2, k2, b2, Wqkv, bqkv, Wo, bo, wf, bf, out):
    ctx = ExitStack()
    with ctx:
        def sem(name):
            return ctx.enter_context(nc.semaphore(name))

        base = 16512
        used = [base]

        def keep(name, shape, dt, size):
            n = size
            for s in shape[1:]:
                n *= s
            t = nc.alloc_sbuf_tensor_at(name, shape, dt, offset=used[0])
            used[0] += -(-n // 32) * 32
            return t

        def place(name, shape, dt, offset):
            return nc.alloc_sbuf_tensor_at(name, shape, dt, offset=base + 9216 + -(-offset // 32) * 32)

        ident = keep("ident", [P, P], F32, 4)
        ident16 = keep("ident16", [P, P], F16, 2)
        iota_s = keep("iota_s", [P, ND], F16, 2)
        iota_k = keep("iota_k", [P, WK], F16, 2)
        neg_w = keep("neg_w", [P, NW], F32, 4)
        kcol = keep("kcol", [P, NB, R * H], F32, 4)
        kcol_leak = keep("kcol_leak", [P, NB, R * H], F32, 4)
        mkt = keep("mkt", [P, H, NW], F32, 4)
        stat = keep("stat", [P, 2, 2, 6], F32, 4)
        mv = keep("mv", [P, 2, 2], F32, 4)
        rstd = keep("rstd", [P, 2, 1], F32, 4)
        bq_col = keep("bq_col", [P, K6], F32, 4)
        cst = keep("cst", [P, 4], F32, 4)
        vare = keep("vare", [P, 2, 1], F32, 4)
        tick = keep("tick", [P, 2], F32, 4)
        ones = keep("ones", [P, P], F32, 4)
        tabrow = keep("tabrow", [1, 4 * 32], I32, 4)
        assert used[0] <= base + 9216, used

        xt_hi = place("xt_hi", [P, K6, NPAD], F16, 0)
        xt_lo = place("xt_lo", [P, K6, NPAD], F16, 15360)
        wst = [place(f"wst{j}", [P, K6, CW], F32, 30720 + 9216 * j) for j in range(2)]
        w_hi = [place(f"w_hi{j}", [P, K6, CW], F16, 49152 + 4608 * j) for j in range(2)]
        w_lo = [place(f"w_lo{j}", [P, K6, CW], F16, 58368 + 4608 * j) for j in range(2)]
        X = place("X", [P, NB, D], F32, 67584)
        KF = place("KF", [P, NB, D], F32, 98304)
        V = place("V", [P, NB, K6, P + 1], F32, 129024)
        QF = place("QF", [P, K6, NPAD], F32, 159984)
        xn = [place(f"xn{j}", [P, D], F32, 159984 + 3072 * j) for j in range(2)]
        ev_t = [place(f"ev_t{j}", [P, CW], F32, 166400 + 1536 * j) for j in range(2)]
        ev_m = [place(f"ev_m{j}", [P, CW], F32, 169600 + 1536 * j) for j in range(2)]
        yt_hi = place("yt_hi", [P, K6, NPAD], F16, 98304)
        yt_lo = place("yt_lo", [P, K6, NPAD], F16, 98304 + 15360)
        q_t = [place(f"q_t{j}", [P, RG], F32, 129024 + 1280 * j) for j in range(2)]
        q_m = [place(f"q_m{j}", [P, RG], F32, 131584 + 1280 * j) for j in range(2)]
        kvd = place("kvd", [P, K6, P], F32, 134144)
        zd = place("zd", [P, K6, P], F32, 137216)
        den = [place(f"den{j}", [P, RG], F32, 140288 + 1280 * j) for j in range(2)]
        yv = [place(f"yv{j}", [P, RG], F32, 142848 + 1280 * j) for j in range(2)]
        ao = [place(f"ao{j}", [P, CW], F32, 145408 + 1536 * j) for j in range(2)]
        bk_bc = place("bk_bc", [P, 2 * D], F32, 190704)
        bsum = place("bsum", [P, D], F32, 196848)
        b2_bc0 = place("b2_bc0", [P, D], F32, 199936)
        ev = [place(f"ev{j}", [P, 2, 2, HD], F16, 67584 + 1536 * j) for j in range(2)]
        ev2 = [place(f"ev2_{j}", [P, 2, CW], F16, 67584 + 1536 * j) for j in range(2)]
        qk_bc = place("qk_bc", [P, 2 * H, D], F32, 70656)
        dot_junk = [place(f"dot_junk{j}", [P, CW], BF16, 95232 + 768 * j) for j in range(2)]
        wqk_p = place("wqk_p", [P, 2, K6, 2 * R * H], F32, 96768)
        wqk = place("wqk", [P, K6, 2 * R * H], F32, 97920)
        wqk_hi = place("wqk_hi", [P, K6, 2 * R * H], F16, 98496)
        wqk_lo = place("wqk_lo", [P, K6, 2 * R * H], F16, 98784)
        kq = place("kq", [2 * R * H, NPAD], F32, 99072)
        hn = [place(f"hn{j}", [P, D], F32, 104192 + 3072 * j) for j in range(2)]
        CT = place("CT", [P, NB, R, ND], U16, 124160)
        assert 124160 + NB * R * ND * 2 <= 202600
        oh_s = place("oh_s", [P, OHS, ND], F16, 0)
        oh_k = place("oh_k", [P, OHS, P], F16, 10240)
        c_row = [place(f"c_row{j}", [P, ND], F32, 11264 + 5120 * j) for j in range(2)]
        mb = [place(f"mb{j}", [P, ND], BF16, 21504 + 2560 * j) for j in range(2)]
        kbc = place("kbc", [P, H, ND], F32, 26624)
        tt_junk = [place(f"tt_junk{j}", [P, ND], BF16, 89120 + 2560 * j) for j in range(H)]
        e_int = place("e_int", [P, 3, 3, ET], I32, 49400)
        e_flt = place("e_flt", [P, 3, 3, ET], F32, 53920)
        e_key = place("e_key", [P, 3, ET], F32, 58432)
        tmm = place("tmm", [P, 3, 2], F32, 59936)
        tbc = place("tbc", [P, 3, 2, 32], F32, 59968)
        srow = place("srow", [32, 2, NT], F32, 60736)
        wlo = place("wlo", [32, 2], F32, 63296)
        tix = place("tix", [32, 2, NT], F32, 63328)
        ovl = place("ovl", [32, NT], F32, 65888)
        wrk = place("wrk", [32, NT], F32, 67168)
        tab = place("tab", [32, 8], F32, 68448)
        tabi = place("tabi", [32, 4], I32, 68512)
        ltri = place("ltri", [32, 32], F32, 68544)
        keyT = place("keyT", [P, 2 * NT], F32, 84000)
        srcT = place("srcT", [P, 2 * NT], F32, 86560)
        mk4 = [place(f"mk4_{j}", [P, H], F32, 68672 + 32 * j) for j in range(2)]
        qr = place("qr", [32, R * H, WD], F32, 70656)
        mr = place("mr", [32, H, WK], F32, 72672)
        al = place("al", [32, R, H, WD], F32, 74688)
        al2 = place("al2", [32, R, H, WD], F32, 76704)
        mx = place("mx", [32, H, WD], F32, 78720)
        mx2 = place("mx2", [32, H, WD], F32, 79392)
        tq = place("tq", [32, 2, R * H, WD], F32, 80064)
        xrh = [place(f"xrh{j}", [P, R, NB, XH], F16, 23168 * j) for j in range(2)]
        qbc = [place(f"qbc{j}", [P, 2, ND], F32, 46336 + 10080 * j) for j in range(2)]
        vb = [place(f"vb{j}", [P, ND], F32, 66496 + 5056 * j) for j in range(2)]
        pf = [place(f"pf{j}", [P, ND], F32, 76608 + 5056 * j) for j in range(2)]
        ph = [place(f"ph{j}", [P, ND + 4], F16, 86720 + 2528 * j) for j in range(2)]
        pl = [place(f"pl{j}", [P, ND + 4], F16, 91776 + 2528 * j) for j in range(2)]
        he = place("he", [P, NDB, HD + 1], F32, 96832)
        he_z = place("he_z", [P, NDB, 1], F32, 104608)
        he_m = place("he_m", [P, NDB, HD], F32, 104704)
        he_e = place("he_e", [P, NDB, HD], F32, 112384)
        b1_bc = place("b1_bc", [P, D], F32, 120064)
        assert 120064 + 3072 <= 124160
        x2 = place("x2", [P, R, NB, XR2], F16, 0)
        qb2 = [place(f"qb2_{j}", [P, 2, R, GW], F32, 92288 + 6048 * j) for j in range(2)]
        v2 = [place(f"v2_{j}", [P, GW], F32, 104384 + 1024 * j) for j in range(2)]
        p2 = [place(f"p2_{j}", [P, GW], F32, 106432 + 1024 * j) for j in range(2)]
        ph2 = [place(f"ph2_{j}", [P, GW + 4], F16, 108480 + 512 * j) for j in range(2)]
        pl2 = [place(f"pl2_{j}", [P, GW + 4], F16, 109504 + 512 * j) for j in range(2)]
        ot = [place(f"ot{j}", [P, D], F32, 110528 + 3072 * j) for j in range(2)]
        ac = [place(f"ac{j}", [P, D], F32, 116672 + 3072 * j) for j in range(2)]
        oz = [place(f"oz{j}", [P, 2], F32, 122816 + 32 * j) for j in range(2)]
        kbc2 = place("kbc2", [P, ND], F32, 92288)
        mb2 = [place(f"mb2_{j}", [P, ND], BF16, 97344 + 2560 * j) for j in range(2)]
        tt_junk2 = [place(f"tt_junk2_{j}", [P, ND], BF16, 102464 + 2560 * j) for j in range(2)]
        qr2 = place("qr2", [32, R, WD], F32, 110528)
        mr2 = place("mr2", [32, 1, WK], F32, 111040)
        al_2 = place("al_2", [32, R, 1, WD], F32, 111552)
        al2_2 = place("al2_2", [32, R, 1, WD], F32, 112064)
        mx_2 = place("mx_2", [32, 1, WD], F32, 112576)
        mx2_2 = place("mx2_2", [32, 1, WD], F32, 112768)
        tq2 = place("tq2", [32, 2, R, WD], F32, 112960)
        mk2 = [place(f"mk2_{j}", [P, 1], F32, 114016 + 32 * j) for j in range(2)]
        wf8 = place("wf8", [P, K6, D // 4], I32, 0)
        wf16 = place("wf16", [P, K6, D], F16, 4608)
        bf_bc = place("bf_bc", [P, D], F32, 13824)
        fx = [place(f"fx{j}", [P, D], F32, 16896 + 3072 * j) for j in range(2)]
        fn = [place(f"fn{j}", [P, D], F32, 23040 + 3072 * j) for j in range(2)]
        fq = [place(f"fq{j}", [P, D], F16, 29184 + 1536 * j) for j in range(2)]
        fqt = [place(f"fqt{j}", [P, K6, P], F16, 32256 + 1536 * j) for j in range(2)]
        fo = [place(f"fo{j}", [P, D], F32, 35328 + 3072 * j) for j in range(2)]

        ps = ctx.enter_context(nc.psum_tensor("ps", [P, 8, 512], F32))
        ps16 = ps[:, :, :].bitcast(F16)

        def scratch(name, shape, dt):
            return nc.dram_tensor(name, shape, dt, kind="Internal").ap()

        acc_d = scratch("acc_d", (NPAD, D), F32)
        xr_d = scratch("xr_d", (H, R, NB, P, 2 * HD), F16)
        x2_d = scratch("x2_d", (R, NB, P, 2 * D), F16)
        kq_d = scratch("kq_d", (2 * R * H, NPAD), F32)
        kq2_d = scratch("kq2_d", (2 * R, NPAD), F32)
        mb_d = scratch("mb_d", (NW, WK, ND), BF16)
        tab_d = scratch("tab_d", (1, 4 * 32), I32)
        tq_d = scratch("tq_d", (2, R * H, ND), F32)
        tq2_d = scratch("tq2_d", (2, R, ND), F32)
        h_d = scratch("h_d", (ND, D), F32)
        y_d = scratch("y_d", (ND, D), F32)


        def sub(t, i):
            v = t[:, ds(i, 1)]
            if len(v.shape) == 2:
                return v
            names = "abcd"[:len(v.shape) - 2]
            return v.rearrange(f"p o {' '.join(names)} -> p (o {names[0]}) {' '.join(names[1:])}")

        consts_done = sem("consts_done")
        x_in = sem("x_in")
        bias_in = sem("bias_in")
        st_done = sem("st_done")
        mv_done = sem("mv_done")
        vare_done = sem("vare_done")
        rstd_done = sem("rstd_done")
        ln_done = sem("ln_done")
        tr_done = sem("tr_done")
        th_done = sem("th_done")
        tl_done = sem("tl_done")
        w_in = [sem(f"w_in{j}") for j in range(2)]
        w_hi_done = sem("w_hi_done")
        w_lo_done = sem("w_lo_done")
        g_done = sem("g_done")
        g_free = sem("g_free")
        kv_m = sem("kv_m")
        kv_e = sem("kv_e")
        kv_out = sem("kv_out")
        kvs_done = sem("kvs_done")
        kvd_done = sem("kvd_done")
        q_done = sem("q_done")
        q_free = sem("q_free")
        q_mm = sem("q_mm")
        q_ee = sem("q_ee")
        q_out = sem("q_out")
        y_done = sem("y_done")
        y_den = sem("y_den")
        y_hi = sem("y_hi")
        y_lo = sem("y_lo")
        xb_done = sem("xb_done")
        ao_out = [sem(f"ao_out{j}") for j in range(2)]

        qk_in = sem("qk_in")
        xr_hi = sem("xr_hi")
        ev_out = [sem(f"ev_out{j}") for j in range(2)]
        dot_step = sem("dot_step")
        wqk_step = sem("wqk_step")
        kc_done = sem("kc_done")
        kc_free = sem("kc_free")
        kl_done = sem("kl_done")
        kr_done = sem("kr_done")
        kr_out = sem("kr_out")
        kq_st = sem("kq_st")
        e_in = sem("e_in")
        e_step = sem("e_step")
        e_const = sem("e_const")
        e_tr = sem("e_tr")
        e_row = sem("e_row")
        e_base = sem("e_base")
        tab_st = sem("tab_st")
        tab_in = sem("tab_in")
        kbc_in = sem("kbc_in")
        ct_clear = sem("ct_clear")
        oh_rdy = sem("oh_rdy")
        oh_free = sem("oh_free")
        c_free = sem("c_free")
        ct_tr = sem("ct_tr")
        ct_done = sem("ct_done")
        mb_done = sem("mb_done")
        mb_out = [sem(f"mb_out{j}") for j in range(2)]
        mk_step = sem("mk_step")
        qr_in = sem("qr_in")
        t_tr = sem("t_tr")
        t_step = sem("t_step")
        tq_st = sem("tq_st")

        xrh_in = [sem(f"xrh_in{j}") for j in range(2)]
        qb_in = [sem(f"qb_in{j}") for j in range(2)]
        b1_in = sem("b1_in")
        one_done = sem("one_done")
        v_step = sem("v_step")
        x_done = sem("x_done")
        p_done = sem("p_done")
        phi_done = sem("phi_done")
        plo_done = sem("plo_done")
        mm_done = sem("mm_done")
        he_done = sem("he_done")
        hz_step = sem("hz_step")
        hm_step = sem("hm_step")
        hx_step = sem("hx_step")
        hf_done = sem("hf_done")
        h_st = sem("h_st")
        hn_in = [sem(f"hn_in{j}") for j in range(2)]
        pad_done = sem("pad_done")
        qk2_in = sem("qk2_in")
        kq2_st = sem("kq2_st")
        k2_in = sem("k2_in")
        mb_in = [sem(f"mb_in{j}") for j in range(2)]
        mk2_step = sem("mk2_step")
        q2_in = sem("q2_in")
        x2_in = sem("x2_in")
        q2b_in = [sem(f"q2b_in{j}") for j in range(2)]
        ac_in = [sem(f"ac_in{j}") for j in range(2)]
        o_step = sem("o_step")
        ot_out = [sem(f"ot_out{j}") for j in range(2)]
        wf_in = sem("wf_in")
        wf_done = sem("wf_done")
        fx_in = [sem(f"fx_in{j}") for j in range(2)]
        f_step = sem("f_step")
        f_tr = sem("f_tr")
        f_cp = sem("f_cp")
        f_mm = sem("f_mm")
        f_out = sem("f_out")
        fo_done = sem("fo_done")
        fo_st = [sem(f"fo_st{j}") for j in range(2)]

        def chunks():
            out = [Wqkv[:, D + c * CW:D + (c + 1) * CW] for c in range(4)]
            out += [Wqkv[:, c * CW:(c + 1) * CW] for c in range(2)]
            out += [Wo[:, c * CW:(c + 1) * CW] for c in range(2)]
            out += [W1[r, :, c * CW:(c + 1) * CW] for r in range(R) for c in range(2)]
            return [w.rearrange("(k p) n -> p k n", p=P) for w in out]

        def weights_free(eng, c):
            if c < C_Q:
                eng.wait_ge(g_done, NB * (c + 1))
            elif c < C_O:
                eng.wait_ge(q_done, 3 * NRG * (c - C_Q + 1))
            else:
                eng.wait_ge(g_done, NB * (c - 1))

        CH = chunks()

        def store_xr(sp, m):
            r, h0 = m // 2, m % 2 * 2
            with sp.Fori(0, NB // 2) as ii:
                for j in range(2):
                    i = 2 * ii + j
                    sp.wait_ge(g_free, (6 + m) * NB + i + 3)
                    sp.dma_start(xr_d[h0:h0 + 2, r, ds(i, 1), :, :].rearrange("h o p n -> p (o h) n"),
                                 ev[j][:, :, :, :].rearrange("p h s n -> p h (s n)")).then_inc(ev_out[j], 16)

        CH2 = [W2[r, :, c * CW:(c + 1) * CW].rearrange("(k p) n -> p k n", p=P) for r in range(R) for c in range(2)]
        C_Q, C_O, C_X = 4, 6, 8
        C_2 = C_X + 2 * R

        def store_h(sp, h):
            sp.wait_ge(hf_done, h + 1)
            sp.dma_start(h_d[:, h * HD:(h + 1) * HD].rearrange("(b p) n -> p b n", p=DB), he_m[0:DB, :, :]).then_inc(h_st, 16)

        def store_x2(sp, m):
            r, hf = m // 2, m % 2
            with sp.Fori(0, NB // 2) as ii:
                for j in range(2):
                    i = 2 * ii + j
                    sp.wait_ge(g_free, (12 + m) * NB + i + 3)
                    sp.dma_start(x2_d[r, ds(i, 1), :, :].rearrange("o p (s n) -> p (o s) n", s=2)[:, :, hf * CW:(hf + 1) * CW],
                                 ev2[j][:, :, :]).then_inc(ev_out[j], 16)

        def store_y(sp, g):
            for b in range(2):
                sp.wait_ge(o_step, 8 * g + 4 * b + 4)
                sp.dma_start(y_d[(2 * g + b) * DB:(2 * g + b + 1) * DB, :], ot[b][0:DB, :]).then_inc(ot_out[b], 16)

        def store_out(sp, b):
            rows = DB if b < NDB - 1 else DTAIL
            sp.wait_ge(fo_done, b + 1)
            sp.dma_start(out[b * DB:b * DB + rows, :], fo[b % 2][0:rows, :]).then_inc(fo_st[b % 2], 16)

        block = ctx.enter_context(nc.Block())

        @block.sync
        def _(sp):
            sp.wait_ge(consts_done, 1)
            sp.dma_start(X[:, 0:NB - 1, :], x[0:(NB - 1) * P, :].rearrange("(b p) d -> p b d", p=P)).then_inc(x_in, 16)
            sp.dma_start(X[0:TAIL, NB - 1, :], x[(NB - 1) * P:N, :]).then_inc(x_in, 16)
            sp.dma_start(bk_bc[:, :], bqkv[D:3 * D].unsqueeze(0).to_broadcast([P, 2 * D])).then_inc(bias_in, 16)
            sp.dma_start(bq_col[:, :], bqkv[0:D].rearrange("(k p) -> p k", p=P), allow_slow_non_contiguous=True).then_inc(bias_in, 16)
            sp.dma_start(bsum[:, :], bo.unsqueeze(0).to_broadcast([P, D])).then_inc(bias_in, 16)
            sp.dma_start(b2_bc0[:, :], b2.unsqueeze(0).to_broadcast([P, D])).then_inc(bias_in, 16)
            for c, w in enumerate(CH[:C_X]):
                if c >= 2:
                    sp.wait_ge(w_hi_done, c - 1)
                    sp.wait_ge(w_lo_done, c - 1)
                sp.dma_start(wst[c % 2][:, :, :], w).then_inc(w_in[c % 2], 16)
            for c in range(2):
                with sp.Fori(0, NB // 2) as ii:
                    for j in range(2):
                        i = 2 * ii + j
                        sp.wait_ge(g_free, 4 * NB + c * NB + i + 3)
                        sp.dma_start(acc_d[ds(i * P, P), c * CW:(c + 1) * CW], ao[j][:, :]).then_inc(ao_out[j], 16)
            for j in range(2):
                sp.wait_ge(ao_out[j], 16 * NB)

            sp.wait_ge(g_free, 6 * NB + 2)
            sp.dma_start(qk_bc[:, 0:H, :], q1.unsqueeze(0).to_broadcast([P, H, D])).then_inc(qk_in, 16)
            sp.dma_start(qk_bc[:, H:2 * H, :], k1.unsqueeze(0).to_broadcast([P, H, D])).then_inc(qk_in, 16)
            for c in range(C_X, C_X + 2 * R):
                m = c - C_X
                sp.wait_ge(w_hi_done, c - 1)
                sp.wait_ge(w_lo_done, c - 1)
                if m >= 2:
                    sp.wait_ge(dot_step, DOTS * (m - 1))
                sp.dma_start(wst[c % 2][:, :, :], CH[c]).then_inc(w_in[c % 2], 16)
                if m >= 1:
                    store_xr(sp, m - 1)
            store_xr(sp, 2 * R - 1)
            sp.wait_ge(kr_out, NRG)
            sp.dma_start(kq_d[:, :], kq[:, :]).then_inc(kq_st, 16)

            sp.wait_ge(kl_done, NB)
            for j in range(2):
                sp.wait_ge(ev_out[j], 16 * R * NB)
            for a, arr in enumerate((src, dst, et)):
                rows = arr.rearrange("(t e) -> t e", e=ET)
                sp.dma_start(e_int[:, 0:2, a, :], rows[0:2 * P, :].rearrange("(c p) e -> p c e", p=P)).then_inc(e_in, 16)
                sp.dma_start(e_int[0:NT - 2 * P, 2, a, :], rows[2 * P:NT, :]).then_inc(e_in, 16)
            sp.wait_ge(kq_st, 16)
            for r in range(R):
                rows = kq_d[R * H + r * H:R * H + (r + 1) * H, 0:ND]
                sp.dma_start(kbc[r:WK:R, :, :], rows.unsqueeze(0).to_broadcast([WD, H, ND])).then_inc(kbc_in, 16)
            sp.wait_ge(e_row, 7)
            sp.dma_start(tab_d.rearrange("o (w c) -> (o w) c", c=4), tabi[:, :]).then_inc(tab_st, 16)
            sp.wait_ge(tab_st, 16)
            sp.dma_start(tabrow[:, :], tab_d[:, :]).then_inc(tab_in, 16)
            with sp.Fori(0, NW // 2) as wi:
                for jw in range(2):
                    w = 2 * wi + jw
                    sp.wait_ge(mb_done, w + 3)
                    sp.dma_start(mb_d[ds(w, 1), :, :].rearrange("o p n -> (o p) n"), mb[jw][0:WK, :]).then_inc(mb_out[jw], 16)
            sp.dma_start(qr[0:NW, :, :], kq_d[0:R * H, 0:ND].rearrange("a (w d) -> w a d", d=WD)).then_inc(qr_in, 16)
            for j in range(2):
                sp.wait_ge(mb_out[j], 16 * NW // 2)
            sp.wait_ge(t_step, 14)
            sp.dma_start(tq_d.rearrange("s a (w d) -> w (s a) d", d=WD), tq[0:NW, :, :, :].rearrange("w s a d -> w (s a) d")).then_inc(tq_st, 16)
            sp.wait_ge(tq_st, 16)

            sp.wait_ge(ct_done, 3 * NW + 2)
            sp.dma_start(b1_bc[:, :], b1.unsqueeze(0).to_broadcast([P, D])).then_inc(b1_in, 16)
            for h in range(H):
                if h < 2:
                    loads = (0, 1) if h == 0 else ()
                else:
                    sp.wait_ge(mm_done, (h - 1) * R * NB + 2)
                    loads = (h,)
                for r in range(R):
                    i = h * R + r
                    if i >= 2:
                        sp.wait_ge(v_step, 2 * (i - 1) * NB)
                    sp.dma_start(qbc[i % 2][:, :, :], tq_d[:, r * H + h, :].unsqueeze(0).to_broadcast([P, 2, ND])).then_inc(qb_in[i % 2], 16)
                    if r == 0:
                        for g in loads:
                            sp.dma_start(xrh[g % 2][:, :, :, 0:2 * HD].rearrange("p r b n -> p (r b) n"),
                                         xr_d[g].rearrange("r b p n -> p (r b) n")).then_inc(xrh_in[g % 2], 16)
                if h >= 1:
                    store_h(sp, h - 1)
            store_h(sp, H - 1)

            sp.wait_ge(h_st, 16 * H)
            sp.wait_ge(mm_done, H * R * NB + 2)
            for m in range(2):
                sp.dma_start(wst[m][:, :, :], CH2[m]).then_inc(w_in[m], 16)
            sp.dma_start(qk_bc[:, 0, :], q2.to_broadcast([P, D])).then_inc(qk2_in, 16)
            sp.dma_start(qk_bc[:, 1, :], k2.to_broadcast([P, D])).then_inc(qk2_in, 16)
            with sp.Fori(0, NDB // 2) as ii:
                for j in range(2):
                    b = 2 * ii + j
                    sp.wait_ge(tl_done, 2 * NB + 2 * b + 2)
                    sp.dma_start(hn[j][0:DB, :], h_d[ds(b * DB, DB), :]).then_inc(hn_in[j], 16)
            for m in range(2 * R):
                if m >= 2:
                    sp.wait_ge(w_hi_done, C_2 + m - 1)
                    sp.wait_ge(w_lo_done, C_2 + m - 1)
                    sp.wait_ge(dot_step, 2 * R * DOTS + DOTS2 * (m - 1))
                    sp.dma_start(wst[m % 2][:, :, :], CH2[m]).then_inc(w_in[m % 2], 16)
                if m >= 1:
                    store_x2(sp, m - 1)
            store_x2(sp, 2 * R - 1)
            sp.wait_ge(kr_out, 2 * NRG)
            sp.dma_start(kq2_d[:, :], kq[0:2 * R, :]).then_inc(kq2_st, 16)
            sp.wait_ge(kl_done, 2 * NB)
            for j in range(2):
                sp.wait_ge(ev_out[j], 16 * 2 * R * NB)
            sp.wait_ge(kq2_st, 16)
            for r in range(R):
                sp.dma_start(kbc2[r:WK:R, :], kq2_d[R + r, 0:ND].unsqueeze(0).to_broadcast([WD, ND])).then_inc(k2_in, 16)
            sp.dma_start(qr2[0:NW, :, :], kq2_d[0:R, 0:ND].rearrange("a (w d) -> w a d", d=WD)).then_inc(q2_in, 16)
            with sp.Fori(0, NW // 2) as wi:
                for jw in range(2):
                    w = 2 * wi + jw
                    sp.wait_ge(mk2_step, 2 * w + 1)
                    sp.dma_start(mb2[jw][0:WK, :], mb_d[ds(w, 1), :, :].rearrange("o p n -> (o p) n")).then_inc(mb_in[jw], 16)
            for r in range(R):
                sp.dma_start(x2[:, r, :, 0:2 * D], x2_d[r].rearrange("b p n -> p b n")).then_inc(x2_in, 16)
            sp.wait_ge(t_step, 28)
            sp.dma_start(tq2_d.rearrange("s a (w d) -> w (s a) d", d=WD), tq2[0:NW, :, :, :].rearrange("w s a d -> w (s a) d")).then_inc(tq_st, 16)
            sp.wait_ge(tq_st, 32)

            for g in range(NG):
                if g >= 2:
                    sp.wait_ge(v_step, V2_0 + 2 * (g - 1) * R * NB)
                sp.dma_start(qb2[g % 2][:, :, :, :].rearrange("p s r d -> p (s r) d"),
                             tq2_d[:, :, g * GW:(g + 1) * GW].rearrange("s r d -> (s r) d").unsqueeze(0).to_broadcast([P, 2 * R, GW])
                             ).then_inc(q2b_in[g % 2], 16)
                if g >= 1:
                    sp.wait_ge(o_step, 8 * g)
                for b in range(2):
                    sp.dma_start(ac[b][0:DB, :], acc_d[(2 * g + b) * DB:(2 * g + b + 1) * DB, :]).then_inc(ac_in[b], 16)
                if g >= 1:
                    store_y(sp, g - 1)
            store_y(sp, NG - 1)
            for b in range(2):
                sp.wait_ge(ot_out[b], 16 * NG)

            sp.dma_start(wf8[:, :, :], wf.rearrange("(k p) n -> p k n", p=P)).then_inc(wf_in, 16)
            sp.dma_start(bf_bc[:, :], bf.unsqueeze(0).to_broadcast([P, D])).then_inc(wf_in, 16)
            for b in range(NDB):
                if b >= 2:
                    sp.wait_ge(fo_done, b - 1)
                sp.dma_start(fx[b % 2][0:DB, :], y_d[b * DB:(b + 1) * DB, :]).then_inc(fx_in[b % 2], 16)
                if b >= 1:
                    store_out(sp, b - 1)
            store_out(sp, NDB - 1)
            for j in range(2):
                sp.wait_ge(fo_st[j], 16 * NDB // 2)

        @block.gpsimd
        def _(pool):
            pool.memset(X[:, NB - 1, :], 0.0).then_inc(consts_done, 1)
            pool.memset(ident[:, :], 0.0)
            pool.memset(ones[:, :], 1.0)
            pool.memset(cst[:, 0:1], 1e-5)
            pool.memset(cst[:, 1:2], -0.5)
            pool.memset(cst[:, 2:3], 0.02)
            pool.iota(iota_s[:, :], [[1, ND]], base=0, channel_multiplier=0, allow_small_or_imprecise_dtypes=True)
            pool.iota(iota_k[:, :], [[1, WK]], base=0, channel_multiplier=0, allow_small_or_imprecise_dtypes=True)
            pool.iota(neg_w[:, :], [[-WK, NW]], base=0, channel_multiplier=0, allow_small_or_imprecise_dtypes=True)
            pool.memset(V[:, :, :, P:P + 1].rearrange("p b k o -> p (b k) o"), 1.0).then_inc(consts_done, 1)
            pool.wait_ge(consts_done, 2)
            pool.affine_select(out=ident[:, :], in_=ident[:, :], compare_op=ALU.not_equal, fill=1.0, base=0,
                               pattern=[[-1, P]], channel_multiplier=1).then_inc(consts_done, 1)
            pool.wait_ge(consts_done, 3)
            pool.tensor_copy(ident16[:, :], ident[:, :]).then_inc(consts_done, 1)

            def w_lo_part(c):
                pool.wait_ge(w_hi_done, c + 1)
                if c >= 2:
                    weights_free(pool, c - 2)
                pool.tensor_tensor(w_lo[c % 2][:, :, :], wst[c % 2][:, :, :], w_hi[c % 2][:, :, :], ALU.subtract).then_inc(w_lo_done, 1)

            def rstd_part(j, n):
                pool.wait_ge(mv_done, n + 1)
                pool.tensor_tensor(vare[:, j, :], mv[:, j, 1:2], cst[:, 0:1], ALU.add).then_inc(vare_done, 1)
                pool.wait_ge(vare_done, n + 1)
                pool.tensor_tensor(rstd[:, j, :], vare[:, j, :], cst[:, 1:2], ALU.pow).then_inc(rstd_done, 1)

            with pool.Fori(0, NB // 2) as ii:
                for j in range(2):
                    rstd_part(j, 2 * ii + j)
            w_lo_part(0)
            w_lo_part(1)
            w_lo_part(2)
            w_lo_part(3)
            pool.wait_ge(bias_in, 64)
            pool.tensor_tensor(bsum[:, :], bsum[:, :], b2_bc0[:, :], ALU.add).then_inc(xb_done, 1)
            pool.wait_ge(xb_done, 1)
            pool.wait_ge(ln_done, NB)
            w_lo_part(4)
            with pool.Fori(0, NB) as i:
                pool.tensor_tensor(sub(X, i), sub(X, i), bsum[:, :], ALU.add).then_inc(xb_done, 1)
            w_lo_part(5)
            w_lo_part(6)
            w_lo_part(7)
            with pool.Fori(0, K6) as p6:
                for g in range(NRG):
                    pool.wait_ge(y_hi, NRG * p6 + g + 1)
                    pool.tensor_tensor(sub(yt_lo, p6)[:, g * RG:(g + 1) * RG], yv[g % 2][:, :], sub(yt_hi, p6)[:, g * RG:(g + 1) * RG],
                                       ALU.subtract).then_inc(y_lo, 1)
            for c in range(C_X, C_X + 2 * R):
                w_lo_part(c)

            pool.wait_ge(kl_done, NB)
            pool.wait_ge(kr_out, NRG)
            for j in range(2):
                pool.wait_ge(ev_out[j], 16 * R * NB)
            pool.iota(wlo[:, :], [[WK - 1, 2]], base=0, channel_multiplier=WK, allow_small_or_imprecise_dtypes=True)
            pool.iota(tix[:, 0, :], [[1, NT]], base=1, channel_multiplier=0, allow_small_or_imprecise_dtypes=True)
            pool.iota(tix[:, 1, :], [[1, NT]], base=1000, channel_multiplier=0, allow_small_or_imprecise_dtypes=True)
            pool.affine_select(out=ltri[:, :], in_=ones[0:32, 0:32], compare_op=ALU.is_gt, fill=0.0, base=0,
                               pattern=[[1, 32]], channel_multiplier=-1).then_inc(e_const, 1)
            pool.memset(oh_k[:, :, :], 0.0).then_inc(e_const, 1)
            pool.memset(CT[:, NB - 1, :, :], 0).then_inc(ct_clear, 1)

            pool.wait_ge(b1_in, 16)
            for j in range(2):
                pool.memset(xrh[j][:, :, :, 2 * HD:2 * HD + 1].rearrange("p r b o -> p (r b) o"), 1.0)
                pool.memset(ph[j][:, ND:ND + 4], 0.0)
                pool.memset(pl[j][:, ND:ND + 4], 0.0).then_inc(one_done, 1)

            def head_tail(h):
                pool.wait_ge(hz_step, 2 * h + 2)
                if h >= 1:
                    pool.wait_ge(h_st, 16 * h)
                pool.tensor_tensor(he_m[0:DB, :, :], he[0:DB, :, 0:HD], he_z[0:DB, :, :].to_broadcast([DB, NDB, HD]), ALU.mult).then_inc(hm_step, 1)
                pool.wait_ge(hm_step, 2 * h + 1)
                pool.tensor_tensor(he_m[0:DB, :, :], he_m[0:DB, :, :], b1_bc[0:DB, h * HD:(h + 1) * HD].unsqueeze(1).to_broadcast([DB, NDB, HD]),
                                   ALU.add).then_inc(hm_step, 1)

            for h in range(H):
                for r in range(R):
                    with pool.Fori(0, NB // 2) as ss:
                        for j in range(2):
                            n = (h * R + r) * NB + 2 * ss + j
                            pool.wait_ge(phi_done, n + 1)
                            pool.wait_ge(mm_done, n + 1)
                            pool.tensor_tensor(pl[j][:, 0:ND], pf[j][:, :], ph[j][:, 0:ND], ALU.subtract).then_inc(plo_done, 1)
                    if r == 0 and h >= 1:
                        head_tail(h - 1)
            head_tail(H - 1)

            pool.wait_ge(h_st, 16 * H)
            pool.wait_ge(mm_done, H * R * NB + 2)
            pool.memset(xt_hi[:, :, ND:NPAD], 0.0)
            pool.memset(xt_lo[:, :, ND:NPAD], 0.0).then_inc(pad_done, 1)
            for m in range(2 * R):
                w_lo_part(C_2 + m)

            pool.wait_ge(t_step, 28)
            pool.memset(x2[:, :, :, 2 * D:2 * D + 1].rearrange("p r b o -> p (r b) o"), 1.0)
            for j in range(2):
                pool.memset(ph2[j][:, GW:GW + 4], 0.0)
                pool.memset(pl2[j][:, GW:GW + 4], 0.0).then_inc(one_done, 1)
            for g in range(NG):
                for r in range(R):
                    with pool.Fori(0, NB // 2) as ss:
                        for j in range(2):
                            n = H * R * NB + (g * R + r) * NB + 2 * ss + j
                            pool.wait_ge(phi_done, n + 1)
                            pool.wait_ge(mm_done, n + 1)
                            pool.tensor_tensor(pl2[j][:, 0:GW], p2[j][:, :], ph2[j][:, 0:GW], ALU.subtract).then_inc(plo_done, 1)

            def add_x(b):
                pool.wait_ge(f_out, 2 * b + 2)
                pool.tensor_tensor(fo[b % 2][0:DB, :], fo[b % 2][0:DB, :], fx[b % 2][0:DB, :], ALU.add).then_inc(fo_done, 1)

            for b in range(NDB):
                rstd_part(b % 2, NB + b)
                if b >= 1:
                    add_x(b - 1)
            add_x(NDB - 1)

        @block.scalar
        def _(act):

            def w_hi_part(c):
                act.wait_ge(w_in[c % 2], 16 * (c // 2 + 1))
                if c >= 2:
                    weights_free(act, c - 2)
                act.activation(w_hi[c % 2][:, :, :], wst[c % 2][:, :, :], ACT.Copy).then_inc(w_hi_done, 1)

            w_hi_part(0)
            w_hi_part(1)
            with act.Fori(0, NB // 2) as ii:
                for j in range(2):
                    for hf in range(2):
                        n = 2 * (2 * ii + j) + hf
                        act.wait_ge(tr_done, n + 1)
                        act.activation(xt_hi[:, 3 * hf:3 * hf + 3, ds((2 * ii + j) * P, P)],
                                       ps[:, 2 * j + hf, 0:3 * P].rearrange("p (k n) -> p k n", k=3), ACT.Copy).then_inc(th_done, 1)
            for c in range(2):
                with act.Fori(0, NB // 2) as ii:
                    for j in range(2):
                        n = c * NB + 2 * ii + j
                        act.wait_ge(g_free, n + 3)
                        act.wait_ge(kv_out, n + 1)
                        act.activation(ev_m[j][:, :], ev_t[j][:, :], ACT.Relu, scale=-1.0).then_inc(kv_m, 1)
                        act.wait_ge(kv_m, n + 1)
                        act.activation(ev_m[j][:, :], ev_m[j][:, :], ACT.Exp, scale=-1.0).then_inc(kv_e, 1)
                w_hi_part(c + 2)
            w_hi_part(4)
            w_hi_part(5)
            for c in range(2):
                with act.Fori(0, 3) as fb:
                    for g in range(NRG):
                        n = (3 * c + fb) * NRG + g
                        act.wait_ge(q_free, n + 5)
                        act.wait_ge(q_out, n + 1)
                        act.activation(q_m[g % 2][:, :], q_t[g % 2][:, :], ACT.Relu, scale=-1.0).then_inc(q_mm, 1)
                        act.wait_ge(q_mm, n + 1)
                        act.activation(q_m[g % 2][:, :], q_m[g % 2][:, :], ACT.Exp, scale=-1.0).then_inc(q_ee, 1)
                w_hi_part(C_O + c)
            with act.Fori(0, K6) as p6:
                for g in range(NRG):
                    act.wait_ge(y_den, 3 * (NRG * p6 + g) + 6)
                    act.activation(sub(yt_hi, p6)[:, g * RG:(g + 1) * RG], yv[g % 2][:, :], ACT.Copy).then_inc(y_hi, 1)
            w_hi_part(C_X)
            w_hi_part(C_X + 1)
            act.wait_ge(g_free, 6 * NB + 2)
            for m in range(2 * R):
                with act.Fori(0, NB // 2) as ii:
                    for j in range(2):
                        n = m * NB + 2 * ii + j
                        act.wait_ge(ev_out[j], 16 * (m * NB // 2 + ii))
                        act.wait_ge(g_done, 6 * NB + n + 1)
                        act.activation(ev[j][:, :, 1, :], ps[:, 6 + j, 0:CW].rearrange("p (h n) -> p h n", h=2), ACT.Copy).then_inc(xr_hi, 1)
                if m + 2 < 2 * R:
                    w_hi_part(C_X + m + 2)
            for g in range(NRG):
                act.wait_ge(kr_done, g + 1)
                act.activation(kq[:, g * RG:(g + 1) * RG], ps[0:2 * R * H, g, 0:RG], ACT.Copy).then_inc(kr_out, 1)
            for i in range(0, NB, 2):
                act.wait_ge(kc_free, i + 4)
                act.activation(kcol_leak[:, i:i + 2, :], kcol[:, i:i + 2, :], ACT.Copy, scale=0.2).then_inc(kl_done, 2)

            act.wait_ge(tab_in, 16)
            act.wait_ge(ct_clear, 1)
            with act.Fori(0, NW // 2) as wi:
                for jw in range(2):
                    w = 2 * wi + jw
                    count = act.value_load(tabrow[0:1, ds(4 * w + 1, 1)], min_val=3, max_val=NT)
                    first = act.value_load(tabrow[0:1, ds(4 * w + 2, 1)], min_val=0, max_val=NW * NT)
                    act.wait_ge(ct_tr, 3 * w + 3)
                    act.wait_ge(mb_done, w + 1)
                    act.wait_ge(oh_free, first + count + OHS)
                    act.activation(c_row[jw][0:WK, :].rearrange("p (a n) -> p a n", a=3), ps[0:WK, 3 * jw:3 * jw + 3, 0:ND // 3],
                                   ACT.Copy).then_inc(c_free, 1)
                for jw in range(2):
                    w = 2 * wi + jw
                    for g in range(3):
                        bank = 6 + (3 * jw + g) % 2
                        act.wait_ge(ct_tr, 3 * w + g + 7)
                        if g < 2:
                            act.activation(CT[:, 4 * g:4 * g + 4, :, ds(w * WD, WD)],
                                           ps[:, bank, 0:4 * WK].rearrange("p (i d r) -> p i r d", i=4, r=R), ACT.Copy).then_inc(ct_done, 1)
                        else:
                            rows = ND - (NB - 1) * P
                            act.activation(CT[:, 8, :, ds(w * WD, WD)], ps[:, bank, 0:WK].rearrange("p (d r) -> p r d", r=R), ACT.Copy)
                            act.activation(CT[0:rows, 9, :, ds(w * WD, WD)],
                                           ps[0:rows, bank, WK:2 * WK].rearrange("p (d r) -> p r d", r=R), ACT.Copy).then_inc(ct_done, 1)

            def head_tail(h):
                act.wait_ge(hm_step, 2 * h + 2)
                if h >= 1:
                    act.wait_ge(hf_done, h)
                act.activation(he_e[0:DB, :, :], he_m[0:DB, :, :], ACT.Relu, scale=-1.0).then_inc(hx_step, 1)
                act.wait_ge(hx_step, 3 * h + 1)
                act.activation(he_e[0:DB, :, :], he_e[0:DB, :, :], ACT.Exp, scale=-1.0).then_inc(hx_step, 1)
                act.activation(he[0:DB, :, 0:HD], he_m[0:DB, :, :], ACT.Relu).then_inc(hx_step, 1)

            for h in range(H):
                for r in range(R):
                    with act.Fori(0, NB // 2) as ss:
                        n = (h * R + r) * NB + 2 * ss
                        for j in range(2):
                            act.wait_ge(v_step, 2 * (n + j) + 2)
                            act.activation(vb[j][:, :], vb[j][:, :], ACT.Exp).then_inc(x_done, 1)
                        for j in range(2):
                            act.wait_ge(p_done, n + j + 3)
                            act.wait_ge(mm_done, n + j + 1)
                            act.activation(ph[j][:, 0:ND], pf[j][:, :], ACT.Copy).then_inc(phi_done, 1)
                    if r == 1 and h >= 1:
                        head_tail(h - 1)
                act.wait_ge(mm_done, (h + 1) * R * NB + 2)
                if h >= 1:
                    act.wait_ge(hf_done, h)
                act.activation(he[0:DB, :, :].rearrange("p (a b) n -> p a (b n)", b=2), ps[0:DB, 0:NDB // 2, 0:2 * (HD + 1)], ACT.Copy).then_inc(he_done, 1)
            head_tail(H - 1)

            w_hi_part(C_2)
            w_hi_part(C_2 + 1)
            with act.Fori(0, NDB // 2) as ii:
                for j in range(2):
                    for hf in range(2):
                        b = 2 * ii + j
                        act.wait_ge(tr_done, 2 * NB + 2 * b + hf + 1)
                        act.activation(xt_hi[:, 3 * hf:3 * hf + 3, ds(b * DB, DB)],
                                       ps[:, 2 * j + hf, 0:3 * DB].rearrange("p (k n) -> p k n", k=3), ACT.Copy).then_inc(th_done, 1)
            for m in range(2 * R):
                with act.Fori(0, NB // 2) as ii:
                    for j in range(2):
                        n = (2 * R + m) * NB + 2 * ii + j
                        act.wait_ge(ev_out[j], 16 * ((2 * R + m) * NB // 2 + ii))
                        act.wait_ge(g_done, 6 * NB + n + 1)
                        act.activation(ev2[j][:, 1, :], ps[:, 6 + j, 0:CW], ACT.Copy).then_inc(xr_hi, 1)
                if m + 2 < 2 * R:
                    w_hi_part(C_2 + m + 2)
            for g in range(NRG):
                act.wait_ge(kr_done, NRG + g + 1)
                act.activation(kq[0:2 * R, g * RG:(g + 1) * RG], ps[0:2 * R, g, 0:RG], ACT.Copy).then_inc(kr_out, 1)
            for i in range(0, NB, 2):
                act.wait_ge(kc_free, NB + i + 4)
                act.activation(kcol_leak[:, i:i + 2, 0:R], kcol[:, i:i + 2, 0:R], ACT.Copy, scale=0.2).then_inc(kl_done, 2)

            for g in range(NG):
                for r in range(R):
                    with act.Fori(0, NB // 2) as ss:
                        n = H * R * NB + (g * R + r) * NB + 2 * ss
                        for j in range(2):
                            act.wait_ge(v_step, 2 * (n + j) + 2)
                            act.activation(v2[j][:, :], v2[j][:, :], ACT.Exp).then_inc(x_done, 1)
                        for j in range(2):
                            act.wait_ge(p_done, n + j + 3)
                            act.wait_ge(mm_done, n + j + 1)
                            act.activation(ph2[j][:, 0:GW], p2[j][:, :], ACT.Copy).then_inc(phi_done, 1)

            act.wait_ge(wf_in, 32)
            act.activation(wf16[:, :, :], wf8[:, :, :].bitcast(I8), ACT.Copy).then_inc(wf_done, 1)
            for b in range(NDB):
                act.wait_ge(f_tr, b + 1)
                act.activation(fqt[b % 2][:, :, 0:DB], ps16[:, b % 2, 0:K6 * DB].rearrange("p (k n) -> p k n", k=K6), ACT.Copy).then_inc(f_cp, 1)

        @block.vector
        def _(dve):
            dve.sem_inc(tl_done, 4)
            dve.sem_inc(g_free, 2)
            dve.sem_inc(q_free, 4)
            dve.sem_inc(y_lo, 2)
            dve.sem_inc(y_den, 3)
            dve.sem_inc(kv_out, 2)
            dve.sem_inc(q_out, 2)
            dve.wait_ge(x_in, 32)

            def row_stats(src, j, n, rows=P):
                for hf in range(2):
                    dve.bn_stats(stat[0:rows, j, hf, :], src[0:rows, hf * CW:(hf + 1) * CW]).then_inc(st_done, 1)
                dve.wait_ge(st_done, 2 * n + 2)
                dve.memset(tick[:, j:j + 1], 0.0)
                dve.bn_aggr(mv[0:rows, j, :], stat[0:rows, j, :, :].rearrange("p a b -> p (a b)")).then_inc(mv_done, 1)

            def lo_half(i, j, hf):
                dve.wait_ge(th_done, 2 * i + hf + 1)
                dve.tensor_tensor(xt_lo[:, 3 * hf:3 * hf + 3, ds(i * P, P)],
                                  ps[:, 2 * j + hf, 0:3 * P].rearrange("p (k n) -> p k n", k=3),
                                  xt_hi[:, 3 * hf:3 * hf + 3, ds(i * P, P)], ALU.subtract).then_inc(tl_done, 1)

            with dve.Fori(0, NB // 2) as ii:
                for j in range(2):
                    row_stats(sub(X, 2 * ii + j), j, 2 * ii + j)
                for j in range(2):
                    i = 2 * ii + j
                    dve.wait_ge(rstd_done, i + 1)
                    dve.wait_ge(tl_done, 2 * i + 2)
                    dve.tensor_scalar(xn[j][:, :], sub(X, i), mv[:, j, 0:1], rstd[:, j, :], ALU.subtract, ALU.mult).then_inc(ln_done, 1)
                for j in range(2):
                    for hf in range(2):
                        lo_half(2 * ii + j, j, hf)

            dve.wait_ge(bias_in, 64)
            for c in range(2):
                with dve.Fori(0, NB // 2) as ii:
                    for j in range(2):
                        n = c * NB + 2 * ii + j
                        dve.wait_ge(g_done, n + 1)
                        dve.wait_ge(kv_out, n + 1)
                        dve.tensor_tensor(ev_t[j][:, :], ps[:, 6 + j, 0:CW], bk_bc[:, c * CW:(c + 1) * CW], ALU.add).then_inc(g_free, 1)
                    for j in range(2):
                        n = c * NB + 2 * ii + j
                        dve.wait_ge(kv_e, n + 1)
                        dve.scalar_tensor_tensor(sub(KF, 2 * ii + j)[:, c * CW:(c + 1) * CW], ev_t[j][:, :], 0.0, ev_m[j][:, :],
                                                 ALU.max, ALU.add).then_inc(kv_out, 1)
            for c in range(2):
                with dve.Fori(0, NB // 2) as ii:
                    for j in range(2):
                        i = 2 * ii + j
                        n = (2 + c) * NB + i
                        dve.wait_ge(g_done, n + 1)
                        dve.tensor_tensor(sub(V, i)[:, 3 * c:3 * c + 3, 0:P], ps[:, 6 + j, 0:CW].rearrange("p (k n) -> p k n", k=3),
                                          bk_bc[:, D + c * CW:D + (c + 1) * CW].rearrange("p (k n) -> p k n", k=3), ALU.add).then_inc(g_free, 1)
            dve.wait_ge(kvs_done, 2)
            dve.memset(kvd[:, :, :], 0.0)
            dve.memset(zd[:, :, :], 0.0).then_inc(kvd_done, 1)
            dve.wait_ge(kvd_done, 1)
            for p6 in range(K6):
                o = p6 % 3 * (P + 1)
                for hf in range(2):
                    h0, h1 = 64 * hf, 64 * hf + 64
                    dve.tensor_copy(kvd[h0:h1, p6, h0:h1], ps[h0:h1, 4 + p6 // 3, o + h0:o + h1])
                    last = dve.tensor_scalar(zd[h0:h1, p6, h0:h1], ones[h0:h1, 0:64], ps[h0:h1, 4 + p6 // 3, o + P:o + P + 1], None, ALU.mult)
            last.then_inc(kvd_done, 1)
            for c in range(2):
                with dve.Fori(0, 3) as fb:
                    for g in range(NRG):
                        n = (3 * c + fb) * NRG + g
                        dve.wait_ge(q_done, n + 1)
                        dve.wait_ge(q_out, n + 1)
                        dve.tensor_scalar(q_t[g % 2][:, :], ps[:, g, 0:RG], sub(bq_col, 3 * c + fb), None, ALU.add).then_inc(q_free, 1)
                        if g % 2:
                            for g2 in (g - 1, g):
                                n2 = (3 * c + fb) * NRG + g2
                                dve.wait_ge(q_ee, n2 + 1)
                                dve.scalar_tensor_tensor(sub(QF, 3 * c + fb)[:, g2 * RG:(g2 + 1) * RG], q_t[g2 % 2][:, :], 0.0, q_m[g2 % 2][:, :],
                                                         ALU.max, ALU.add).then_inc(q_out, 1)
            with dve.Fori(0, K6) as p6:
                for g in range(NRG):
                    n = NRG * p6 + g
                    dve.wait_ge(y_done, n + 1)
                    dve.tensor_scalar(den[g % 2][:, :], ps[:, 2 + g % 2, 0:RG], 1e-6, None, ALU.max).then_inc(y_den, 1)
                    dve.wait_ge(y_den, 3 * n + 4)
                    dve.reciprocal(den[g % 2][:, :], den[g % 2][:, :]).then_inc(y_den, 1)
                    dve.wait_ge(y_den, 3 * n + 5)
                    dve.wait_ge(y_lo, n + 1)
                    dve.tensor_tensor(yv[g % 2][:, :], ps[:, g % 2, 0:RG], den[g % 2][:, :], ALU.mult).then_inc(y_den, 1)
            for c in range(2):
                with dve.Fori(0, NB // 2) as ii:
                    for j in range(2):
                        i = 2 * ii + j
                        dve.wait_ge(g_done, 4 * NB + c * NB + i + 1)
                        dve.wait_ge(ao_out[j], 16 * (c * NB // 2 + ii))
                        dve.wait_ge(xb_done, NB + 1)
                        dve.tensor_tensor(ao[j][:, :], ps[:, 6 + j, 0:CW], sub(X, i)[:, c * CW:(c + 1) * CW], ALU.add).then_inc(g_free, 1)

            dve.sem_inc(kc_free, 2)
            dots = 0
            for m in range(2 * R):
                r, hf = m // 2, m % 2
                todo = [(k, q) for k in range(K6) for q in range(2 * H)]
                assert len(todo) == DOTS
                for i in range(NB):
                    if i == 0:
                        dve.wait_ge(w_in[m % 2], 16 * ((C_X + m) // 2 + 1))
                        dve.wait_ge(qk_in, 32)
                    for k, q in todo[i * DOTS // NB:(i + 1) * DOTS // NB]:
                        if dots >= 2:
                            dve.wait_ge(dot_step, dots - 1)
                        col = q // H * R * H + r * H + q % H
                        dve.tensor_tensor_reduce(out=dot_junk[dots % 2][:, :], in0=wst[m % 2][:, k, :], in1=qk_bc[:, q, hf * CW:(hf + 1) * CW],
                                                 scale=1.0, scalar=0.0, op0=ALU.mult, op1=ALU.add,
                                                 accum_out=wqk_p[:, hf, k, col:col + 1]).then_inc(dot_step, 1)
                        dots += 1
                    n = m * NB + i
                    dve.wait_ge(xr_hi, n + 1)
                    dve.tensor_tensor(ev[i % 2][:, :, 0, :], ps[:, 6 + i % 2, 0:CW].rearrange("p (h n) -> p h n", h=2), ev[i % 2][:, :, 1, :],
                                      ALU.subtract).then_inc(g_free, 1)
            dve.wait_ge(dot_step, dots)
            dve.tensor_tensor(wqk[:, :, :], wqk_p[:, 0, :, :], wqk_p[:, 1, :, :], ALU.add).then_inc(wqk_step, 1)
            dve.wait_ge(wqk_step, 1)
            dve.tensor_copy(wqk_hi[:, :, :], wqk[:, :, :]).then_inc(wqk_step, 1)
            dve.wait_ge(wqk_step, 2)
            dve.tensor_tensor(wqk_lo[:, :, :], wqk[:, :, :], wqk_hi[:, :, :], ALU.subtract).then_inc(wqk_step, 1)
            for i in range(NB):
                dve.wait_ge(kc_done, i + 1)
                dve.tensor_copy(kcol[:, i, :], ps[:, 4 + i % 2, R * H:2 * R * H]).then_inc(kc_free, 1)

            rest = NT - 2 * P
            dve.wait_ge(kr_out, NRG)
            for j in range(2):
                dve.wait_ge(ev_out[j], 16 * R * NB)
            dve.wait_ge(e_in, 96)
            dve.tensor_copy(e_flt[:, 0:2, :, :], e_int[:, 0:2, :, :])
            dve.tensor_copy(e_flt[0:rest, 2, :, :], e_int[0:rest, 2, :, :]).then_inc(e_step, 1)
            dve.wait_ge(e_step, 1)
            dve.scalar_tensor_tensor(e_key[:, 0:2, :], e_flt[:, 0:2, 1, :], 3.0, e_flt[:, 0:2, 2, :], ALU.mult, ALU.add)
            dve.scalar_tensor_tensor(e_key[0:rest, 2, :], e_flt[0:rest, 2, 1, :], 3.0, e_flt[0:rest, 2, 2, :], ALU.mult, ALU.add).then_inc(e_step, 1)
            dve.wait_ge(e_step, 2)
            for c, rows in enumerate((P, P, rest)):
                for m, op in enumerate((ALU.min, ALU.max)):
                    last = dve.tensor_reduce(tmm[0:rows, c, m:m + 1], e_key[0:rows, c, :], AX.X, op)
            last.then_inc(e_step, 1)
            dve.wait_ge(e_step, 3)
            for c, rows in enumerate((P, P, rest)):
                for m in range(2):
                    last = dve.tensor_scalar(tbc[0:rows, c, m, :], ones[0:rows, 0:32], tmm[0:rows, c, m:m + 1], None, ALU.mult)
            last.then_inc(e_step, 1)
            dve.wait_ge(e_tr, 1)
            dve.tensor_copy(keyT[0:ET, 0:NT], ps[0:ET, 0, 0:NT])
            dve.tensor_copy(srcT[0:ET, 0:NT], ps[0:ET, 1, 0:NT])
            dve.tensor_copy(srow[:, 0, :], ps[0:32, 2, 0:NT])
            dve.tensor_copy(srow[:, 1, :], ps[0:32, 3, 0:NT]).then_inc(e_row, 1)
            dve.wait_ge(e_const, 2)
            dve.wait_ge(e_row, 1)
            dve.tensor_scalar(wrk[:, :], srow[:, 0, :], wlo[:, 1:2], None, ALU.is_le).then_inc(e_row, 1)
            dve.wait_ge(e_row, 2)
            dve.scalar_tensor_tensor(ovl[:, :], srow[:, 1, :], wlo[:, 0:1], wrk[:, :], ALU.is_ge, ALU.mult).then_inc(e_row, 1)
            dve.wait_ge(e_row, 3)
            dve.scalar_tensor_tensor(srow[:, 0, :], ovl[:, :], -1000.0, tix[:, 1, :], ALU.mult, ALU.add)
            dve.tensor_tensor(srow[:, 1, :], ovl[:, :], tix[:, 0, :], ALU.mult).then_inc(e_row, 1)
            dve.wait_ge(e_row, 4)
            dve.tensor_reduce(tab[:, 3:4], srow[:, 0, :], AX.X, ALU.min)
            dve.tensor_reduce(tab[:, 4:5], srow[:, 1, :], AX.X, ALU.max).then_inc(e_row, 1)
            dve.wait_ge(e_row, 5)
            dve.tensor_scalar(tab[:, 0:1], tab[:, 3:4], float(NT - 3), None, ALU.min).then_inc(e_base, 1)
            dve.wait_ge(e_base, 1)
            dve.tensor_tensor(tab[:, 5:6], tab[:, 4:5], tab[:, 0:1], ALU.subtract).then_inc(e_base, 1)
            dve.wait_ge(e_base, 2)
            dve.tensor_scalar(tab[:, 1:2], tab[:, 5:6], 3.0, None, ALU.max).then_inc(e_row, 1)
            dve.wait_ge(e_tr, 2)
            dve.tensor_copy(tab[:, 2:3], ps[0:32, 4, 0:1]).then_inc(e_base, 1)
            dve.wait_ge(e_base, 3)
            dve.wait_ge(e_row, 6)
            dve.tensor_copy(tabi[:, :], tab[:, 0:4]).then_inc(e_row, 1)

            dve.sem_inc(oh_free, OHS)
            dve.sem_inc(c_free, 2)
            dve.sem_inc(ct_tr, 6)
            dve.sem_inc(ct_done, 2)
            dve.sem_inc(mb_done, 2)
            dve.wait_ge(tab_in, 16)
            dve.wait_ge(kbc_in, 48)
            with dve.Fori(0, NW // 2) as wi:
                for jw in range(2):
                    w = 2 * wi + jw
                    tile0 = dve.value_load(tabrow[0:1, ds(4 * w, 1)], min_val=0, max_val=NT - 3)
                    count = dve.value_load(tabrow[0:1, ds(4 * w + 1, 1)], min_val=3, max_val=NT)
                    first = dve.value_load(tabrow[0:1, ds(4 * w + 2, 1)], min_val=0, max_val=NW * NT)
                    with dve.Fori(0, count) as jj:
                        slot = (first + jj) % OHS
                        dve.wait_ge(oh_free, first + jj + 1)
                        dve.tensor_scalar(oh_s[0:ET, ds(slot, 1), :].rearrange("p o n -> p (o n)"), iota_s[0:ET, :], srcT[0:ET, ds(tile0 + jj, 1)], None,
                                          ALU.is_equal).then_inc(oh_rdy, 1)
                        dve.tensor_scalar(oh_k[0:ET, ds(slot, 1), 0:WK].rearrange("p o n -> p (o n)"), iota_k[0:ET, :], keyT[0:ET, ds(tile0 + jj, 1)],
                                          neg_w[0:ET, ds(w, 1)], ALU.subtract, ALU.is_equal).then_inc(oh_rdy, 1)
                for jw in range(2):
                    w = 2 * wi + jw
                    dve.wait_ge(c_free, w + 3)
                    dve.wait_ge(mb_out[jw], 16 * wi)
                    dve.tensor_scalar(mb[jw][0:WK, :], c_row[jw][0:WK, :], 0.0, BIG, ALU.is_equal, ALU.mult).then_inc(mb_done, 1)
                    dve.wait_ge(mb_done, w + 3)
                    dve.wait_ge(mk_step, 5 * w)
                    dve.memset(tick[:, jw:jw + 1], 0.0)
                    for h in range(H):
                        dve.tensor_tensor_reduce(out=tt_junk[h][0:WK, :], in0=mb[jw][0:WK, :], in1=kbc[0:WK, h, :], scale=1.0, scalar=2 * BIG,
                                                 op0=ALU.add, op1=ALU.max, accum_out=mk4[jw][0:WK, h:h + 1]).then_inc(mk_step, 1)
                    dve.wait_ge(mk_step, 5 * w + 4)
                    dve.tensor_copy(mkt[0:WK, :, ds(w, 1)].rearrange("p h o -> p (h o)"), mk4[jw][0:WK, :]).then_inc(mk_step, 1)

            def softmax_tables(t0, nh, tr_count, q_sem, q_count, mr, qr, al, al2, mx, mx2, tq):
                dve.wait_ge(t_tr, tr_count)
                dve.tensor_copy(mr[0:NW, :, :], ps[0:NW, 0, 0:nh * WK].rearrange("p (h k) -> p h k", h=nh)).then_inc(t_step, 1)
                dve.wait_ge(q_sem, q_count)
                dve.wait_ge(t_step, t0 + 1)
                qv = qr[0:NW, :, :].rearrange("p (r h) d -> p r h d", r=R)
                for r in range(R):
                    dve.tensor_tensor(al[0:NW, r, :, :], mr[0:NW, :, :].rearrange("p h (d r) -> p h d r", r=R)[:, :, :, r], qv[:, r, :, :],
                                      ALU.add).then_inc(t_step, 1)
                dve.wait_ge(t_step, t0 + 4)
                flat = al[0:NW, :, :, :].rearrange("p a b c -> p (a b c)")
                dve.scalar_tensor_tensor(al2[0:NW, :, :, :].rearrange("p a b c -> p (a b c)"), flat, 0.2, flat, ALU.mult, ALU.max).then_inc(t_step, 1)
                dve.wait_ge(t_step, t0 + 5)
                dve.tensor_tensor(mx[0:NW, :, :], al2[0:NW, 0, :, :], al2[0:NW, 1, :, :], ALU.max).then_inc(t_step, 1)
                dve.wait_ge(t_step, t0 + 6)
                dve.tensor_tensor(mx2[0:NW, :, :], mx[0:NW, :, :], al2[0:NW, 2, :, :], ALU.max).then_inc(t_step, 1)
                dve.wait_ge(t_step, t0 + 7)
                dve.scalar_tensor_tensor(mx[0:NW, :, :], mx2[0:NW, :, :], 1e-2 * BIG, mx2[0:NW, :, :], ALU.is_gt, ALU.mult).then_inc(t_step, 1)
                dve.wait_ge(t_step, t0 + 8)
                tv = tq[0:NW, :, :, :].rearrange("p s (r h) d -> p s r h d", r=R)
                for r in range(R):
                    dve.tensor_tensor(tv[:, 0, r, :, :], qv[:, r, :, :], mx[0:NW, :, :], ALU.subtract).then_inc(t_step, 1)
                    dve.scalar_tensor_tensor(tv[:, 1, r, :, :], qv[:, r, :, :], 0.2, mx[0:NW, :, :], ALU.mult, ALU.subtract).then_inc(t_step, 1)

            softmax_tables(0, H, 1, qr_in, 16, mr, qr, al, al2, mx, mx2, tq)

            dve.sem_inc(p_done, 2)
            dve.sem_inc(plo_done, 2)
            dve.sem_inc(mm_done, 2)

            def head_z(h):
                dve.wait_ge(he_done, h + 1)
                dve.tensor_scalar(he_z[0:DB, :, :], he[0:DB, :, HD:HD + 1], 1e-30, None, ALU.max).then_inc(hz_step, 1)
                dve.wait_ge(hz_step, 2 * h + 1)
                dve.reciprocal(he_z[0:DB, :, :], he_z[0:DB, :, :]).then_inc(hz_step, 1)

            def head_out(h):
                dve.wait_ge(hx_step, 3 * h + 3)
                for b in range(0, NDB, 5):
                    last = dve.scalar_tensor_tensor(he_m[0:DB, b:b + 5, :], he_e[0:DB, b:b + 5, :], -1.0, he[0:DB, b:b + 5, 0:HD], ALU.add, ALU.add)
                last.then_inc(hf_done, 1)

            for h in range(H):
                for r in range(R):
                    i = h * R + r
                    a = r * H + h
                    dve.wait_ge(qb_in[i % 2], 16 * (i // 2 + 1))
                    with dve.Fori(0, NB // 2) as ss:
                        n = i * NB + 2 * ss
                        for j in range(2):
                            s = 2 * ss + j
                            dve.wait_ge(p_done, n + j + 1)
                            dve.tensor_scalar(vb[j][:, :], qbc[i % 2][:, 1, :], sub(kcol_leak, s)[:, a:a + 1], None, ALU.add).then_inc(v_step, 1)
                            dve.wait_ge(v_step, 2 * (n + j) + 1)
                            dve.scalar_tensor_tensor(vb[j][:, :], qbc[i % 2][:, 0, :], sub(kcol, s)[:, a:a + 1], vb[j][:, :],
                                                     ALU.add, ALU.max).then_inc(v_step, 1)
                        for j in range(2):
                            dve.wait_ge(x_done, n + j + 1)
                            dve.wait_ge(plo_done, n + j + 1)
                            dve.scalar_tensor_tensor(pf[j][:, :], vb[j][:, :], 2.0, CT[:, ds(2 * ss + j, 1), r, :].rearrange("p o n -> p (o n)"),
                                                     ALU.min, ALU.mult).then_inc(p_done, 1)
                    if h >= 1 and r == 0:
                        head_z(h - 1)
                    if h >= 1 and r == 1:
                        head_out(h - 1)
            head_z(H - 1)
            head_out(H - 1)

            with dve.Fori(0, NDB // 2) as ii:
                for j in range(2):
                    for hf in range(2):
                        b = 2 * ii + j
                        dve.wait_ge(th_done, 2 * NB + 2 * b + hf + 1)
                        dve.tensor_tensor(xt_lo[:, 3 * hf:3 * hf + 3, ds(b * DB, DB)],
                                          ps[:, 2 * j + hf, 0:3 * DB].rearrange("p (k n) -> p k n", k=3),
                                          xt_hi[:, 3 * hf:3 * hf + 3, ds(b * DB, DB)], ALU.subtract).then_inc(tl_done, 1)
            for m in range(2 * R):
                r, hf = m // 2, m % 2
                todo = [(k, q) for k in range(K6) for q in range(2)]
                assert len(todo) == DOTS2
                for i in range(NB):
                    if i == 0:
                        dve.wait_ge(w_in[m % 2], 16 * ((C_2 + m) // 2 + 1))
                        dve.wait_ge(qk2_in, 32)
                    for k, q in todo[i * DOTS2 // NB:(i + 1) * DOTS2 // NB]:
                        dve.wait_ge(dot_step, dots - 1)
                        col = q * R + r
                        dve.tensor_tensor_reduce(out=dot_junk[dots % 2][:, :], in0=wst[m % 2][:, k, :], in1=qk_bc[:, q, hf * CW:(hf + 1) * CW],
                                                 scale=1.0, scalar=0.0, op0=ALU.mult, op1=ALU.add,
                                                 accum_out=wqk_p[:, hf, k, col:col + 1]).then_inc(dot_step, 1)
                        dots += 1
                    n = (2 * R + m) * NB + i
                    dve.wait_ge(xr_hi, n + 1)
                    dve.tensor_tensor(ev2[i % 2][:, 0, :], ps[:, 6 + i % 2, 0:CW], ev2[i % 2][:, 1, :], ALU.subtract).then_inc(g_free, 1)
            dve.wait_ge(dot_step, dots)
            c6 = slice(0, 2 * R)
            dve.tensor_tensor(wqk[:, :, c6], wqk_p[:, 0, :, c6], wqk_p[:, 1, :, c6], ALU.add).then_inc(wqk_step, 1)
            dve.wait_ge(wqk_step, 4)
            dve.tensor_copy(wqk_hi[:, :, c6], wqk[:, :, c6]).then_inc(wqk_step, 1)
            dve.wait_ge(wqk_step, 5)
            dve.tensor_tensor(wqk_lo[:, :, c6], wqk[:, :, c6], wqk_hi[:, :, c6], ALU.subtract).then_inc(wqk_step, 1)
            for i in range(NB):
                dve.wait_ge(kc_done, NB + i + 1)
                dve.tensor_copy(kcol[:, i, 0:R], ps[:, 4 + i % 2, R:2 * R]).then_inc(kc_free, 1)
            dve.sem_inc(mk2_step, 4)
            dve.wait_ge(k2_in, 48)
            with dve.Fori(0, NW // 2) as wi:
                for jw in range(2):
                    w = 2 * wi + jw
                    dve.wait_ge(mb_in[jw], 16 * wi + 16)
                    dve.wait_ge(mk2_step, 2 * w + 4)
                    dve.memset(tick[:, jw:jw + 1], 0.0)
                    dve.tensor_tensor_reduce(out=tt_junk2[jw][0:WK, :], in0=mb2[jw][0:WK, :], in1=kbc2[0:WK, :], scale=1.0, scalar=2 * BIG,
                                             op0=ALU.add, op1=ALU.max, accum_out=mk2[jw][0:WK, :]).then_inc(mk2_step, 1)
                    dve.wait_ge(mk2_step, 2 * w + 5)
                    dve.tensor_copy(mkt[0:WK, 0, ds(w, 1)], mk2[jw][0:WK, :]).then_inc(mk2_step, 1)
            softmax_tables(14, 1, 2, q2_in, 16, mr2, qr2, al_2, al2_2, mx_2, mx2_2, tq2)

            def group_out(g):
                dve.wait_ge(mm_done, H * R * NB + (g + 1) * R * NB + 2)
                for b in range(2):
                    k = 8 * g + 4 * b
                    bank = 4 * (g % 2) + 2 * b
                    dve.wait_ge(ac_in[b], 16 * (g + 1))
                    if g >= 1:
                        dve.wait_ge(ot_out[b], 16 * g)
                    dve.tensor_scalar(oz[b][0:DB, 0:1], ps[0:DB, bank + 1, CW:CW + 1], 1e-30, None, ALU.max).then_inc(o_step, 1)
                    dve.wait_ge(o_step, k + 1)
                    dve.reciprocal(oz[b][0:DB, 1:2], oz[b][0:DB, 0:1]).then_inc(o_step, 1)
                    dve.wait_ge(o_step, k + 2)
                    for hf in range(2):
                        dve.scalar_tensor_tensor(ot[b][0:DB, hf * CW:(hf + 1) * CW], ps[0:DB, bank + hf, 0:CW], oz[b][0:DB, 1:2],
                                                 ac[b][0:DB, hf * CW:(hf + 1) * CW], ALU.mult, ALU.add).then_inc(o_step, 1)

            for g in range(NG):
                dve.wait_ge(q2b_in[g % 2], 16 * (g // 2 + 1))
                for r in range(R):
                    with dve.Fori(0, NB // 2) as ss:
                        n = H * R * NB + (g * R + r) * NB + 2 * ss
                        for j in range(2):
                            s = 2 * ss + j
                            dve.wait_ge(p_done, n + j + 1)
                            dve.tensor_scalar(v2[j][:, :], qb2[g % 2][:, 1, r, :], sub(kcol_leak, s)[:, r:r + 1], None, ALU.add).then_inc(v_step, 1)
                            dve.wait_ge(v_step, 2 * (n + j) + 1)
                            dve.scalar_tensor_tensor(v2[j][:, :], qb2[g % 2][:, 0, r, :], sub(kcol, s)[:, r:r + 1], v2[j][:, :],
                                                     ALU.add, ALU.max).then_inc(v_step, 1)
                        for j in range(2):
                            dve.wait_ge(x_done, n + j + 1)
                            dve.wait_ge(plo_done, n + j + 1)
                            dve.scalar_tensor_tensor(p2[j][:, :], v2[j][:, :], 2.0,
                                                     CT[:, ds(2 * ss + j, 1), r, g * GW:(g + 1) * GW].rearrange("p o n -> p (o n)"),
                                                     ALU.min, ALU.mult).then_inc(p_done, 1)
                    if r == 0 and g >= 1:
                        group_out(g - 1)
            group_out(NG - 1)

            def block_out(b):
                j = b % 2
                dve.wait_ge(f_mm, b + 1)
                if b >= 2:
                    dve.wait_ge(fo_st[j], 16 * (b // 2))
                for hf in range(2):
                    dve.scalar_tensor_tensor(fo[j][0:DB, hf * CW:(hf + 1) * CW], ps[0:DB, 2 + 2 * j + hf, 0:CW], 0.02 * 0.01,
                                             bf_bc[0:DB, hf * CW:(hf + 1) * CW], ALU.mult, ALU.add).then_inc(f_out, 1)

            for b in range(NDB):
                j = b % 2
                dve.wait_ge(fx_in[j], 16 * (b // 2 + 1))
                row_stats(fx[j][:, :], j, NB + b, DB)
                dve.wait_ge(rstd_done, NB + b + 1)
                if b >= 2:
                    dve.wait_ge(f_tr, b - 1)
                dve.tensor_scalar(fn[j][0:DB, :], fx[j][0:DB, :], mv[0:DB, j, 0:1], rstd[0:DB, j, :], ALU.subtract, ALU.mult).then_inc(f_step, 1)
                dve.wait_ge(f_step, 4 * b + 1)
                dve.tensor_scalar(fn[j][0:DB, :], fn[j][0:DB, :], 50.0, MAGIC, ALU.mult, ALU.add).then_inc(f_step, 1)
                dve.wait_ge(f_step, 4 * b + 2)
                dve.tensor_scalar(fn[j][0:DB, :], fn[j][0:DB, :], -MAGIC, 127.0, ALU.add, ALU.min).then_inc(f_step, 1)
                dve.wait_ge(f_step, 4 * b + 3)
                dve.tensor_scalar(fq[j][0:DB, :], fn[j][0:DB, :], -128.0, None, ALU.max).then_inc(f_step, 1)
                if b >= 1:
                    block_out(b - 1)
            block_out(NDB - 1)

        @block.tensor
        def _(pe):
            pe.wait_ge(consts_done, 4)
            with pe.Fori(0, NB // 2) as ii:
                for j in range(2):
                    i = 2 * ii + j
                    pe.wait_ge(ln_done, i + 1)
                    for hf in range(2):
                        pe.wait_ge(tl_done, 2 * i + hf + 1)
                        for k in range(3):
                            last = pe.transpose(ps[:, 2 * j + hf, k * P:(k + 1) * P], xn[j][:, (3 * hf + k) * P:(3 * hf + k + 1) * P], ident[:, :])
                        last.then_inc(tr_done, 1)

            def product(c, t_hi, t_lo, i, bank):
                hi, lo = w_hi[c % 2], w_lo[c % 2]
                for k in range(K6):
                    a_hi, a_lo = t_hi[:, k, ds(i * P, P)], t_lo[:, k, ds(i * P, P)]
                    pe.matmul(ps[:, bank, 0:CW], a_hi, hi[:, k, :], start=(k == 0), stop=False)
                    pe.matmul(ps[:, bank, 0:CW], a_hi, lo[:, k, :], start=False, stop=False)
                    last = pe.matmul(ps[:, bank, 0:CW], a_lo, hi[:, k, :], start=False, stop=(k == K6 - 1))
                return last

            pe.wait_ge(tl_done, 2 * NB + 4)
            for c in range(4):
                pe.wait_ge(w_lo_done, c + 1)
                with pe.Fori(0, NB // 2) as ii:
                    for j in range(2):
                        n = c * NB + 2 * ii + j
                        pe.wait_ge(g_free, n + 1)
                        product(c, xt_hi, xt_lo, 2 * ii + j, 6 + j).then_inc(g_done, 1)
            pe.wait_ge(kv_out, 2 * NB + 2)
            pe.wait_ge(g_free, 4 * NB + 2)
            for p6 in range(K6):
                o = p6 % 3 * (P + 1)
                for b in range(NB):
                    rows = P if b < NB - 1 else TAIL
                    last = pe.matmul(ps[:, 4 + p6 // 3, o:o + P + 1], KF[0:rows, b, p6 * P:(p6 + 1) * P], V[0:rows, b, p6, :],
                                     start=(b == 0), stop=(b == NB - 1))
                if p6 % 3 == 2:
                    last.then_inc(kvs_done, 1)
            for c in range(2):
                cc = C_Q + c
                pe.wait_ge(w_lo_done, cc + 1)
                with pe.Fori(0, 3) as fb:
                    for k in range(K6):
                        w_h, w_l = w_hi[cc % 2][:, k, ds(fb * P, P)], w_lo[cc % 2][:, k, ds(fb * P, P)]
                        for step, (w, t) in enumerate(((w_h, xt_hi), (w_h, xt_lo), (w_l, xt_hi))):
                            for g in range(NRG):
                                n = (3 * c + fb) * NRG + g
                                if k == 0 and step == 0:
                                    pe.wait_ge(q_free, n + 1)
                                last = pe.matmul(ps[:, g, 0:RG], w, t[:, k, g * RG:(g + 1) * RG], start=(k == 0 and step == 0),
                                                 stop=(k == K6 - 1 and step == 2))
                                if k == K6 - 1 and step == 2:
                                    last.then_inc(q_done, 1)
            pe.wait_ge(kvd_done, 2)
            pe.wait_ge(q_out, 2 * 3 * NRG + 2)
            for p6 in range(K6):
                for g in range(NRG):
                    n = NRG * p6 + g
                    pe.wait_ge(y_den, 3 * n)
                    pe.matmul(ps[:, g % 2, 0:RG], kvd[:, p6, :], QF[:, p6, g * RG:(g + 1) * RG], start=True, stop=True)
                    pe.matmul(ps[:, 2 + g % 2, 0:RG], zd[:, p6, :], QF[:, p6, g * RG:(g + 1) * RG], start=True, stop=True).then_inc(y_done, 1)
            pe.wait_ge(y_lo, K6 * NRG + 2)
            for c in range(2):
                cc = C_O + c
                pe.wait_ge(w_lo_done, cc + 1)
                with pe.Fori(0, NB // 2) as ii:
                    for j in range(2):
                        pe.wait_ge(g_free, 4 * NB + c * NB + 2 * ii + j + 1)
                        product(cc, yt_hi, yt_lo, 2 * ii + j, 6 + j).then_inc(g_done, 1)

            for m in range(2 * R):
                cc = C_X + m
                pe.wait_ge(w_lo_done, cc + 1)
                with pe.Fori(0, NB // 2) as ii:
                    for j in range(2):
                        pe.wait_ge(g_free, 6 * NB + m * NB + 2 * ii + j + 1)
                        product(cc, xt_hi, xt_lo, 2 * ii + j, 6 + j).then_inc(g_done, 1)
            pe.wait_ge(wqk_step, 3)
            for i in range(NB):
                pe.wait_ge(kc_free, i + 1)
                for k in range(K6):
                    a_hi, a_lo = xt_hi[:, k, i * P:(i + 1) * P], xt_lo[:, k, i * P:(i + 1) * P]
                    o = ps[:, 4 + i % 2, 0:2 * R * H]
                    pe.matmul(o, a_hi, wqk_hi[:, k, :], start=(k == 0), stop=False)
                    pe.matmul(o, a_hi, wqk_lo[:, k, :], start=False, stop=False)
                    last = pe.matmul(o, a_lo, wqk_hi[:, k, :], start=False, stop=(k == K6 - 1))
                last.then_inc(kc_done, 1)
            for g in range(NRG):
                for k in range(K6):
                    for step, (w, t) in enumerate(((wqk_hi, xt_hi), (wqk_hi, xt_lo), (wqk_lo, xt_hi))):
                        last = pe.matmul(ps[0:2 * R * H, g, 0:RG], w[:, k, :], t[:, k, g * RG:(g + 1) * RG], start=(k == 0 and step == 0),
                                         stop=(k == K6 - 1 and step == 2))
                last.then_inc(kr_done, 1)

            pe.wait_ge(e_step, 4)
            for c, rows in enumerate((P, P, NT - 2 * P)):
                o = slice(c * P, c * P + rows)
                pe.transpose(ps[0:ET, 0, o], e_key[0:rows, c, :], ident[0:rows, 0:rows])
                pe.transpose(ps[0:ET, 1, o], e_flt[0:rows, c, 0, :], ident[0:rows, 0:rows])
                for m in range(2):
                    last = pe.transpose(ps[0:32, 2 + m, o], tbc[0:rows, c, m, :], ident[0:rows, 0:rows])
            last.then_inc(e_tr, 1)
            pe.wait_ge(e_row, 6)
            pe.wait_ge(e_const, 2)
            pe.matmul(ps[0:32, 4, 0:1], ltri[:, :], tab[:, 1:2], start=True, stop=True).then_inc(e_tr, 1)

            pe.wait_ge(tab_in, 16)
            with pe.Fori(0, NW // 2) as wi:
                for jw in range(2):
                    w = 2 * wi + jw
                    count = pe.value_load(tabrow[0:1, ds(4 * w + 1, 1)], min_val=3, max_val=NT)
                    first = pe.value_load(tabrow[0:1, ds(4 * w + 2, 1)], min_val=0, max_val=NW * NT)

                    def tile(jj, start, stop, jw=jw, first=first):
                        slot = (first + jj) % OHS
                        pe.wait_ge(oh_rdy, 2 * (first + jj) + 2)
                        for q in range(3):
                            last = pe.matmul(ps[:, 3 * jw + q, 0:ND // 3], oh_k[0:ET, ds(slot, 1), :].rearrange("p o n -> p (o n)"),
                                             oh_s[0:ET, ds(slot, 1), q * ND // 3:(q + 1) * ND // 3].rearrange("p o n -> p (o n)"), start=start, stop=stop,
                                             skip_group_check=True)
                        last.then_inc(oh_free, 1)

                    pe.wait_ge(c_free, w + 1)
                    tile(0, True, False)
                    with pe.Fori(1, count - 1) as jj:
                        tile(jj, False, False)
                    tile(count - 1, False, True)
                for jw in range(2):
                    w = 2 * wi + jw
                    pe.wait_ge(c_free, w + 3)
                    for g in range(3):
                        pe.wait_ge(ct_done, 3 * w + g + 1)
                        for i in range(4 * g, min(4 * g + 4, NB)):
                            n = min(P, ND - i * P)
                            last = pe.transpose(ps[0:n, 6 + (3 * jw + g) % 2, (i - 4 * g) * WK:(i - 4 * g + 1) * WK],
                                                c_row[jw][0:WK, i * P:i * P + n], ident[0:WK, 0:WK])
                        last.then_inc(ct_tr, 1)
            pe.wait_ge(mk_step, 5 * NW)
            for h in range(H):
                last = pe.transpose(ps[0:NW, 0, h * WK:(h + 1) * WK], mkt[0:WK, h, :], ident[0:WK, 0:WK])
            last.then_inc(t_tr, 1)

            pe.wait_ge(one_done, 2)

            def unit_products(h, r, s, j, first, last_unit):
                rows = xrh[h % 2][:, r, :, :]
                lo = rows[:, ds(s, 1), 0:HD].rearrange("p o n -> p (o n)")
                hi = rows[:, ds(s, 1), HD:2 * HD + 1].rearrange("p o n -> p (o n)")
                for b in range(NDB):
                    o = b % 2 * (HD + 1)
                    out_hi, out_lo = ps[:, b // 2, o:o + HD + 1], ps[:, b // 2, o:o + HD]
                    p_hi, p_lo = ph[j][:, b * DB:b * DB + P], pl[j][:, b * DB:b * DB + P]
                    pe.matmul(out_hi, p_hi, hi, start=(first and b % 2 == 0), stop=False, skip_group_check=True)
                    pe.matmul(out_lo, p_hi, lo, start=False, stop=False, skip_group_check=True)
                    mm = pe.matmul(out_hi, p_lo, hi, start=False, stop=last_unit, skip_group_check=True)
                mm.then_inc(mm_done, 1)

            for h in range(H):
                pe.wait_ge(xrh_in[h % 2], 16 * (h // 2 + 1))
                if h >= 1:
                    pe.wait_ge(he_done, h)
                for r in range(R):
                    for s in range(2 if r == 0 else 0):
                        pe.wait_ge(plo_done, (h * R + r) * NB + s + 3)
                        unit_products(h, r, s, s, s == 0, False)
                    with pe.Fori(1 if r == 0 else 0, NB // 2) as ss:
                        for j in range(2):
                            pe.wait_ge(plo_done, (h * R + r) * NB + 2 * ss + j + 3)
                            unit_products(h, r, 2 * ss + j, j, False, False)

            pe.wait_ge(he_done, H)
            pe.wait_ge(pad_done, 1)
            with pe.Fori(0, NDB // 2) as ii:
                for j in range(2):
                    b = 2 * ii + j
                    pe.wait_ge(hn_in[j], 16 * ii + 16)
                    for hf in range(2):
                        pe.wait_ge(tl_done, 2 * NB + 2 * b + hf + 1)
                        for k in range(3):
                            last = pe.transpose(ps[:, 2 * j + hf, k * DB:(k + 1) * DB], hn[j][0:DB, (3 * hf + k) * P:(3 * hf + k + 1) * P],
                                                ident[0:DB, 0:DB])
                        last.then_inc(tr_done, 1)
            pe.wait_ge(tl_done, 4 * NB + 4)
            for m in range(2 * R):
                cc = C_2 + m
                pe.wait_ge(w_lo_done, cc + 1)
                with pe.Fori(0, NB // 2) as ii:
                    for j in range(2):
                        pe.wait_ge(g_free, 12 * NB + m * NB + 2 * ii + j + 1)
                        product(cc, xt_hi, xt_lo, 2 * ii + j, 6 + j).then_inc(g_done, 1)
            pe.wait_ge(wqk_step, 6)
            for i in range(NB):
                pe.wait_ge(kc_free, NB + i + 1)
                for k in range(K6):
                    a_hi, a_lo = xt_hi[:, k, i * P:(i + 1) * P], xt_lo[:, k, i * P:(i + 1) * P]
                    o = ps[:, 4 + i % 2, 0:2 * R]
                    pe.matmul(o, a_hi, wqk_hi[:, k, 0:2 * R], start=(k == 0), stop=False)
                    pe.matmul(o, a_hi, wqk_lo[:, k, 0:2 * R], start=False, stop=False)
                    last = pe.matmul(o, a_lo, wqk_hi[:, k, 0:2 * R], start=False, stop=(k == K6 - 1))
                last.then_inc(kc_done, 1)
            for g in range(NRG):
                for k in range(K6):
                    for step, (w, t) in enumerate(((wqk_hi, xt_hi), (wqk_hi, xt_lo), (wqk_lo, xt_hi))):
                        last = pe.matmul(ps[0:2 * R, g, 0:RG], w[:, k, 0:2 * R], t[:, k, g * RG:(g + 1) * RG], start=(k == 0 and step == 0),
                                         stop=(k == K6 - 1 and step == 2))
                last.then_inc(kr_done, 1)
            pe.wait_ge(mk2_step, 2 * NW + 4)
            pe.wait_ge(kr_out, 2 * NRG)
            pe.transpose(ps[0:NW, 0, 0:WK], mkt[0:WK, 0, :], ident[0:WK, 0:WK]).then_inc(t_tr, 1)

            pe.wait_ge(x2_in, 16 * R)
            pe.wait_ge(one_done, 4)
            pe.wait_ge(t_step, 16)

            def unit_products2(g, r, s, j, first):
                rows = x2[:, r, :, :]

                def cols(a, b):
                    return rows[:, ds(s, 1), a:b].rearrange("p o n -> p (o n)")

                for b in range(2):
                    bank = 4 * (g % 2) + 2 * b
                    p_hi, p_lo = ph2[j][:, b * DB:b * DB + P], pl2[j][:, b * DB:b * DB + P]
                    for p, off, n1 in ((p_hi, D, 1), (p_hi, 0, 0), (p_lo, D, 1)):
                        start = first and p is p_hi and n1 == 1
                        pe.matmul(ps[:, bank, 0:CW], p, cols(off, off + CW), start=start, stop=False, skip_group_check=True)
                        mm = pe.matmul(ps[:, bank + 1, 0:CW + n1], p, cols(off + CW, off + D + n1), start=start, stop=False, skip_group_check=True)
                mm.then_inc(mm_done, 1)

            for g in range(NG):
                if g >= 2:
                    pe.wait_ge(o_step, 8 * (g - 1))
                for r in range(R):
                    n0 = H * R * NB + (g * R + r) * NB
                    for s in range(2 if r == 0 else 0):
                        pe.wait_ge(plo_done, n0 + s + 3)
                        unit_products2(g, r, s, s, s == 0)
                    with pe.Fori(1 if r == 0 else 0, NB // 2) as ss:
                        for j in range(2):
                            pe.wait_ge(plo_done, n0 + 2 * ss + j + 3)
                            unit_products2(g, r, 2 * ss + j, j, False)

            pe.wait_ge(wf_done, 1)
            pe.wait_ge(o_step, 8 * NG)

            def ffn_product(b):
                j = b % 2
                pe.wait_ge(f_cp, b + 1)
                if b >= 2:
                    pe.wait_ge(f_out, 2 * (b - 1))
                for hf in range(2):
                    for k in range(K6):
                        mm = pe.matmul(ps[0:DB, 2 + 2 * j + hf, 0:CW], fqt[j][:, k, 0:DB], wf16[:, k, hf * CW:(hf + 1) * CW],
                                       start=(k == 0), stop=(k == K6 - 1))
                mm.then_inc(f_mm, 1)

            for b in range(NDB):
                pe.wait_ge(f_step, 4 * b + 4)
                if b >= 2:
                    pe.wait_ge(f_cp, b - 1)
                for k in range(K6):
                    last = pe.transpose(ps16[:, b % 2, k * DB:(k + 1) * DB], fq[b % 2][0:DB, k * P:(k + 1) * P], ident16[0:DB, 0:DB])
                last.then_inc(f_tr, 1)
                if b >= 1:
                    ffn_product(b - 1)
            ffn_product(NDB - 1)



_INS = ["x", "src", "dst", "edge_type_3", "L0_gnn_W1", "L0_gnn_q1", "L0_gnn_k1", "L0_gnn_b1", "L0_gnn_W2", "L0_gnn_q2",
        "L0_gnn_k2", "L0_gnn_b2", "L0_mix_W_qkv", "L0_mix_b_qkv", "L0_mix_W_out", "L0_mix_b_out", "L0_ffn_weight_t",
        "L0_ffn_bias"]


def kernel(**inputs):
    import numpy as _np
    import concourse.bacc as _bacc
    from concourse import mybir as _mybir
    from concourse.bass_utils import run_bass_kernel_spmd as _run

    nc = _bacc.Bacc("TRN2", target_bir_lowering=False, num_devices=1)
    arrays, args = {}, []
    for name in _INS:
        a = _np.asarray(inputs[name])
        if name[7:] in ("q1", "k1", "q2", "k2"):
            a = a.T
        a = _np.ascontiguousarray(a)
        if a.dtype == _np.int8:
            a = a.view(_np.int32)
        arrays[f"in_{name}"] = a
        args.append(nc.dram_tensor(f"in_{name}", a.shape, _mybir.dt.from_np(a.dtype), kind="ExternalInput").ap())
    out = nc.dram_tensor("out_x", (N, D), F32, kind="ExternalOutput").ap()
    build(nc, *args, out)
    r = _run(nc, [arrays], core_ids=[0])
    return r.results[0]["out_x"]
```

```python
from contextlib import ExitStack

import concourse.bass as bass
from concourse import mybir

F32 = mybir.dt.float32
F16 = mybir.dt.float16
BF16 = mybir.dt.bfloat16
I32 = mybir.dt.int32
I8 = mybir.dt.int8
U16 = mybir.dt.uint16
ALU = mybir.AluOpType
ACT = mybir.ActivationFunctionType
AX = mybir.AxisListType
ds = bass.ds

P = 128
N = 1250
D = 768
E = 40000
R = 3
H = 4
HD = D // H
K6 = D // P
NB = -(-N // P)
NPAD = NB * P
TAIL = N - (NB - 1) * P
WD = 42
WK = WD * R
NW = -(-N // WD)
ND = NW * WD
DB = 3 * WD
NDB = ND // DB
DTAIL = N - (NDB - 1) * DB
ET = 125
NT = E // ET
NP = NT // 2
CW = 384
XH = 2 * HD + 2
XR2 = 2 * D + 2
V2_0 = 2 * H * R * NB
NRG = 4
RG = NPAD // NRG
BIG = -1e30
GW = 2 * DB
NG = ND // GW
M2_0 = 1
KEEP = 12800
WT_TILES = 2 * R * K6
PW = 25
OHS = 4
MAGIC = 12582912.0


def build(nc, x, src, dst, et, W1, q1, k1, b1, W2, q2, k2, b2, Wqkv, bqkv, Wo, bo, wf, bf, W1t, W2t, out):
    ctx = ExitStack()
    with ctx:
        def sem(name):
            return ctx.enter_context(nc.semaphore(name))

        base = 16512
        used = [base]

        def keep(name, shape, dt, size):
            n = size
            for s in shape[1:]:
                n *= s
            t = nc.alloc_sbuf_tensor_at(name, shape, dt, offset=used[0])
            used[0] += -(-n // 32) * 32
            return t

        def place(name, shape, dt, offset):
            return nc.alloc_sbuf_tensor_at(name, shape, dt, offset=base + KEEP + -(-offset // 32) * 32)

        ident = keep("ident", [P, P], F32, 4)
        ident16 = keep("ident16", [P, P], F16, 2)
        iota_s = keep("iota_s", [P, ND], F16, 2)
        iota_k = keep("iota_k", [P, WK], F16, 2)
        neg_w = keep("neg_w", [P, NW], F32, 4)
        kcol = keep("kcol", [P, NB, R * H], F32, 4)
        kcol_leak = keep("kcol_leak", [P, NB, R * H], F32, 4)
        mkt = keep("mkt", [P, H, NW], F32, 4)
        stat = keep("stat", [P, 2, 2, 6], F32, 4)
        mv = keep("mv", [P, 2, 2], F32, 4)
        rstd = keep("rstd", [P, 2, 1], F32, 4)
        bq_col = keep("bq_col", [P, K6], F32, 4)
        cst = keep("cst", [P, 4], F32, 4)
        vare = keep("vare", [P, 2, 1], F32, 4)
        tick = keep("tick", [P, 2], F32, 4)
        ones = keep("ones", [P, P], F32, 4)
        tabrow = keep("tabrow", [1, 4 * 32], I32, 4)
        zm = keep("zm", [P, K6, 2 * K6], F32, 4)
        wqk_hi = keep("wqk_hi", [P, K6, 2 * R * H], F16, 2)
        wqk_lo = keep("wqk_lo", [P, K6, 2 * R * H], F16, 2)
        wqk2_hi = keep("wqk2_hi", [P, K6, 2 * R], F16, 2)
        wqk2_lo = keep("wqk2_lo", [P, K6, 2 * R], F16, 2)
        keyT = keep("keyT", [P, 2 * NT], F32, 4)
        srcT = keep("srcT", [P, 2 * NT], F32, 4)
        assert used[0] <= base + KEEP, used

        xt_hi = place("xt_hi", [P, K6, NPAD], F16, 0)
        xt_lo = place("xt_lo", [P, K6, NPAD], F16, 15360)
        wst = [place(f"wst{j}", [P, K6, CW], F32, 30720 + 9216 * j) for j in range(2)]
        w_hi = [place(f"w_hi{j}", [P, K6, CW], F16, 49152 + 4608 * j) for j in range(2)]
        w_lo = [place(f"w_lo{j}", [P, K6, CW], F16, 58368 + 4608 * j) for j in range(2)]
        X = place("X", [P, NB, D], F32, 67584)
        KF = place("KF", [P, NB, D], F32, 98304)
        V = place("V", [P, NB, K6, P + 1], F32, 129024)
        QF = place("QF", [P, K6, NPAD], F32, 159984)
        xn = [place(f"xn{j}", [P, D], F32, 159984 + 3072 * j) for j in range(2)]
        ev_t = [place(f"ev_t{j}", [P, CW], F32, 166400 + 1536 * j) for j in range(2)]
        ev_m = [place(f"ev_m{j}", [P, CW], F32, 169600 + 1536 * j) for j in range(2)]
        yt_hi = place("yt_hi", [P, K6, NPAD], F16, 98304)
        yt_lo = place("yt_lo", [P, K6, NPAD], F16, 98304 + 15360)
        q_t = [place(f"q_t{j}", [P, RG], F32, 129024 + 1280 * j) for j in range(2)]
        q_m = [place(f"q_m{j}", [P, RG], F32, 131584 + 1280 * j) for j in range(2)]
        kvd = place("kvd", [P, K6, P], F32, 134144)
        spread = place("spread", [2 * K6, K6, P], F32, 137216)
        rden = place("rden", [2 * K6, NPAD], F32, 129024)
        rbc = [place(f"rbc{j}", [P, RG], F32, 140288 + 1280 * j) for j in range(2)]
        yv = [place(f"yv{j}", [P, RG], F32, 142848 + 1280 * j) for j in range(2)]
        wt = [place(f"wt{j}", [P, D], F32, 148480 + 3072 * j) for j in range(3)]
        qkn = place("qkn", [P, K6, 2, H], F32, 157696)
        qkn2 = place("qkn2", [P, K6, 2], F32, 157888)
        kq = place("kq", [2 * R * H, NPAD], F32, 129024)
        ao = [place(f"ao{j}", [P, CW], F32, 145408 + 1536 * j) for j in range(2)]
        bk_bc = place("bk_bc", [P, 2 * D], F32, 190704)
        bsum = place("bsum", [P, D], F32, 196848)
        b2_bc0 = place("b2_bc0", [P, D], F32, 173056)
        ev = [place(f"ev{j}", [P, 2, 2, HD], F16, 67584 + 1536 * j) for j in range(2)]
        ev2 = [place(f"ev2_{j}", [P, 2, CW], F16, 67584 + 1536 * j) for j in range(2)]
        hn = [place(f"hn{j}", [P, D], F32, 70784 + 3072 * j) for j in range(2)]
        kq2 = place("kq2", [2 * R, NPAD], F32, 82944)
        CT = place("CT", [P, NB, R, ND], U16, 124160)
        assert 124160 + NB * R * ND * 2 <= 202600
        oh_s = place("oh_s", [P, OHS, ND], F16, 70656)
        oh_k = place("oh_k", [P, OHS, P], F16, 80736)
        c_row = place("c_row", [P, ND], F32, 81760)
        mb = [place(f"mb{j}", [P, ND], BF16, 86816 + 2560 * j) for j in range(2)]
        kbc = place("kbc", [P, H, ND], F32, 91936)
        tt_junk = [place(f"tt_junk{j}", [P, ND], BF16, 112096 + 2528 * j) for j in range(H)]
        mk4 = [place(f"mk4_{j}", [P, H], F32, 122208 + 32 * j) for j in range(2)]
        e_int = place("e_int", [P, 3, 3, ET], I32, 98304)
        e_flt = place("e_flt", [P, 3, 3, ET], F32, 102816)
        e_key = place("e_key", [P, 3, ET], F32, 107328)
        tmm = place("tmm", [P, 3, 2], F32, 108832)
        tbc = place("tbc", [P, 3, 2, 32], F32, 108864)
        srow = place("srow", [32, 2, NT], F32, 109632)
        wlo = place("wlo", [32, 2], F32, 112192)
        tix = place("tix", [32, 2, NT], F32, 112224)
        ovl = place("ovl", [32, NT], F32, 114784)
        wrk = place("wrk", [32, NT], F32, 116064)
        tab = place("tab", [32, 8], F32, 117344)
        tabi = place("tabi", [32, 4], I32, 117408)
        ltri = place("ltri", [32, 32], F32, 117440)
        qr = place("qr", [32, R * H, WD], F32, 105312)
        mr = place("mr", [32, H, WK], F32, 107328)
        al = place("al", [32, R, H, WD], F32, 109344)
        al2 = place("al2", [32, R, H, WD], F32, 111360)
        mx = place("mx", [32, H, WD], F32, 113376)
        mx2 = place("mx2", [32, H, WD], F32, 114048)
        tq = place("tq", [32, 2, R * H, WD], F32, 114720)
        xrh = [place(f"xrh{j}", [P, R, NB, XH], F16, (72064, 0)[j]) for j in range(2)]
        qbc = [place(f"qbc{j}", [P, 2, ND], F32, 95232 + 10080 * j) for j in range(2)]
        vb = [place(f"vb{j}", [P, ND], F32, 23168 + 5056 * j) for j in range(2)]
        pf = [place(f"pf{j}", [P, ND], F32, 33280 + 5056 * j) for j in range(2)]
        ph = [place(f"ph{j}", [P, ND + 4], F16, 43392 + 2528 * j) for j in range(2)]
        pl = [place(f"pl{j}", [P, ND + 4], F16, 48448 + 2528 * j) for j in range(2)]
        he = place("he", [P, NDB, HD + 1], F32, 53504)
        he_z = place("he_z", [P, NDB, 1], F32, 123072)
        he_m = place("he_m", [P, NDB, HD], F32, 61312)
        he_e = place("he_e", [P, NDB, HD], F32, 115392)
        b1_bc = place("b1_bc", [P, D], F32, 68992)
        x2 = [place(f"x2_{r}", [P, NB, XR2], F16, (70784, 0, 30784)[r]) for r in range(R)]
        qb2 = [place(f"qb2_{j}", [P, 2, R, GW], F32, 101568 + 6048 * j) for j in range(2)]
        v2 = [place(f"v2_{j}", [P, GW], F32, 113664 + 1024 * j) for j in range(2)]
        p2 = [place(f"p2_{j}", [P, GW], F32, 115712 + 1024 * j) for j in range(2)]
        ph2 = [place(f"ph2_{j}", [P, GW + 4], F16, 117760 + 512 * j) for j in range(2)]
        pl2 = [place(f"pl2_{j}", [P, GW + 4], F16, 118784 + 512 * j) for j in range(2)]
        ot = [place(f"ot{j}", [P, D], F32, (67712, 119808)[j]) for j in range(2)]
        ac = [place(f"ac{j}", [P, D], F32, 61568 + 3072 * j) for j in range(2)]
        oz = [place(f"oz{j}", [P, 2], F32, 122880 + 32 * j) for j in range(2)]
        kbc2 = place("kbc2", [P, ND], F32, 101568)
        mb2 = [place(f"mb2_{j}", [P, ND], BF16, 106624 + 2560 * j) for j in range(2)]
        tt_junk2 = [place(f"tt_junk2_{j}", [P, ND], BF16, 111744 + 2560 * j) for j in range(2)]
        qr2 = place("qr2", [32, R, WD], F32, 116864)
        mr2 = place("mr2", [32, 1, WK], F32, 117376)
        al_2 = place("al_2", [32, R, 1, WD], F32, 117888)
        al2_2 = place("al2_2", [32, R, 1, WD], F32, 118400)
        mx_2 = place("mx_2", [32, 1, WD], F32, 118912)
        mx2_2 = place("mx2_2", [32, 1, WD], F32, 119104)
        tq2 = place("tq2", [32, 2, R, WD], F32, 119296)
        mk2 = [place(f"mk2_{j}", [P, 1], F32, 120320 + 32 * j) for j in range(2)]
        wf8 = place("wf8", [P, K6, D // 4], I32, 0)
        wf16 = place("wf16", [P, K6, D], F16, 4608)
        bf_bc = place("bf_bc", [P, D], F32, 13824)
        fx = [place(f"fx{j}", [P, D], F32, 16896 + 3072 * j) for j in range(2)]
        fn = [place(f"fn{j}", [P, D], F32, 23040 + 3072 * j) for j in range(2)]
        fq = [place(f"fq{j}", [P, D], F16, 29184 + 1536 * j) for j in range(2)]
        fqt = [place(f"fqt{j}", [P, K6, P], F16, 32256 + 1536 * j) for j in range(2)]
        fo = [place(f"fo{j}", [P, D], F32, 35328 + 3072 * j) for j in range(2)]

        ps = ctx.enter_context(nc.psum_tensor("ps", [P, 8, 512], F32))
        ps16 = ps[:, :, :].bitcast(F16)

        def scratch(name, shape, dt):
            return nc.dram_tensor(name, shape, dt, kind="Internal").ap()

        acc_d = scratch("acc_d", (NPAD, D), F32)
        xr_d = scratch("xr_d", (H, R, NB, P, 2 * HD), F16)
        x2_d = scratch("x2_d", (R, NB, P, 2 * D), F16)
        kq_d = scratch("kq_d", (2 * R * H, NPAD), F32)
        kq2_d = scratch("kq2_d", (2 * R, NPAD), F32)
        mb_d = scratch("mb_d", (NW, WK, ND), BF16)
        tab_d = scratch("tab_d", (1, 4 * 32), I32)
        tq_d = scratch("tq_d", (2, R * H, ND), F32)
        tq2_d = scratch("tq2_d", (2, R, ND), F32)
        h_d = scratch("h_d", (ND, D), F32)
        y_d = scratch("y_d", (ND, D), F32)


        def sub(t, i):
            v = t[:, ds(i, 1)]
            if len(v.shape) == 2:
                return v
            names = "abcd"[:len(v.shape) - 2]
            return v.rearrange(f"p o {' '.join(names)} -> p (o {names[0]}) {' '.join(names[1:])}")

        consts_done = sem("consts_done")
        x_in = sem("x_in")
        bias_in = sem("bias_in")
        st_done = sem("st_done")
        mv_done = sem("mv_done")
        vare_done = sem("vare_done")
        rstd_done = sem("rstd_done")
        ln_done = sem("ln_done")
        tr_done = sem("tr_done")
        th_done = sem("th_done")
        tl_done = sem("tl_done")
        w_in = [sem(f"w_in{j}") for j in range(2)]
        w_hi_done = sem("w_hi_done")
        w_lo_done = sem("w_lo_done")
        g_done = sem("g_done")
        g_free = sem("g_free")
        kv_m = sem("kv_m")
        kv_e = sem("kv_e")
        kv_out = sem("kv_out")
        kvs_done = sem("kvs_done")
        kvd_done = sem("kvd_done")
        q_done = sem("q_done")
        q_free = sem("q_free")
        q_mm = sem("q_mm")
        q_ee = sem("q_ee")
        q_out = sem("q_out")
        r_mm = sem("r_mm")
        r_step = sem("r_step")
        y_done = sem("y_done")
        rbc_done = sem("rbc_done")
        y_v = sem("y_v")
        y_hi = sem("y_hi")
        y_lo = sem("y_lo")
        xb_done = sem("xb_done")
        ao_out = [sem(f"ao_out{j}") for j in range(2)]

        qkn_in = sem("qkn_in")
        wt_in = [sem(f"wt_in{j}") for j in range(3)]
        wt_used = sem("wt_used")
        xr_hi = sem("xr_hi")
        ev_out = [sem(f"ev_out{j}") for j in range(2)]
        wqk_step = sem("wqk_step")
        kc_done = sem("kc_done")
        kc_free = sem("kc_free")
        kl_done = sem("kl_done")
        kr_done = sem("kr_done")
        kr_out = sem("kr_out")
        kq_st = sem("kq_st")
        e_in = sem("e_in")
        e_step = sem("e_step")
        e_const = sem("e_const")
        e_tr = sem("e_tr")
        e_row = sem("e_row")
        e_base = sem("e_base")
        tab_st = sem("tab_st")
        tab_in = sem("tab_in")
        kbc_in = sem("kbc_in")
        ct_clear = sem("ct_clear")
        oh_rdy = sem("oh_rdy")
        oh_free = sem("oh_free")
        c_free = sem("c_free")
        ct_tr = sem("ct_tr")
        ct_done = sem("ct_done")
        mb_done = sem("mb_done")
        mb_out = [sem(f"mb_out{j}") for j in range(2)]
        mk_step = sem("mk_step")
        qr_in = sem("qr_in")
        t_tr = sem("t_tr")
        t_step = sem("t_step")
        tq_st = sem("tq_st")

        xrh_in = [sem(f"xrh_in{j}") for j in range(2)]
        qb_in = [sem(f"qb_in{j}") for j in range(2)]
        b1_in = sem("b1_in")
        one_done = sem("one_done")
        v_step = sem("v_step")
        x_done = sem("x_done")
        p_done = sem("p_done")
        phi_done = sem("phi_done")
        plo_done = sem("plo_done")
        mm_done = sem("mm_done")
        he_done = sem("he_done")
        hz_step = sem("hz_step")
        hm_step = sem("hm_step")
        hx_step = sem("hx_step")
        hf_done = sem("hf_done")
        h_st = sem("h_st")
        hn_in = [sem(f"hn_in{j}") for j in range(2)]
        pad_done = sem("pad_done")
        kq2_st = sem("kq2_st")
        k2_in = sem("k2_in")
        mb_in = [sem(f"mb_in{j}") for j in range(2)]
        mk2_step = sem("mk2_step")
        q2_in = sem("q2_in")
        x2_in = [sem(f"x2_in{r}") for r in range(R)]
        q2b_in = [sem(f"q2b_in{j}") for j in range(2)]
        ac_in = [sem(f"ac_in{j}") for j in range(2)]
        o_step = sem("o_step")
        ot_out = [sem(f"ot_out{j}") for j in range(2)]
        wf_in = sem("wf_in")
        wf_done = sem("wf_done")
        fx_in = [sem(f"fx_in{j}") for j in range(2)]
        f_step = sem("f_step")
        f_tr = sem("f_tr")
        f_cp = sem("f_cp")
        f_mm = sem("f_mm")
        f_out = sem("f_out")
        fo_done = sem("fo_done")
        fo_st = [sem(f"fo_st{j}") for j in range(2)]

        def chunks():
            out = [Wqkv[:, D + c * CW:D + (c + 1) * CW] for c in range(4)]
            out += [Wqkv[:, c * CW:(c + 1) * CW] for c in range(2)]
            out += [Wo[:, c * CW:(c + 1) * CW] for c in range(2)]
            out += [W1[r, :, c * CW:(c + 1) * CW] for r in range(R) for c in range(2)]
            return [w.rearrange("(k p) n -> p k n", p=P) for w in out]

        def weights_free(eng, c):
            if c < C_Q:
                eng.wait_ge(g_done, NB * (c + 1))
            elif c < C_O:
                eng.wait_ge(q_done, 3 * NRG * (c - C_Q + 1))
            else:
                eng.wait_ge(g_done, NB * (c - 1))

        CH = chunks()

        def w1_segments():
            out, p = [], 0
            while p < NW // 2:
                def chunk(w):
                    return 2 * w // NB if w < PW else None
                q = p + 1
                while q < NW // 2 and q != 1 and (chunk(2 * q), chunk(2 * q + 1)) == (chunk(2 * p), chunk(2 * p + 1)):
                    q += 1
                out.append((p, q, (chunk(2 * p), chunk(2 * p + 1))))
                p = q
            return out

        def window(eng, w, with_tile0=True):
            tile0 = eng.value_load(tabrow[0:1, ds(4 * w, 1)], min_val=0, max_val=NP - 2) if with_tile0 else None
            count = eng.value_load(tabrow[0:1, ds(4 * w + 1, 1)], min_val=2, max_val=NP)
            first = eng.value_load(tabrow[0:1, ds(4 * w + 2, 1)], min_val=0, max_val=NW * NP)
            return tile0, count, first

        def splittable(p1):
            return min(2 * R, min(4 * p1, 2 * PW) // NB + 2)

        def store_xr(sp, m, i, j):
            r, h0 = m // 2, m % 2 * 2
            sp.dma_start(xr_d[h0:h0 + 2, r, ds(i, 1), :, :].rearrange("h o p n -> p (o h) n"),
                         ev[j][:, :, :, :].rearrange("p h s n -> p h (s n)")).then_inc(ev_out[j], 16)

        CH2 = [W2[r, :, c * CW:(c + 1) * CW].rearrange("(k p) n -> p k n", p=P) for r in range(R) for c in range(2)]
        C_Q, C_O, C_X = 4, 6, 8
        C_2 = C_X + 2 * R

        def weights_load(sp, m):
            sp.wait_ge(w_hi_done, C_X + m - 1)
            sp.wait_ge(w_lo_done, C_X + m - 1)
            sp.dma_start(wst[m % 2][:, :, :], CH[C_X + m]).then_inc(w_in[m % 2], 16)

        def load_head(sp, g):
            sp.dma_start(xrh[g % 2][:, :, :, 0:2 * HD].rearrange("p r b n -> p (r b) n"),
                         xr_d[g].rearrange("r b p n -> p (r b) n")).then_inc(xrh_in[g % 2], 16)

        def store_h(sp, h):
            sp.wait_ge(hf_done, h + 1)
            sp.dma_start(h_d[:, h * HD:(h + 1) * HD].rearrange("(b p) n -> p b n", p=DB), he_m[0:DB, :, :]).then_inc(h_st, 16)

        def store_x2(sp, m, i, j):
            r, hf = m // 2, m % 2
            sp.dma_start(x2_d[r, ds(i, 1), :, :].rearrange("o p (s n) -> p (o s) n", s=2)[:, :, hf * CW:(hf + 1) * CW],
                         ev2[j][:, :, :]).then_inc(ev_out[j], 16)

        def load_q2(sp, g):
            sp.dma_start(qb2[g % 2][:, :, :, :].rearrange("p s r d -> p (s r) d"),
                         tq2_d[:, :, g * GW:(g + 1) * GW].rearrange("s r d -> (s r) d").unsqueeze(0).to_broadcast([P, 2 * R, GW])
                         ).then_inc(q2b_in[g % 2], 16)

        def store_y(sp, g):
            for b in range(2):
                sp.wait_ge(o_step, 8 * g + 4 * b + 4)
                sp.dma_start(y_d[(2 * g + b) * DB:(2 * g + b + 1) * DB, :], ot[b][0:DB, :]).then_inc(ot_out[b], 16)

        def store_out(sp, b):
            rows = DB if b < NDB - 1 else DTAIL
            sp.wait_ge(fo_done, b + 1)
            sp.dma_start(out[b * DB:b * DB + rows, :], fo[b % 2][0:rows, :]).then_inc(fo_st[b % 2], 16)

        block = ctx.enter_context(nc.Block())

        @block.sync
        def _(sp):
            for a, arr in enumerate((src, dst, et)):
                rows = arr.rearrange("(t e) -> t e", e=ET)
                sp.dma_start(e_int[:, 0:2, a, :], rows[0:2 * P, :].rearrange("(c p) e -> p c e", p=P)).then_inc(e_in, 16)
                sp.dma_start(e_int[0:NT - 2 * P, 2, a, :], rows[2 * P:NT, :]).then_inc(e_in, 16)
            sp.wait_ge(consts_done, 1)
            sp.dma_start(X[:, 0:NB - 1, :], x[0:(NB - 1) * P, :].rearrange("(b p) d -> p b d", p=P)).then_inc(x_in, 16)
            sp.dma_start(X[0:TAIL, NB - 1, :], x[(NB - 1) * P:N, :]).then_inc(x_in, 16)
            sp.dma_start(bk_bc[:, :], bqkv[D:3 * D].unsqueeze(0).to_broadcast([P, 2 * D])).then_inc(bias_in, 16)
            sp.dma_start(bq_col[:, :], bqkv[0:D].rearrange("(k p) -> p k", p=P), allow_slow_non_contiguous=True).then_inc(bias_in, 16)
            sp.dma_start(bsum[:, :], bo.unsqueeze(0).to_broadcast([P, D])).then_inc(bias_in, 16)
            sp.dma_start(b2_bc0[:, :], b2.unsqueeze(0).to_broadcast([P, D])).then_inc(bias_in, 16)
            for c, w in enumerate(CH[:C_X]):
                if c == 2:
                    sp.wait_ge(e_row, 7)
                    sp.dma_start(tab_d.rearrange("o (w c) -> (o w) c", c=4), tabi[:, :]).then_inc(tab_st, 16)
                    sp.wait_ge(tab_st, 16)
                    sp.dma_start(tabrow[:, :], tab_d[:, :]).then_inc(tab_in, 16)
                if c >= 2:
                    sp.wait_ge(w_hi_done, c - 1)
                    sp.wait_ge(w_lo_done, c - 1)
                sp.dma_start(wst[c % 2][:, :, :], w).then_inc(w_in[c % 2], 16)
            sp.wait_ge(kvs_done, 2)
            sp.dma_start(qkn[:, :, 0, :], q1.rearrange("(k p) h -> p k h", p=P), allow_slow_non_contiguous=True).then_inc(qkn_in, 16)
            sp.dma_start(qkn[:, :, 1, :], k1.rearrange("(k p) h -> p k h", p=P), allow_slow_non_contiguous=True).then_inc(qkn_in, 16)
            sp.dma_start(qkn2[:, :, 0:1], q2.rearrange("(k p) h -> p k h", p=P), allow_slow_non_contiguous=True).then_inc(qkn_in, 16)
            sp.dma_start(qkn2[:, :, 1:2], k2.rearrange("(k p) h -> p k h", p=P), allow_slow_non_contiguous=True).then_inc(qkn_in, 16)
            for t in range(WT_TILES):
                if t >= 3:
                    sp.wait_ge(wt_used, t - 2)
                w = (W1t, W2t)[t // (WT_TILES // 2)]
                sp.dma_start(wt[t % 3][:, :], w[t // K6 % R, t % K6 * P:(t % K6 + 1) * P, :]).then_inc(wt_in[t % 3], 16)
            sp.wait_ge(kr_out, NRG)
            sp.dma_start(kq_d[:, :], kq[:, :]).then_inc(kq_st, 16)
            for m in range(2):
                weights_load(sp, m)
            for c in range(2):
                with sp.Fori(0, NB // 2) as ii:
                    for j in range(2):
                        i = 2 * ii + j
                        sp.wait_ge(g_free, 4 * NB + c * NB + i + 3)
                        sp.dma_start(acc_d[ds(i * P, P), c * CW:(c + 1) * CW], ao[j][:, :]).then_inc(ao_out[j], 16)
            for j in range(2):
                sp.wait_ge(ao_out[j], 16 * NB + 16)

            sp.wait_ge(kq_st, 16)
            sp.wait_ge(kl_done, 1)
            sp.wait_ge(g_free, 6 * NB + 2)
            for r in range(R):
                rows = kq_d[R * H + r * H:R * H + (r + 1) * H, 0:ND]
                sp.dma_start(kbc[r:WK:R, :, :], rows.unsqueeze(0).to_broadcast([WD, H, ND])).then_inc(kbc_in, 16)
            loaded = 4
            for m in range(2, loaded):
                weights_load(sp, m)
            for p0, p1, chunk in w1_segments():
                with sp.Fori(p0, p1) as wi:
                    for jw in range(2):
                        w = 2 * wi + jw
                        sp.wait_ge(mb_done, w + 3)
                        sp.dma_start(mb_d[ds(w, 1), :, :].rearrange("o p n -> (o p) n"), mb[jw][0:WK, :]).then_inc(mb_out[jw], 16)
                        if chunk[jw] is not None:
                            for j in range(2):
                                sp.wait_ge(g_free, 6 * NB + 2 * w + j + 3)
                                store_xr(sp, chunk[jw], 2 * w + j - NB * chunk[jw], j)
                for m in range(loaded, min(2 * R, splittable(p1) + 2)):
                    weights_load(sp, m)
                loaded = min(2 * R, splittable(p1) + 2)
            for j in range(2):
                sp.wait_ge(ev_out[j], 16 * PW + 16)
                sp.wait_ge(mb_out[j], 16 * NW // 2 + 16)
            sp.wait_ge(mk_step, 5 * NW + 5)
            sp.wait_ge(ct_tr, 3 * NW + 3)
            sp.dma_start(qr[0:NW, :, :], kq_d[0:R * H, 0:ND].rearrange("a (w d) -> w a d", d=WD)).then_inc(qr_in, 16)
            load_head(sp, 0)
            sp.wait_ge(t_step, 14)
            sp.dma_start(tq_d.rearrange("s a (w d) -> w (s a) d", d=WD), tq[0:NW, :, :, :].rearrange("w s a d -> w (s a) d")).then_inc(tq_st, 16)
            with sp.Fori(PW, PW + NB // 2) as v:
                for j in range(2):
                    sp.wait_ge(g_free, 6 * NB + 2 * v + j + 3)
                    store_xr(sp, 2 * R - 1, 2 * v + j - NB * (2 * R - 1), j)
            for j in range(2):
                sp.wait_ge(ev_out[j], 16 * (PW + NB // 2) + 16)
            sp.wait_ge(tq_st, 16)

            sp.wait_ge(ct_done, 3 * NW + 2)
            sp.dma_start(b1_bc[:, :], b1.unsqueeze(0).to_broadcast([P, D])).then_inc(b1_in, 16)
            for h in range(H):
                if h >= 2:
                    sp.wait_ge(mm_done, (h - 1) * R * NB + 2)
                loads = ((1,), (), (2,), (3,))[h]
                for r in range(R):
                    i = h * R + r
                    if i >= 2:
                        sp.wait_ge(v_step, 2 * (i - 1) * NB)
                    sp.dma_start(qbc[i % 2][:, :, :], tq_d[:, r * H + h, :].unsqueeze(0).to_broadcast([P, 2, ND])).then_inc(qb_in[i % 2], 16)
                    if r == 0:
                        for g in loads:
                            load_head(sp, g)
                if h >= 1:
                    store_h(sp, h - 1)
            store_h(sp, H - 1)

            sp.wait_ge(h_st, 16 * H)
            sp.wait_ge(mm_done, H * R * NB + 2)
            for m in range(2):
                sp.dma_start(wst[m][:, :, :], CH2[m]).then_inc(w_in[m], 16)
            with sp.Fori(0, NDB // 2) as ii:
                for j in range(2):
                    b = 2 * ii + j
                    sp.wait_ge(tl_done, 2 * NB + 2 * b + 2)
                    sp.dma_start(hn[j][0:DB, :], h_d[ds(b * DB, DB), :]).then_inc(hn_in[j], 16)
            sp.wait_ge(kr_out, 2 * NRG)
            sp.dma_start(kq2_d[:, :], kq2[:, :]).then_inc(kq2_st, 16)
            sp.wait_ge(kq2_st, 16)
            for r in range(R):
                sp.dma_start(kbc2[r:WK:R, :], kq2_d[R + r, 0:ND].unsqueeze(0).to_broadcast([WD, ND])).then_inc(k2_in, 16)
            sp.dma_start(qr2[0:NW, :, :], kq2_d[0:R, 0:ND].rearrange("a (w d) -> w a d", d=WD)).then_inc(q2_in, 16)

            def weights_load2(m):
                sp.wait_ge(w_hi_done, C_2 + m - 1)
                sp.wait_ge(w_lo_done, C_2 + m - 1)
                sp.dma_start(wst[m % 2][:, :, :], CH2[m]).then_inc(w_in[m % 2], 16)

            for m in range(2 * R):
                if 2 <= m + 2 < 2 * R:
                    weights_load2(m + 2)
                with sp.Fori(0, NB // 2) as ii:
                    if M2_0 <= m < M2_0 + 3:
                        for jw in range(2):
                            w = 2 * (NB // 2 * (m - M2_0) + ii) + jw
                            sp.wait_ge(mk2_step, 2 * w + 1)
                            sp.dma_start(mb2[jw][0:WK, :], mb_d[ds(w, 1), :, :].rearrange("o p n -> (o p) n")).then_inc(mb_in[jw], 16)
                    for j in range(2):
                        sp.wait_ge(g_free, (12 + m) * NB + 2 * ii + j + 3)
                        store_x2(sp, m, 2 * ii + j, j)
                if m == 2:
                    for j in range(2):
                        sp.wait_ge(ev_out[j], 16 * (R * NB + 3 * NB // 2) + 16)
                    sp.dma_start(x2[0][:, :, 0:2 * D], x2_d[0].rearrange("b p n -> p b n")).then_inc(x2_in[0], 16)
                if m == 2 * R - 2:
                    sp.wait_ge(t_step, 28)
                    sp.dma_start(tq2_d.rearrange("s a (w d) -> w (s a) d", d=WD), tq2[0:NW, :, :, :].rearrange("w s a d -> w (s a) d")).then_inc(tq_st, 16)
                    sp.wait_ge(tq_st, 32)
                    for g in range(2):
                        load_q2(sp, g)
            for j in range(2):
                sp.wait_ge(ev_out[j], 16 * 2 * R * NB + 16)
            sp.wait_ge(g_done, 18 * NB)
            for r in range(1, R):
                sp.dma_start(x2[r][:, :, 0:2 * D], x2_d[r].rearrange("b p n -> p b n")).then_inc(x2_in[r], 16)

            for g in range(NG):
                if g >= 2:
                    sp.wait_ge(v_step, V2_0 + 2 * (g - 1) * R * NB)
                    load_q2(sp, g)
                if g >= 1:
                    sp.wait_ge(o_step, 8 * g)
                for b in range(2):
                    sp.dma_start(ac[b][0:DB, :], acc_d[(2 * g + b) * DB:(2 * g + b + 1) * DB, :]).then_inc(ac_in[b], 16)
                if g >= 1:
                    store_y(sp, g - 1)
            store_y(sp, NG - 1)
            for b in range(2):
                sp.wait_ge(ot_out[b], 16 * NG)

            sp.dma_start(wf8[:, :, :], wf.rearrange("(k p) n -> p k n", p=P)).then_inc(wf_in, 16)
            sp.dma_start(bf_bc[:, :], bf.unsqueeze(0).to_broadcast([P, D])).then_inc(wf_in, 16)
            for b in range(NDB):
                if b >= 2:
                    sp.wait_ge(fo_done, b - 1)
                sp.dma_start(fx[b % 2][0:DB, :], y_d[b * DB:(b + 1) * DB, :]).then_inc(fx_in[b % 2], 16)
                if b >= 1:
                    store_out(sp, b - 1)
            store_out(sp, NDB - 1)
            for j in range(2):
                sp.wait_ge(fo_st[j], 16 * NDB // 2)

        @block.gpsimd
        def _(pool):
            pool.memset(X[:, NB - 1, :], 0.0).then_inc(consts_done, 1)
            pool.memset(ident[:, :], 0.0)
            pool.memset(ones[:, :], 1.0)
            pool.memset(cst[:, 0:1], 1e-5)
            pool.memset(cst[:, 1:2], -0.5)
            pool.memset(cst[:, 2:3], 0.02)
            pool.memset(V[:, :, :, P:P + 1].rearrange("p b k o -> p (b k) o"), 1.0).then_inc(consts_done, 1)
            pool.wait_ge(consts_done, 2)
            pool.affine_select(out=ident[:, :], in_=ident[:, :], compare_op=ALU.not_equal, fill=1.0, base=0,
                               pattern=[[-1, P]], channel_multiplier=1).then_inc(consts_done, 1)
            pool.wait_ge(consts_done, 3)
            pool.tensor_copy(ident16[:, :], ident[:, :]).then_inc(consts_done, 1)

            pool.iota(wlo[:, :], [[WK - 1, 2]], base=0, channel_multiplier=WK, allow_small_or_imprecise_dtypes=True)
            pool.iota(tix[:, 0, :].rearrange("p (t u) -> p t u", u=2), [[1, NP], [0, 2]], base=1, channel_multiplier=0, allow_small_or_imprecise_dtypes=True)
            pool.iota(tix[:, 1, :].rearrange("p (t u) -> p t u", u=2), [[1, NP], [0, 2]], base=1000, channel_multiplier=0, allow_small_or_imprecise_dtypes=True)
            pool.affine_select(out=ltri[:, :], in_=ones[0:32, 0:32], compare_op=ALU.is_gt, fill=0.0, base=0,
                               pattern=[[1, 32]], channel_multiplier=-1).then_inc(e_const, 1)

            def w_lo_part(c):
                pool.wait_ge(w_hi_done, c + 1)
                if c >= 2:
                    weights_free(pool, c - 2)
                pool.tensor_tensor(w_lo[c % 2][:, :, :], wst[c % 2][:, :, :], w_hi[c % 2][:, :, :], ALU.subtract).then_inc(w_lo_done, 1)

            def rstd_part(j, n):
                pool.wait_ge(mv_done, n + 1)
                pool.tensor_tensor(vare[:, j, :], mv[:, j, 1:2], cst[:, 0:1], ALU.add).then_inc(vare_done, 1)
                pool.wait_ge(vare_done, n + 1)
                pool.tensor_tensor(rstd[:, j, :], vare[:, j, :], cst[:, 1:2], ALU.pow).then_inc(rstd_done, 1)

            with pool.Fori(0, NB // 2) as ii:
                for j in range(2):
                    rstd_part(j, 2 * ii + j)
            w_lo_part(0)
            w_lo_part(1)
            w_lo_part(2)
            w_lo_part(3)
            pool.iota(iota_s[:, :], [[1, ND]], base=0, channel_multiplier=0, allow_small_or_imprecise_dtypes=True)
            pool.iota(iota_k[:, :], [[1, WK]], base=0, channel_multiplier=0, allow_small_or_imprecise_dtypes=True)
            pool.iota(neg_w[:, :], [[-WK, NW]], base=0, channel_multiplier=0, allow_small_or_imprecise_dtypes=True).then_inc(consts_done, 1)
            pool.wait_ge(bias_in, 64)
            pool.tensor_tensor(bsum[:, :], bsum[:, :], b2_bc0[:, :], ALU.add).then_inc(xb_done, 1)
            pool.wait_ge(xb_done, 1)
            pool.wait_ge(ln_done, NB)
            w_lo_part(4)
            with pool.Fori(0, NB) as i:
                pool.tensor_tensor(sub(X, i), sub(X, i), bsum[:, :], ALU.add).then_inc(xb_done, 1)
            w_lo_part(5)
            w_lo_part(6)
            w_lo_part(7)
            for n in range(K6 * NRG):
                g, p6 = n // K6, n % K6
                pool.wait_ge(y_hi, n + 1)
                pool.tensor_tensor(yt_lo[:, p6, g * RG:(g + 1) * RG], yv[n % 2][:, :], yt_hi[:, p6, g * RG:(g + 1) * RG],
                                   ALU.subtract).then_inc(y_lo, 1)

            w_lo_part(C_X)
            pool.wait_ge(g_free, 6 * NB + 2)
            pool.memset(oh_k[:, :, :], 0.0).then_inc(ct_clear, 1)
            pool.memset(CT[:, NB - 1, :, :], 0).then_inc(ct_clear, 1)
            for m in range(1, 2 * R):
                w_lo_part(C_X + m)

            pool.wait_ge(b1_in, 16)
            for j in range(2):
                pool.memset(xrh[j][:, :, :, 2 * HD:2 * HD + 1].rearrange("p r b o -> p (r b) o"), 1.0)
                pool.memset(ph[j][:, ND:ND + 4], 0.0)
                pool.memset(pl[j][:, ND:ND + 4], 0.0).then_inc(one_done, 1)

            def head_tail(h):
                pool.wait_ge(hz_step, 2 * h + 2)
                if h >= 1:
                    pool.wait_ge(h_st, 16 * h)
                pool.tensor_tensor(he_m[0:DB, :, :], he[0:DB, :, 0:HD], he_z[0:DB, :, :].to_broadcast([DB, NDB, HD]), ALU.mult).then_inc(hm_step, 1)
                pool.wait_ge(hm_step, 2 * h + 1)
                pool.tensor_tensor(he_m[0:DB, :, :], he_m[0:DB, :, :], b1_bc[0:DB, h * HD:(h + 1) * HD].unsqueeze(1).to_broadcast([DB, NDB, HD]),
                                   ALU.add).then_inc(hm_step, 1)

            for h in range(H):
                for r in range(R):
                    with pool.Fori(0, NB // 2) as ss:
                        for j in range(2):
                            n = (h * R + r) * NB + 2 * ss + j
                            pool.wait_ge(phi_done, n + 1)
                            pool.wait_ge(mm_done, n + 1)
                            pool.tensor_tensor(pl[j][:, 0:ND], pf[j][:, :], ph[j][:, 0:ND], ALU.subtract).then_inc(plo_done, 1)
                    if r == 0 and h >= 1:
                        head_tail(h - 1)
            head_tail(H - 1)

            pool.wait_ge(h_st, 16 * H)
            pool.wait_ge(mm_done, H * R * NB + 2)
            pool.memset(xt_hi[:, :, ND:NPAD], 0.0)
            pool.memset(xt_lo[:, :, ND:NPAD], 0.0).then_inc(pad_done, 1)
            for m in range(2 * R):
                w_lo_part(C_2 + m)

            pool.wait_ge(tq_st, 32)
            pool.memset(x2[0][:, :, 2 * D:2 * D + 1], 1.0)
            for j in range(2):
                pool.memset(ph2[j][:, GW:GW + 4], 0.0)
                pool.memset(pl2[j][:, GW:GW + 4], 0.0).then_inc(one_done, 1)
            pool.wait_ge(g_done, 18 * NB)
            for r in range(1, R):
                pool.memset(x2[r][:, :, 2 * D:2 * D + 1], 1.0).then_inc(one_done, 1)
            for g in range(NG):
                for r in range(R):
                    with pool.Fori(0, NB // 2) as ss:
                        for j in range(2):
                            n = H * R * NB + (g * R + r) * NB + 2 * ss + j
                            pool.wait_ge(phi_done, n + 1)
                            pool.wait_ge(mm_done, n + 1)
                            pool.tensor_tensor(pl2[j][:, 0:GW], p2[j][:, :], ph2[j][:, 0:GW], ALU.subtract).then_inc(plo_done, 1)

            def add_x(b):
                pool.wait_ge(f_out, 2 * b + 2)
                pool.tensor_tensor(fo[b % 2][0:DB, :], fo[b % 2][0:DB, :], fx[b % 2][0:DB, :], ALU.add).then_inc(fo_done, 1)

            for b in range(NDB):
                rstd_part(b % 2, NB + b)
                if b >= 1:
                    add_x(b - 1)
            add_x(NDB - 1)

        @block.scalar
        def _(act):

            def w_hi_part(c):
                act.wait_ge(w_in[c % 2], 16 * (c // 2 + 1))
                if c >= 2:
                    weights_free(act, c - 2)
                act.activation(w_hi[c % 2][:, :, :], wst[c % 2][:, :, :], ACT.Copy).then_inc(w_hi_done, 1)

            w_hi_part(0)
            w_hi_part(1)
            with act.Fori(0, NB // 2) as ii:
                for j in range(2):
                    for hf in range(2):
                        n = 2 * (2 * ii + j) + hf
                        act.wait_ge(tr_done, n + 1)
                        act.activation(xt_hi[:, 3 * hf:3 * hf + 3, ds((2 * ii + j) * P, P)],
                                       ps[:, 2 * j + hf, 0:3 * P].rearrange("p (k n) -> p k n", k=3), ACT.Copy).then_inc(th_done, 1)
            for c in range(2):
                with act.Fori(0, NB // 2) as ii:
                    for j in range(2):
                        n = c * NB + 2 * ii + j
                        act.wait_ge(g_free, n + 3)
                        act.wait_ge(kv_out, n + 1)
                        act.activation(ev_m[j][:, :], ev_t[j][:, :], ACT.Relu, scale=-1.0).then_inc(kv_m, 1)
                        act.wait_ge(kv_m, n + 1)
                        act.activation(ev_m[j][:, :], ev_m[j][:, :], ACT.Exp, scale=-1.0).then_inc(kv_e, 1)
                w_hi_part(c + 2)
            w_hi_part(4)
            w_hi_part(5)
            for c in range(2):
                with act.Fori(0, 3) as fb:
                    for g in range(NRG):
                        n = (3 * c + fb) * NRG + g
                        act.wait_ge(q_free, n + 5)
                        act.wait_ge(q_out, n + 1)
                        act.activation(q_m[g % 2][:, :], q_t[g % 2][:, :], ACT.Relu, scale=-1.0).then_inc(q_mm, 1)
                        act.wait_ge(q_mm, n + 1)
                        act.activation(q_m[g % 2][:, :], q_m[g % 2][:, :], ACT.Exp, scale=-1.0).then_inc(q_ee, 1)
                w_hi_part(C_O + c)
            def y_hi_part(n):
                g, p6 = n // K6, n % K6
                act.wait_ge(y_v, n + 1)
                act.activation(yt_hi[:, p6, g * RG:(g + 1) * RG], yv[n % 2][:, :], ACT.Copy).then_inc(y_hi, 1)

            for n in range(K6 * NRG):
                act.wait_ge(y_done, n + 1)
                if n >= 2:
                    act.wait_ge(y_v, n - 1)
                act.activation(rbc[n % 2][:, :], ps[:, 2 + n % 2, 0:RG], ACT.Copy).then_inc(rbc_done, 1)
                if n >= 1:
                    y_hi_part(n - 1)
            y_hi_part(K6 * NRG - 1)
            act.wait_ge(wt_used, WT_TILES)
            act.activation(wqk_hi[:, :, :], ps[:, 4, 0:K6 * 2 * R * H].rearrange("p (k n) -> p k n", k=K6), ACT.Copy).then_inc(wqk_step, 1)
            act.activation(wqk2_hi[:, :, :], ps[:, 5, 0:K6 * 2 * R].rearrange("p (k n) -> p k n", k=K6), ACT.Copy).then_inc(wqk_step, 1)
            for g in range(NRG):
                act.wait_ge(kr_done, g + 1)
                act.activation(kq[:, g * RG:(g + 1) * RG], ps[0:2 * R * H, g, 0:RG], ACT.Copy).then_inc(kr_out, 1)
            act.wait_ge(kc_free, 1)
            act.activation(kcol_leak[:, :, :], kcol[:, :, :], ACT.Copy, scale=0.2).then_inc(kl_done, 1)

            act.sem_inc(ev_out[0], 16)
            act.sem_inc(ev_out[1], 16)
            w_hi_part(C_X)
            w_hi_part(C_X + 1)
            act.wait_ge(g_free, 6 * NB + 2)
            act.wait_ge(tab_in, 16)
            act.wait_ge(ct_clear, 2)
            for j in range(2):
                act.wait_ge(ao_out[j], 16 * NB + 16)

            def xr_hi_part(n, k, j):
                act.wait_ge(ev_out[j], 16 * k + 16)
                act.wait_ge(g_done, 6 * NB + n + 1)
                act.activation(ev[j][:, :, 1, :], ps[:, 6 + j, 0:CW].rearrange("p (h n) -> p h n", h=2), ACT.Copy).then_inc(xr_hi, 1)

            split = 2
            for p0, p1, chunk in w1_segments():
                with act.Fori(p0, p1) as wi:
                    for jw in range(2):
                        w = 2 * wi + jw
                        _, count, first = window(act, w, False)
                        act.wait_ge(ct_tr, 3 * w + 3)
                        act.wait_ge(mb_done, w + 2)
                        act.wait_ge(oh_free, first + count + OHS // 2)
                        act.activation(c_row[0:WK, :].rearrange("p (a n) -> p a n", a=3), ps[0:WK, 0:3, 0:ND // 3], ACT.Copy).then_inc(c_free, 1)
                        if chunk[jw] is not None:
                            for j in range(2):
                                xr_hi_part(2 * w + j, w, j)
                        for g in range(3):
                            act.wait_ge(ct_tr, 3 * w + g + 4)
                            if g < 2:
                                act.activation(CT[:, 4 * g:4 * g + 4, :, ds(w * WD, WD)],
                                               ps[:, 3 + g, 0:4 * WK].rearrange("p (i d r) -> p i r d", i=4, r=R), ACT.Copy).then_inc(ct_done, 1)
                            else:
                                rows = ND - (NB - 1) * P
                                act.activation(CT[:, 8, :, ds(w * WD, WD)], ps[:, 5, 0:WK].rearrange("p (d r) -> p r d", r=R), ACT.Copy)
                                act.activation(CT[0:rows, 9, :, ds(w * WD, WD)],
                                               ps[0:rows, 5, WK:2 * WK].rearrange("p (d r) -> p r d", r=R), ACT.Copy).then_inc(ct_done, 1)
                for m in range(split, splittable(p1)):
                    w_hi_part(C_X + m)
                split = splittable(p1)
            with act.Fori(PW, PW + NB // 2) as v:
                for j in range(2):
                    xr_hi_part(2 * v + j, v, j)

            def head_tail(h):
                act.wait_ge(hm_step, 2 * h + 2)
                if h >= 1:
                    act.wait_ge(hf_done, h)
                act.activation(he_e[0:DB, :, :], he_m[0:DB, :, :], ACT.Relu, scale=-1.0).then_inc(hx_step, 1)
                act.wait_ge(hx_step, 3 * h + 1)
                act.activation(he_e[0:DB, :, :], he_e[0:DB, :, :], ACT.Exp, scale=-1.0).then_inc(hx_step, 1)
                act.activation(he[0:DB, :, 0:HD], he_m[0:DB, :, :], ACT.Relu).then_inc(hx_step, 1)

            for h in range(H):
                for r in range(R):
                    with act.Fori(0, NB // 2) as ss:
                        n = (h * R + r) * NB + 2 * ss
                        for j in range(2):
                            act.wait_ge(v_step, 2 * (n + j) + 2)
                            act.activation(vb[j][:, :], vb[j][:, :], ACT.Exp).then_inc(x_done, 1)
                        for j in range(2):
                            act.wait_ge(p_done, n + j + 3)
                            act.wait_ge(mm_done, n + j + 1)
                            act.activation(ph[j][:, 0:ND], pf[j][:, :], ACT.Copy).then_inc(phi_done, 1)
                    if r == 1 and h >= 1:
                        head_tail(h - 1)
                act.wait_ge(mm_done, (h + 1) * R * NB + 2)
                if h >= 1:
                    act.wait_ge(hf_done, h)
                act.activation(he[0:DB, :, :].rearrange("p (a b) n -> p a (b n)", b=2), ps[0:DB, 0:NDB // 2, 0:2 * (HD + 1)], ACT.Copy).then_inc(he_done, 1)
            head_tail(H - 1)

            w_hi_part(C_2)
            w_hi_part(C_2 + 1)
            with act.Fori(0, NDB // 2) as ii:
                for j in range(2):
                    for hf in range(2):
                        b = 2 * ii + j
                        act.wait_ge(tr_done, 2 * NB + 2 * b + hf + 1)
                        act.activation(xt_hi[:, 3 * hf:3 * hf + 3, ds(b * DB, DB)],
                                       ps[:, 2 * j + hf, 0:3 * DB].rearrange("p (k n) -> p k n", k=3), ACT.Copy).then_inc(th_done, 1)
            for g in range(NRG):
                act.wait_ge(kr_done, NRG + g + 1)
                act.activation(kq2[:, g * RG:(g + 1) * RG], ps[0:2 * R, g, 0:RG], ACT.Copy).then_inc(kr_out, 1)
            act.wait_ge(kc_free, 2)
            act.activation(kcol_leak[:, :, 0:R], kcol[:, :, 0:R], ACT.Copy, scale=0.2).then_inc(kl_done, 1)
            for m in range(2 * R):
                with act.Fori(0, NB // 2) as ii:
                    for j in range(2):
                        n = (2 * R + m) * NB + 2 * ii + j
                        act.wait_ge(ev_out[j], 16 * ((2 * R + m) * NB // 2 + ii) + 16)
                        act.wait_ge(g_done, 6 * NB + n + 1)
                        act.activation(ev2[j][:, 1, :], ps[:, 6 + j, 0:CW], ACT.Copy).then_inc(xr_hi, 1)
                if m + 2 < 2 * R:
                    w_hi_part(C_2 + m + 2)

            for g in range(NG):
                for r in range(R):
                    with act.Fori(0, NB // 2) as ss:
                        n = H * R * NB + (g * R + r) * NB + 2 * ss
                        for j in range(2):
                            act.wait_ge(v_step, 2 * (n + j) + 2)
                            act.activation(v2[j][:, :], v2[j][:, :], ACT.Exp).then_inc(x_done, 1)
                        for j in range(2):
                            act.wait_ge(p_done, n + j + 3)
                            act.wait_ge(mm_done, n + j + 1)
                            act.activation(ph2[j][:, 0:GW], p2[j][:, :], ACT.Copy).then_inc(phi_done, 1)

            act.wait_ge(wf_in, 32)
            act.activation(wf16[:, :, :], wf8[:, :, :].bitcast(I8), ACT.Copy).then_inc(wf_done, 1)
            for b in range(NDB):
                act.wait_ge(f_tr, b + 1)
                act.activation(fqt[b % 2][:, :, 0:DB], ps16[:, b % 2, 0:K6 * DB].rearrange("p (k n) -> p k n", k=K6), ACT.Copy).then_inc(f_cp, 1)

        @block.vector
        def _(dve):
            dve.sem_inc(tl_done, 4)
            dve.sem_inc(g_free, 2)
            dve.sem_inc(q_free, 4)
            dve.sem_inc(y_lo, 2)
            dve.sem_inc(kv_out, 2)
            dve.sem_inc(q_out, 2)
            for j in range(2):
                dve.sem_inc(ao_out[j], 16)
            rest = NT - 2 * P
            dve.wait_ge(e_in, 96)
            dve.tensor_copy(e_flt[:, 0:2, :, :], e_int[:, 0:2, :, :])
            dve.tensor_copy(e_flt[0:rest, 2, :, :], e_int[0:rest, 2, :, :]).then_inc(e_step, 1)
            dve.wait_ge(e_step, 1)
            dve.scalar_tensor_tensor(e_key[:, 0:2, :], e_flt[:, 0:2, 1, :], 3.0, e_flt[:, 0:2, 2, :], ALU.mult, ALU.add)
            dve.scalar_tensor_tensor(e_key[0:rest, 2, :], e_flt[0:rest, 2, 1, :], 3.0, e_flt[0:rest, 2, 2, :], ALU.mult, ALU.add).then_inc(e_step, 1)
            dve.wait_ge(e_step, 2)
            for c, rows in enumerate((P, P, rest)):
                for m, op in enumerate((ALU.min, ALU.max)):
                    last = dve.tensor_reduce(tmm[0:rows, c, m:m + 1], e_key[0:rows, c, :], AX.X, op)
            last.then_inc(e_step, 1)
            dve.wait_ge(e_step, 3)
            dve.wait_ge(consts_done, 2)
            for c, rows in enumerate((P, P, rest)):
                for m in range(2):
                    last = dve.tensor_scalar(tbc[0:rows, c, m, :], ones[0:rows, 0:32], tmm[0:rows, c, m:m + 1], None, ALU.mult)
            last.then_inc(e_step, 1)
            dve.wait_ge(e_tr, 1)
            dve.tensor_copy(keyT[0:ET, 0:NT], ps[0:ET, 4, 0:NT])
            dve.tensor_copy(srcT[0:ET, 0:NT], ps[0:ET, 5, 0:NT])
            dve.tensor_copy(srow[:, 0, :], ps[0:32, 6, 0:NT])
            dve.tensor_copy(srow[:, 1, :], ps[0:32, 7, 0:NT]).then_inc(e_row, 1)
            dve.wait_ge(e_const, 1)
            dve.wait_ge(e_row, 1)
            dve.tensor_scalar(wrk[:, :], srow[:, 0, :], wlo[:, 1:2], None, ALU.is_le).then_inc(e_row, 1)
            dve.wait_ge(e_row, 2)
            dve.scalar_tensor_tensor(ovl[:, :], srow[:, 1, :], wlo[:, 0:1], wrk[:, :], ALU.is_ge, ALU.mult).then_inc(e_row, 1)
            dve.wait_ge(e_row, 3)
            dve.scalar_tensor_tensor(srow[:, 0, :], ovl[:, :], -1000.0, tix[:, 1, :], ALU.mult, ALU.add)
            dve.tensor_tensor(srow[:, 1, :], ovl[:, :], tix[:, 0, :], ALU.mult).then_inc(e_row, 1)
            dve.wait_ge(e_row, 4)
            dve.tensor_reduce(tab[:, 3:4], srow[:, 0, :], AX.X, ALU.min)
            dve.tensor_reduce(tab[:, 4:5], srow[:, 1, :], AX.X, ALU.max).then_inc(e_row, 1)
            dve.wait_ge(e_row, 5)
            dve.tensor_scalar(tab[:, 0:1], tab[:, 3:4], float(NP - 2), None, ALU.min).then_inc(e_base, 1)
            dve.wait_ge(e_base, 1)
            dve.tensor_tensor(tab[:, 5:6], tab[:, 4:5], tab[:, 0:1], ALU.subtract).then_inc(e_base, 1)
            dve.wait_ge(e_base, 2)
            dve.tensor_scalar(tab[:, 1:2], tab[:, 5:6], 2.0, None, ALU.max).then_inc(e_row, 1)
            dve.wait_ge(e_tr, 2)
            dve.tensor_copy(tab[:, 2:3], ps[0:32, 4, 0:1]).then_inc(e_base, 1)
            dve.wait_ge(e_base, 3)
            dve.wait_ge(e_row, 6)
            dve.tensor_copy(tabi[:, :], tab[:, 0:4]).then_inc(e_row, 1)
            dve.wait_ge(x_in, 32)

            def row_stats(src, j, n, rows=P):
                for hf in range(2):
                    dve.bn_stats(stat[0:rows, j, hf, :], src[0:rows, hf * CW:(hf + 1) * CW]).then_inc(st_done, 1)
                dve.wait_ge(st_done, 2 * n + 2)
                dve.memset(tick[:, j:j + 1], 0.0)
                dve.bn_aggr(mv[0:rows, j, :], stat[0:rows, j, :, :].rearrange("p a b -> p (a b)")).then_inc(mv_done, 1)

            def lo_half(i, j, hf):
                dve.wait_ge(th_done, 2 * i + hf + 1)
                dve.tensor_tensor(xt_lo[:, 3 * hf:3 * hf + 3, ds(i * P, P)],
                                  ps[:, 2 * j + hf, 0:3 * P].rearrange("p (k n) -> p k n", k=3),
                                  xt_hi[:, 3 * hf:3 * hf + 3, ds(i * P, P)], ALU.subtract).then_inc(tl_done, 1)

            with dve.Fori(0, NB // 2) as ii:
                for j in range(2):
                    row_stats(sub(X, 2 * ii + j), j, 2 * ii + j)
                for j in range(2):
                    i = 2 * ii + j
                    dve.wait_ge(rstd_done, i + 1)
                    dve.wait_ge(tl_done, 2 * i + 2)
                    dve.tensor_scalar(xn[j][:, :], sub(X, i), mv[:, j, 0:1], rstd[:, j, :], ALU.subtract, ALU.mult).then_inc(ln_done, 1)
                for j in range(2):
                    for hf in range(2):
                        lo_half(2 * ii + j, j, hf)

            dve.wait_ge(bias_in, 64)
            dve.wait_ge(tab_st, 16)
            for c in range(2):
                with dve.Fori(0, NB // 2) as ii:
                    for j in range(2):
                        n = c * NB + 2 * ii + j
                        dve.wait_ge(g_done, n + 1)
                        dve.wait_ge(kv_out, n + 1)
                        dve.tensor_tensor(ev_t[j][:, :], ps[:, 6 + j, 0:CW], bk_bc[:, c * CW:(c + 1) * CW], ALU.add).then_inc(g_free, 1)
                    for j in range(2):
                        n = c * NB + 2 * ii + j
                        dve.wait_ge(kv_e, n + 1)
                        dve.scalar_tensor_tensor(sub(KF, 2 * ii + j)[:, c * CW:(c + 1) * CW], ev_t[j][:, :], 0.0, ev_m[j][:, :],
                                                 ALU.max, ALU.add).then_inc(kv_out, 1)
            for c in range(2):
                with dve.Fori(0, NB // 2) as ii:
                    for j in range(2):
                        i = 2 * ii + j
                        n = (2 + c) * NB + i
                        dve.wait_ge(g_done, n + 1)
                        dve.tensor_tensor(sub(V, i)[:, 3 * c:3 * c + 3, 0:P], ps[:, 6 + j, 0:CW].rearrange("p (k n) -> p k n", k=3),
                                          bk_bc[:, D + c * CW:D + (c + 1) * CW].rearrange("p (k n) -> p k n", k=3), ALU.add).then_inc(g_free, 1)
            dve.wait_ge(kvs_done, 2)
            dve.memset(kvd[:, :, :], 0.0)
            dve.memset(zm[:, :, :], 0.0)
            dve.tensor_copy(spread[:, :, :].rearrange("p k (u n) -> p (k u) n", u=2),
                            ident[0:2 * K6, 0:2 * K6].unsqueeze(2).to_broadcast([2 * K6, 2 * K6, P // 2])).then_inc(kvd_done, 1)
            dve.wait_ge(kvd_done, 1)
            for p6 in range(K6):
                o = p6 % 3 * (P + 1)
                for hf in range(2):
                    h0, h1 = 64 * hf, 64 * hf + 64
                    dve.tensor_copy(kvd[h0:h1, p6, h0:h1], ps[h0:h1, 4 + p6 // 3, o + h0:o + h1])
                    last = dve.tensor_copy(zm[h0:h1, p6, 2 * p6 + hf:2 * p6 + hf + 1], ps[h0:h1, 4 + p6 // 3, o + P:o + P + 1])
            last.then_inc(kvd_done, 1)
            dve.wait_ge(xb_done, 1)
            for c in range(2):
                with dve.Fori(0, 3) as fb:
                    for g in range(NRG):
                        n = (3 * c + fb) * NRG + g
                        dve.wait_ge(q_done, n + 1)
                        dve.wait_ge(q_out, n + 1)
                        dve.tensor_scalar(q_t[g % 2][:, :], ps[:, g, 0:RG], sub(bq_col, 3 * c + fb), None, ALU.add).then_inc(q_free, 1)
                        if g % 2:
                            for g2 in (g - 1, g):
                                n2 = (3 * c + fb) * NRG + g2
                                dve.wait_ge(q_ee, n2 + 1)
                                dve.scalar_tensor_tensor(sub(QF, 3 * c + fb)[:, g2 * RG:(g2 + 1) * RG], q_t[g2 % 2][:, :], 0.0, q_m[g2 % 2][:, :],
                                                         ALU.max, ALU.add).then_inc(q_out, 1)
            for g in range(NRG):
                dve.wait_ge(r_mm, g + 1)
                dve.tensor_scalar(rden[:, g * RG:(g + 1) * RG], ps[0:2 * K6, g, 0:RG], 1e-6, None, ALU.max).then_inc(r_step, 1)

            def invert(g):
                dve.wait_ge(r_step, g + 1)
                dve.reciprocal(rden[:, g * RG:(g + 1) * RG], rden[:, g * RG:(g + 1) * RG]).then_inc(r_step, 1)

            for g in range(NRG):
                if g == 0:
                    invert(0)
                if g + 1 < NRG:
                    invert(g + 1)
                for p6 in range(K6):
                    n = K6 * g + p6
                    dve.wait_ge(rbc_done, n + 1)
                    dve.wait_ge(y_lo, n + 1)
                    dve.tensor_tensor(yv[n % 2][:, :], ps[:, n % 2, 0:RG], rbc[n % 2][:, :], ALU.mult).then_inc(y_v, 1)
            dve.wait_ge(wqk_step, 2)
            dve.tensor_tensor(wqk_lo[:, :, :], ps[:, 4, 0:K6 * 2 * R * H].rearrange("p (k n) -> p k n", k=K6), wqk_hi[:, :, :],
                              ALU.subtract).then_inc(wqk_step, 1)
            dve.tensor_tensor(wqk2_lo[:, :, :], ps[:, 5, 0:K6 * 2 * R].rearrange("p (k n) -> p k n", k=K6), wqk2_hi[:, :, :],
                              ALU.subtract).then_inc(wqk_step, 1)
            dve.wait_ge(kc_done, 1)
            dve.tensor_copy(kcol[:, :, :], ps[:, 4, 0:NB * 2 * R * H].rearrange("p (i n) -> p i n", i=NB)[:, :, R * H:2 * R * H]).then_inc(kc_free, 1)
            for c in range(2):
                with dve.Fori(0, NB // 2) as ii:
                    for j in range(2):
                        i = 2 * ii + j
                        dve.wait_ge(g_done, 4 * NB + c * NB + i + 1)
                        dve.wait_ge(ao_out[j], 16 * (c * NB // 2 + ii) + 16)
                        dve.wait_ge(xb_done, NB + 1)
                        dve.tensor_tensor(ao[j][:, :], ps[:, 6 + j, 0:CW], sub(X, i)[:, c * CW:(c + 1) * CW], ALU.add).then_inc(g_free, 1)

            dve.sem_inc(oh_free, OHS // 2)
            dve.sem_inc(c_free, 1)
            dve.sem_inc(ct_tr, 3)
            dve.sem_inc(ct_done, 3)
            dve.sem_inc(mb_done, 2)
            dve.sem_inc(mk_step, 5)
            dve.sem_inc(mb_out[0], 16)
            dve.sem_inc(mb_out[1], 16)
            dve.wait_ge(tab_in, 16)
            dve.wait_ge(ct_clear, 1)
            dve.wait_ge(consts_done, 5)

            def xr_lo_part(n, j):
                dve.wait_ge(xr_hi, n + 1)
                dve.tensor_tensor(ev[j][:, :, 0, :], ps[:, 6 + j, 0:CW].rearrange("p (h n) -> p h n", h=2), ev[j][:, :, 1, :],
                                  ALU.subtract).then_inc(g_free, 1)

            def maxima(w, jw):
                dve.wait_ge(mb_done, w + 3)
                dve.wait_ge(mk_step, 5 * w + 5)
                dve.memset(tick[:, jw:jw + 1], 0.0)
                for h in range(H):
                    dve.tensor_tensor_reduce(out=tt_junk[h][0:WK, :], in0=mb[jw][0:WK, :], in1=kbc[0:WK, h, :], scale=1.0, scalar=2 * BIG,
                                             op0=ALU.add, op1=ALU.max, accum_out=mk4[jw][0:WK, h:h + 1]).then_inc(mk_step, 1)

            def keep_maxima(w, jw):
                dve.wait_ge(mk_step, 5 * w + 9)
                dve.tensor_copy(mkt[0:WK, :, ds(w, 1)].rearrange("p h o -> p (h o)"), mk4[jw][0:WK, :]).then_inc(mk_step, 1)

            for p0, p1, chunk in w1_segments():
                with dve.Fori(p0, p1) as wi:
                    tile0, count, first = window(dve, 2 * wi)
                    for jw in range(2):
                        w = 2 * wi + jw
                        with dve.Fori(0, count) as jj:
                            slot = (first + jj) % (OHS // 2) * 2
                            t = 2 * (tile0 + jj)
                            dve.wait_ge(oh_free, first + jj + 1)
                            for u in range(2):
                                dve.tensor_scalar(oh_s[0:ET, ds(slot + u, 1), :].rearrange("p o n -> p (o n)"), iota_s[0:ET, :],
                                                  srcT[0:ET, ds(t + u, 1)], None, ALU.is_equal)
                                last = dve.tensor_scalar(oh_k[0:ET, ds(slot + u, 1), 0:WK].rearrange("p o n -> p (o n)"), iota_k[0:ET, :],
                                                         keyT[0:ET, ds(t + u, 1)], neg_w[0:ET, ds(w, 1)], ALU.subtract, ALU.is_equal)
                            last.then_inc(oh_rdy, 1)
                        if p0 == 0 and jw == 1:
                            dve.wait_ge(kbc_in, 48)
                        if p0 > 0 or jw > 0:
                            maxima(w - 1, 1 - jw)
                        if jw == 0:
                            tile0, count, first = window(dve, w + 1)
                        if p0 > 0 or jw > 0:
                            keep_maxima(w - 1, 1 - jw)
                        dve.wait_ge(c_free, w + 2)
                        dve.wait_ge(mb_out[jw], 16 * wi + 16)
                        dve.tensor_scalar(mb[jw][0:WK, :], c_row[0:WK, :], 0.0, BIG, ALU.is_equal, ALU.mult).then_inc(mb_done, 1)
                        if chunk[jw] is not None:
                            for j in range(2):
                                xr_lo_part(2 * w + j, j)
            maxima(NW - 1, 1)
            keep_maxima(NW - 1, 1)

            def softmax_tables(t0, nh, tr_count, q_sem, q_count, mr, qr, al, al2, mx, mx2, tq):
                dve.wait_ge(t_tr, tr_count)
                dve.tensor_copy(mr[0:NW, :, :], ps[0:NW, 0, 0:nh * WK].rearrange("p (h k) -> p h k", h=nh)).then_inc(t_step, 1)
                dve.wait_ge(q_sem, q_count)
                dve.wait_ge(t_step, t0 + 1)
                qv = qr[0:NW, :, :].rearrange("p (r h) d -> p r h d", r=R)
                for r in range(R):
                    dve.tensor_tensor(al[0:NW, r, :, :], mr[0:NW, :, :].rearrange("p h (d r) -> p h d r", r=R)[:, :, :, r], qv[:, r, :, :],
                                      ALU.add).then_inc(t_step, 1)
                dve.wait_ge(t_step, t0 + 4)
                flat = al[0:NW, :, :, :].rearrange("p a b c -> p (a b c)")
                dve.scalar_tensor_tensor(al2[0:NW, :, :, :].rearrange("p a b c -> p (a b c)"), flat, 0.2, flat, ALU.mult, ALU.max).then_inc(t_step, 1)
                dve.wait_ge(t_step, t0 + 5)
                dve.tensor_tensor(mx[0:NW, :, :], al2[0:NW, 0, :, :], al2[0:NW, 1, :, :], ALU.max).then_inc(t_step, 1)
                dve.wait_ge(t_step, t0 + 6)
                dve.tensor_tensor(mx2[0:NW, :, :], mx[0:NW, :, :], al2[0:NW, 2, :, :], ALU.max).then_inc(t_step, 1)
                dve.wait_ge(t_step, t0 + 7)
                dve.scalar_tensor_tensor(mx[0:NW, :, :], mx2[0:NW, :, :], 1e-2 * BIG, mx2[0:NW, :, :], ALU.is_gt, ALU.mult).then_inc(t_step, 1)
                dve.wait_ge(t_step, t0 + 8)
                tv = tq[0:NW, :, :, :].rearrange("p s (r h) d -> p s r h d", r=R)
                for r in range(R):
                    dve.tensor_tensor(tv[:, 0, r, :, :], qv[:, r, :, :], mx[0:NW, :, :], ALU.subtract).then_inc(t_step, 1)
                    dve.scalar_tensor_tensor(tv[:, 1, r, :, :], qv[:, r, :, :], 0.2, mx[0:NW, :, :], ALU.mult, ALU.subtract).then_inc(t_step, 1)

            for j in range(2):
                xr_lo_part(2 * PW + j, j)
            softmax_tables(0, H, 1, qr_in, 16, mr, qr, al, al2, mx, mx2, tq)
            with dve.Fori(PW + 1, PW + NB // 2) as v:
                for j in range(2):
                    xr_lo_part(2 * v + j, j)

            dve.sem_inc(p_done, 2)
            dve.sem_inc(plo_done, 2)
            dve.sem_inc(mm_done, 2)

            def head_z(h):
                dve.wait_ge(he_done, h + 1)
                dve.tensor_scalar(he_z[0:DB, :, :], he[0:DB, :, HD:HD + 1], 1e-30, None, ALU.max).then_inc(hz_step, 1)
                dve.wait_ge(hz_step, 2 * h + 1)
                dve.reciprocal(he_z[0:DB, :, :], he_z[0:DB, :, :]).then_inc(hz_step, 1)

            def head_out(h):
                dve.wait_ge(hx_step, 3 * h + 3)
                for b in range(0, NDB, 5):
                    last = dve.scalar_tensor_tensor(he_m[0:DB, b:b + 5, :], he_e[0:DB, b:b + 5, :], -1.0, he[0:DB, b:b + 5, 0:HD], ALU.add, ALU.add)
                last.then_inc(hf_done, 1)

            for h in range(H):
                for r in range(R):
                    i = h * R + r
                    a = r * H + h
                    dve.wait_ge(qb_in[i % 2], 16 * (i // 2 + 1))
                    with dve.Fori(0, NB // 2) as ss:
                        n = i * NB + 2 * ss
                        for j in range(2):
                            s = 2 * ss + j
                            dve.wait_ge(p_done, n + j + 1)
                            dve.tensor_scalar(vb[j][:, :], qbc[i % 2][:, 1, :], sub(kcol_leak, s)[:, a:a + 1], None, ALU.add).then_inc(v_step, 1)
                            dve.wait_ge(v_step, 2 * (n + j) + 1)
                            dve.scalar_tensor_tensor(vb[j][:, :], qbc[i % 2][:, 0, :], sub(kcol, s)[:, a:a + 1], vb[j][:, :],
                                                     ALU.add, ALU.max).then_inc(v_step, 1)
                        for j in range(2):
                            dve.wait_ge(x_done, n + j + 1)
                            dve.wait_ge(plo_done, n + j + 1)
                            dve.scalar_tensor_tensor(pf[j][:, :], vb[j][:, :], 2.0, CT[:, ds(2 * ss + j, 1), r, :].rearrange("p o n -> p (o n)"),
                                                     ALU.min, ALU.mult).then_inc(p_done, 1)
                    if h >= 1 and r == 0:
                        head_z(h - 1)
                    if h >= 1 and r == 1:
                        head_out(h - 1)
            head_z(H - 1)
            head_out(H - 1)

            with dve.Fori(0, NDB // 2) as ii:
                for j in range(2):
                    for hf in range(2):
                        b = 2 * ii + j
                        dve.wait_ge(th_done, 2 * NB + 2 * b + hf + 1)
                        dve.tensor_tensor(xt_lo[:, 3 * hf:3 * hf + 3, ds(b * DB, DB)],
                                          ps[:, 2 * j + hf, 0:3 * DB].rearrange("p (k n) -> p k n", k=3),
                                          xt_hi[:, 3 * hf:3 * hf + 3, ds(b * DB, DB)], ALU.subtract).then_inc(tl_done, 1)
            dve.wait_ge(kc_done, 2)
            dve.tensor_copy(kcol[:, :, 0:R], ps[:, 4, 0:NB * 2 * R].rearrange("p (i n) -> p i n", i=NB)[:, :, R:2 * R]).then_inc(kc_free, 1)
            dve.sem_inc(mk2_step, 4)
            for m in range(2 * R):
                if m == M2_0:
                    dve.wait_ge(k2_in, 48)
                with dve.Fori(0, NB // 2) as ii:
                    for j in range(2):
                        dve.wait_ge(xr_hi, (2 * R + m) * NB + 2 * ii + j + 1)
                        dve.tensor_tensor(ev2[j][:, 0, :], ps[:, 6 + j, 0:CW], ev2[j][:, 1, :], ALU.subtract).then_inc(g_free, 1)
                    if M2_0 <= m < M2_0 + 3:
                        for jw in range(2):
                            w = 2 * (NB // 2 * (m - M2_0) + ii) + jw
                            dve.wait_ge(mb_in[jw], 16 * (NB // 2 * (m - M2_0) + ii) + 16)
                            dve.wait_ge(mk2_step, 2 * w + 4)
                            dve.memset(tick[:, jw:jw + 1], 0.0)
                            dve.tensor_tensor_reduce(out=tt_junk2[jw][0:WK, :], in0=mb2[jw][0:WK, :], in1=kbc2[0:WK, :], scale=1.0, scalar=2 * BIG,
                                                     op0=ALU.add, op1=ALU.max, accum_out=mk2[jw][0:WK, :]).then_inc(mk2_step, 1)
                            dve.wait_ge(mk2_step, 2 * w + 5)
                            dve.tensor_copy(mkt[0:WK, 0, ds(w, 1)], mk2[jw][0:WK, :]).then_inc(mk2_step, 1)
                if m == 2 * R - 2:
                    softmax_tables(14, 1, 2, q2_in, 16, mr2, qr2, al_2, al2_2, mx_2, mx2_2, tq2)

            def group_out(g):
                dve.wait_ge(mm_done, H * R * NB + (g + 1) * R * NB + 2)
                for b in range(2):
                    k = 8 * g + 4 * b
                    bank = 4 * (g % 2) + 2 * b
                    dve.wait_ge(ac_in[b], 16 * (g + 1))
                    if g >= 1:
                        dve.wait_ge(ot_out[b], 16 * g)
                    dve.tensor_scalar(oz[b][0:DB, 0:1], ps[0:DB, bank + 1, CW:CW + 1], 1e-30, None, ALU.max).then_inc(o_step, 1)
                    dve.wait_ge(o_step, k + 1)
                    dve.reciprocal(oz[b][0:DB, 1:2], oz[b][0:DB, 0:1]).then_inc(o_step, 1)
                    dve.wait_ge(o_step, k + 2)
                    for hf in range(2):
                        dve.scalar_tensor_tensor(ot[b][0:DB, hf * CW:(hf + 1) * CW], ps[0:DB, bank + hf, 0:CW], oz[b][0:DB, 1:2],
                                                 ac[b][0:DB, hf * CW:(hf + 1) * CW], ALU.mult, ALU.add).then_inc(o_step, 1)

            for g in range(NG):
                dve.wait_ge(q2b_in[g % 2], 16 * (g // 2 + 1))
                for r in range(R):
                    with dve.Fori(0, NB // 2) as ss:
                        n = H * R * NB + (g * R + r) * NB + 2 * ss
                        for j in range(2):
                            s = 2 * ss + j
                            dve.wait_ge(p_done, n + j + 1)
                            dve.tensor_scalar(v2[j][:, :], qb2[g % 2][:, 1, r, :], sub(kcol_leak, s)[:, r:r + 1], None, ALU.add).then_inc(v_step, 1)
                            dve.wait_ge(v_step, 2 * (n + j) + 1)
                            dve.scalar_tensor_tensor(v2[j][:, :], qb2[g % 2][:, 0, r, :], sub(kcol, s)[:, r:r + 1], v2[j][:, :],
                                                     ALU.add, ALU.max).then_inc(v_step, 1)
                        for j in range(2):
                            dve.wait_ge(x_done, n + j + 1)
                            dve.wait_ge(plo_done, n + j + 1)
                            dve.scalar_tensor_tensor(p2[j][:, :], v2[j][:, :], 2.0,
                                                     CT[:, ds(2 * ss + j, 1), r, g * GW:(g + 1) * GW].rearrange("p o n -> p (o n)"),
                                                     ALU.min, ALU.mult).then_inc(p_done, 1)
                    if r == 0 and g >= 1:
                        group_out(g - 1)
            group_out(NG - 1)

            def block_out(b):
                j = b % 2
                dve.wait_ge(f_mm, b + 1)
                if b >= 2:
                    dve.wait_ge(fo_st[j], 16 * (b // 2))
                for hf in range(2):
                    dve.scalar_tensor_tensor(fo[j][0:DB, hf * CW:(hf + 1) * CW], ps[0:DB, 2 + 2 * j + hf, 0:CW], 0.02 * 0.01,
                                             bf_bc[0:DB, hf * CW:(hf + 1) * CW], ALU.mult, ALU.add).then_inc(f_out, 1)

            for b in range(NDB):
                j = b % 2
                dve.wait_ge(fx_in[j], 16 * (b // 2 + 1))
                row_stats(fx[j][:, :], j, NB + b, DB)
                dve.wait_ge(rstd_done, NB + b + 1)
                if b >= 2:
                    dve.wait_ge(f_tr, b - 1)
                dve.tensor_scalar(fn[j][0:DB, :], fx[j][0:DB, :], mv[0:DB, j, 0:1], rstd[0:DB, j, :], ALU.subtract, ALU.mult).then_inc(f_step, 1)
                dve.wait_ge(f_step, 4 * b + 1)
                dve.tensor_scalar(fn[j][0:DB, :], fn[j][0:DB, :], 50.0, MAGIC, ALU.mult, ALU.add).then_inc(f_step, 1)
                dve.wait_ge(f_step, 4 * b + 2)
                dve.tensor_scalar(fn[j][0:DB, :], fn[j][0:DB, :], -MAGIC, 127.0, ALU.add, ALU.min).then_inc(f_step, 1)
                dve.wait_ge(f_step, 4 * b + 3)
                dve.tensor_scalar(fq[j][0:DB, :], fn[j][0:DB, :], -128.0, None, ALU.max).then_inc(f_step, 1)
                if b >= 1:
                    block_out(b - 1)
            block_out(NDB - 1)

        @block.tensor
        def _(pe):
            pe.wait_ge(consts_done, 4)
            pe.wait_ge(e_step, 4)
            for c, rows in enumerate((P, P, NT - 2 * P)):
                o = slice(c * P, c * P + rows)
                pe.transpose(ps[0:ET, 4, o], e_key[0:rows, c, :], ident[0:rows, 0:rows])
                pe.transpose(ps[0:ET, 5, o], e_flt[0:rows, c, 0, :], ident[0:rows, 0:rows])
                for m in range(2):
                    last = pe.transpose(ps[0:32, 6 + m, o], tbc[0:rows, c, m, :], ident[0:rows, 0:rows])
            last.then_inc(e_tr, 1)
            pe.wait_ge(e_row, 6)
            pe.wait_ge(e_const, 1)
            pe.matmul(ps[0:32, 4, 0:1], ltri[:, :], tab[:, 1:2], start=True, stop=True).then_inc(e_tr, 1)

            with pe.Fori(0, NB // 2) as ii:
                for j in range(2):
                    i = 2 * ii + j
                    pe.wait_ge(ln_done, i + 1)
                    for hf in range(2):
                        pe.wait_ge(tl_done, 2 * i + hf + 1)
                        for k in range(3):
                            last = pe.transpose(ps[:, 2 * j + hf, k * P:(k + 1) * P], xn[j][:, (3 * hf + k) * P:(3 * hf + k + 1) * P], ident[:, :])
                        last.then_inc(tr_done, 1)

            def product(c, t_hi, t_lo, i, bank):
                hi, lo = w_hi[c % 2], w_lo[c % 2]
                for k in range(K6):
                    a_hi, a_lo = t_hi[:, k, ds(i * P, P)], t_lo[:, k, ds(i * P, P)]
                    pe.matmul(ps[:, bank, 0:CW], a_hi, hi[:, k, :], start=(k == 0), stop=False)
                    pe.matmul(ps[:, bank, 0:CW], a_hi, lo[:, k, :], start=False, stop=False)
                    last = pe.matmul(ps[:, bank, 0:CW], a_lo, hi[:, k, :], start=False, stop=(k == K6 - 1))
                return last

            pe.wait_ge(tl_done, 2 * NB + 4)
            for c in range(4):
                pe.wait_ge(w_lo_done, c + 1)
                with pe.Fori(0, NB // 2) as ii:
                    for j in range(2):
                        n = c * NB + 2 * ii + j
                        pe.wait_ge(g_free, n + 1)
                        product(c, xt_hi, xt_lo, 2 * ii + j, 6 + j).then_inc(g_done, 1)
            pe.wait_ge(kv_out, 2 * NB + 2)
            pe.wait_ge(g_free, 4 * NB + 2)
            for p6 in range(K6):
                o = p6 % 3 * (P + 1)
                for b in range(NB):
                    rows = P if b < NB - 1 else TAIL
                    last = pe.matmul(ps[:, 4 + p6 // 3, o:o + P + 1], KF[0:rows, b, p6 * P:(p6 + 1) * P], V[0:rows, b, p6, :],
                                     start=(b == 0), stop=(b == NB - 1))
                if p6 % 3 == 2:
                    last.then_inc(kvs_done, 1)
            def wq_tile(t):
                r, nb = t // K6 % R, t % K6
                pe.wait_ge(wt_in[t % 3], 16 * (t // 3 + 1))
                for k in range(K6):
                    if t < WT_TILES // 2:
                        o = ps[:, 4, k * 2 * R * H:(k + 1) * 2 * R * H].rearrange("p (t x) -> p t x", t=2)[:, :, r * H:(r + 1) * H]
                        q = qkn[:, nb, :, :]
                    else:
                        o = ps[:, 5, k * 2 * R:(k + 1) * 2 * R].rearrange("p (t x) -> p t x", t=2)[:, :, r]
                        q = qkn2[:, nb, :]
                    last = pe.matmul(o, wt[t % 3][:, k * P:(k + 1) * P], q, start=(t % (WT_TILES // 2) == 0 and k == 0), stop=(nb == K6 - 1),
                                     skip_group_check=True)
                last.then_inc(wt_used, 1)

            for c in range(2):
                cc = C_Q + c
                pe.wait_ge(w_lo_done, cc + 1)
                for fb in range(3):
                    for k in range(K6):
                        w_h, w_l = w_hi[cc % 2][:, k, fb * P:(fb + 1) * P], w_lo[cc % 2][:, k, fb * P:(fb + 1) * P]
                        for step, (w, t) in enumerate(((w_h, xt_hi), (w_h, xt_lo), (w_l, xt_hi))):
                            for g in range(NRG):
                                n = (3 * c + fb) * NRG + g
                                if k == 0 and step == 0:
                                    pe.wait_ge(q_free, n + 1)
                                last = pe.matmul(ps[:, g, 0:RG], w, t[:, k, g * RG:(g + 1) * RG], start=(k == 0 and step == 0),
                                                 stop=(k == K6 - 1 and step == 2))
                                if k == K6 - 1 and step == 2:
                                    last.then_inc(q_done, 1)
                    if c == 0 and fb == 0:
                        pe.wait_ge(kvd_done, 2)
                        pe.wait_ge(qkn_in, 64)
                    for t in range(3 * (3 * c + fb), 3 * (3 * c + fb) + 3):
                        wq_tile(t)
            for t in range(WT_TILES // 2, WT_TILES // 2 + 3):
                wq_tile(t)
            pe.wait_ge(q_out, 2 * 3 * NRG + 2)
            for g in range(NRG):
                for p6 in range(K6):
                    last = pe.matmul(ps[0:2 * K6, g, 0:RG], zm[:, p6, :], QF[:, p6, g * RG:(g + 1) * RG], start=(p6 == 0), stop=(p6 == K6 - 1))
                last.then_inc(r_mm, 1)
            for t in range(WT_TILES // 2 + 3, WT_TILES // 2 + 6):
                wq_tile(t)
            for n in range(K6 * NRG):
                g, p6 = n // K6, n % K6
                if p6 == 0:
                    pe.wait_ge(r_step, NRG + g + 1)
                if n >= 2:
                    pe.wait_ge(y_v, n - 1)
                pe.matmul(ps[:, n % 2, 0:RG], kvd[:, p6, :], QF[:, p6, g * RG:(g + 1) * RG], start=True, stop=True)
                pe.matmul(ps[:, 2 + n % 2, 0:RG], spread[:, p6, :], rden[:, g * RG:(g + 1) * RG], start=True, stop=True).then_inc(y_done, 1)
                if n % 2 and WT_TILES // 2 + 6 + n // 2 < WT_TILES:
                    wq_tile(WT_TILES // 2 + 6 + n // 2)
            def node_columns(hi, lo, n):
                for i in range(NB):
                    o = ps[:, 4, i * n:(i + 1) * n]
                    for k in range(K6):
                        a_hi, a_lo = xt_hi[:, k, i * P:(i + 1) * P], xt_lo[:, k, i * P:(i + 1) * P]
                        pe.matmul(o, a_hi, hi[:, k, :], start=(i == 0 and k == 0), stop=False, skip_group_check=True)
                        pe.matmul(o, a_hi, lo[:, k, :], start=False, stop=False, skip_group_check=True)
                        last = pe.matmul(o, a_lo, hi[:, k, :], start=False, stop=(k == K6 - 1), skip_group_check=True)
                last.then_inc(kc_done, 1)

            def node_rows(hi, lo, n):
                for g in range(NRG):
                    for k in range(K6):
                        for step, (w, t) in enumerate(((hi, xt_hi), (hi, xt_lo), (lo, xt_hi))):
                            last = pe.matmul(ps[0:n, g, 0:RG], w[:, k, :], t[:, k, g * RG:(g + 1) * RG], start=(k == 0 and step == 0),
                                             stop=(k == K6 - 1 and step == 2))
                    last.then_inc(kr_done, 1)

            pe.wait_ge(wqk_step, 4)
            node_columns(wqk_hi, wqk_lo, 2 * R * H)
            pe.wait_ge(y_v, K6 * NRG)
            node_rows(wqk_hi, wqk_lo, 2 * R * H)
            pe.wait_ge(y_lo, K6 * NRG + 2)
            for c in range(2):
                cc = C_O + c
                pe.wait_ge(w_lo_done, cc + 1)
                with pe.Fori(0, NB // 2) as ii:
                    for j in range(2):
                        pe.wait_ge(g_free, 4 * NB + c * NB + 2 * ii + j + 1)
                        product(cc, yt_hi, yt_lo, 2 * ii + j, 6 + j).then_inc(g_done, 1)

            pe.wait_ge(tab_in, 16)

            def count_window(w, count, first):
                def tile(jj, start, stop):
                    pe.wait_ge(oh_rdy, first + jj + 1)
                    for u in range(2):
                        slot = (first + jj) % (OHS // 2) * 2 + u
                        for q in range(3):
                            last = pe.matmul(ps[:, q, 0:ND // 3], oh_k[0:ET, ds(slot, 1), :].rearrange("p o n -> p (o n)"),
                                             oh_s[0:ET, ds(slot, 1), q * ND // 3:(q + 1) * ND // 3].rearrange("p o n -> p (o n)"),
                                             start=start and u == 0, stop=stop and u == 1, skip_group_check=True)
                    last.then_inc(oh_free, 1)

                pe.wait_ge(c_free, w + 1)
                tile(0, True, False)
                with pe.Fori(1, count - 1) as jj:
                    tile(jj, False, False)
                tile(count - 1, False, True)

            for p0, p1, chunk in w1_segments():
                for c in chunk:
                    if c is not None:
                        pe.wait_ge(w_lo_done, C_X + c + 1)
                with pe.Fori(p0, p1) as wi:
                    _, count, first = window(pe, 2 * wi, False)
                    for jw in range(2):
                        w = 2 * wi + jw
                        count_window(w, count, first)
                        if chunk[jw] is not None:
                            for j in range(2):
                                pe.wait_ge(g_free, 6 * NB + 2 * w + j + 1)
                                product(C_X + chunk[jw], xt_hi, xt_lo, 2 * w + j - NB * chunk[jw], 6 + j).then_inc(g_done, 1)
                        if jw == 0:
                            _, count, first = window(pe, w + 1, False)
                        pe.wait_ge(c_free, w + 2)
                        for g in range(3):
                            pe.wait_ge(ct_done, 3 * w + g + 1)
                            for i in range(4 * g, min(4 * g + 4, NB)):
                                n = min(P, ND - i * P)
                                last = pe.transpose(ps[0:n, 3 + g, (i - 4 * g) * WK:(i - 4 * g + 1) * WK], c_row[0:WK, i * P:i * P + n], ident[0:WK, 0:WK])
                            last.then_inc(ct_tr, 1)

            def last_products(v0, v1):
                with pe.Fori(v0, v1) as v:
                    for j in range(2):
                        pe.wait_ge(g_free, 6 * NB + 2 * v + j + 1)
                        product(C_X + 2 * R - 1, xt_hi, xt_lo, 2 * v + j - NB * (2 * R - 1), 6 + j).then_inc(g_done, 1)

            pe.wait_ge(w_lo_done, C_X + 2 * R)
            last_products(PW, PW + 1)
            pe.wait_ge(mk_step, 5 * NW + 5)
            for h in range(H):
                last = pe.transpose(ps[0:NW, 0, h * WK:(h + 1) * WK], mkt[0:WK, h, :], ident[0:WK, 0:WK])
            last.then_inc(t_tr, 1)
            last_products(PW + 1, PW + NB // 2)

            pe.wait_ge(one_done, 2)

            def unit_products(h, r, s, j, first, last_unit):
                rows = xrh[h % 2][:, r, :, :]
                lo = rows[:, ds(s, 1), 0:HD].rearrange("p o n -> p (o n)")
                hi = rows[:, ds(s, 1), HD:2 * HD + 1].rearrange("p o n -> p (o n)")
                for b in range(NDB):
                    o = b % 2 * (HD + 1)
                    out_hi, out_lo = ps[:, b // 2, o:o + HD + 1], ps[:, b // 2, o:o + HD]
                    p_hi, p_lo = ph[j][:, b * DB:b * DB + P], pl[j][:, b * DB:b * DB + P]
                    pe.matmul(out_hi, p_hi, hi, start=(first and b % 2 == 0), stop=False, skip_group_check=True)
                    pe.matmul(out_lo, p_hi, lo, start=False, stop=False, skip_group_check=True)
                    mm = pe.matmul(out_hi, p_lo, hi, start=False, stop=last_unit, skip_group_check=True)
                mm.then_inc(mm_done, 1)

            for h in range(H):
                pe.wait_ge(xrh_in[h % 2], 16 * (h // 2 + 1))
                if h >= 1:
                    pe.wait_ge(he_done, h)
                for r in range(R):
                    for s in range(2 if r == 0 else 0):
                        pe.wait_ge(plo_done, (h * R + r) * NB + s + 3)
                        unit_products(h, r, s, s, s == 0, False)
                    with pe.Fori(1 if r == 0 else 0, NB // 2) as ss:
                        for j in range(2):
                            pe.wait_ge(plo_done, (h * R + r) * NB + 2 * ss + j + 3)
                            unit_products(h, r, 2 * ss + j, j, False, False)

            pe.wait_ge(he_done, H)
            pe.wait_ge(pad_done, 1)
            with pe.Fori(0, NDB // 2) as ii:
                for j in range(2):
                    b = 2 * ii + j
                    pe.wait_ge(hn_in[j], 16 * ii + 16)
                    for hf in range(2):
                        pe.wait_ge(tl_done, 2 * NB + 2 * b + hf + 1)
                        for k in range(3):
                            last = pe.transpose(ps[:, 2 * j + hf, k * DB:(k + 1) * DB], hn[j][0:DB, (3 * hf + k) * P:(3 * hf + k + 1) * P],
                                                ident[0:DB, 0:DB])
                        last.then_inc(tr_done, 1)
            pe.wait_ge(tl_done, 4 * NB + 4)
            node_rows(wqk2_hi, wqk2_lo, 2 * R)
            node_columns(wqk2_hi, wqk2_lo, 2 * R)
            for m in range(2 * R):
                cc = C_2 + m
                pe.wait_ge(w_lo_done, cc + 1)
                with pe.Fori(0, NB // 2) as ii:
                    for j in range(2):
                        pe.wait_ge(g_free, 12 * NB + m * NB + 2 * ii + j + 1)
                        product(cc, xt_hi, xt_lo, 2 * ii + j, 6 + j).then_inc(g_done, 1)
                if m == 2 * R - 2:
                    pe.wait_ge(mk2_step, 2 * NW + 4)
                    pe.wait_ge(kr_out, 2 * NRG)
                    pe.transpose(ps[0:NW, 0, 0:WK], mkt[0:WK, 0, :], ident[0:WK, 0:WK]).then_inc(t_tr, 1)

            pe.wait_ge(one_done, 4)
            pe.wait_ge(t_step, 16)

            def unit_products2(g, r, s, j, first):
                rows = x2[r]

                def cols(a, b):
                    return rows[:, ds(s, 1), a:b].rearrange("p o n -> p (o n)")

                for b in range(2):
                    bank = 4 * (g % 2) + 2 * b
                    p_hi, p_lo = ph2[j][:, b * DB:b * DB + P], pl2[j][:, b * DB:b * DB + P]
                    for p, off, n1 in ((p_hi, D, 1), (p_hi, 0, 0), (p_lo, D, 1)):
                        start = first and p is p_hi and n1 == 1
                        pe.matmul(ps[:, bank, 0:CW], p, cols(off, off + CW), start=start, stop=False, skip_group_check=True)
                        mm = pe.matmul(ps[:, bank + 1, 0:CW + n1], p, cols(off + CW, off + D + n1), start=start, stop=False, skip_group_check=True)
                mm.then_inc(mm_done, 1)

            for g in range(NG):
                if g >= 2:
                    pe.wait_ge(o_step, 8 * (g - 1))
                if g == 1:
                    pe.wait_ge(g_free, 18 * NB + 2)
                for r in range(R):
                    if g == 0:
                        pe.wait_ge(x2_in[r], 16)
                        if r == 1:
                            pe.wait_ge(one_done, 2 + R + 1)
                    n0 = H * R * NB + (g * R + r) * NB
                    for s in range(2 if r == 0 else 0):
                        pe.wait_ge(plo_done, n0 + s + 3)
                        unit_products2(g, r, s, s, s == 0)
                    with pe.Fori(1 if r == 0 else 0, NB // 2) as ss:
                        for j in range(2):
                            pe.wait_ge(plo_done, n0 + 2 * ss + j + 3)
                            unit_products2(g, r, 2 * ss + j, j, False)

            pe.wait_ge(wf_done, 1)
            pe.wait_ge(o_step, 8 * NG)

            def ffn_product(b):
                j = b % 2
                pe.wait_ge(f_cp, b + 1)
                if b >= 2:
                    pe.wait_ge(f_out, 2 * (b - 1))
                for hf in range(2):
                    for k in range(K6):
                        mm = pe.matmul(ps[0:DB, 2 + 2 * j + hf, 0:CW], fqt[j][:, k, 0:DB], wf16[:, k, hf * CW:(hf + 1) * CW],
                                       start=(k == 0), stop=(k == K6 - 1))
                mm.then_inc(f_mm, 1)

            for b in range(NDB):
                pe.wait_ge(f_step, 4 * b + 4)
                if b >= 2:
                    pe.wait_ge(f_cp, b - 1)
                for k in range(K6):
                    last = pe.transpose(ps16[:, b % 2, k * DB:(k + 1) * DB], fq[b % 2][0:DB, k * P:(k + 1) * P], ident16[0:DB, 0:DB])
                last.then_inc(f_tr, 1)
                if b >= 1:
                    ffn_product(b - 1)
            ffn_product(NDB - 1)



_INS = ["x", "src", "dst", "edge_type_3", "L0_gnn_W1", "L0_gnn_q1", "L0_gnn_k1", "L0_gnn_b1", "L0_gnn_W2", "L0_gnn_q2",
        "L0_gnn_k2", "L0_gnn_b2", "L0_mix_W_qkv", "L0_mix_b_qkv", "L0_mix_W_out", "L0_mix_b_out", "L0_ffn_weight_t",
        "L0_ffn_bias"]


def kernel(**inputs):
    import numpy as _np
    import concourse.bacc as _bacc
    from concourse import mybir as _mybir
    from concourse.bass_utils import run_bass_kernel_spmd as _run

    nc = _bacc.Bacc("TRN2", target_bir_lowering=False, num_devices=1)
    arrays, args = {}, []
    for name in _INS:
        a = _np.asarray(inputs[name])
        a = _np.ascontiguousarray(a)
        if a.dtype == _np.int8:
            a = a.view(_np.int32)
        arrays[f"in_{name}"] = a
        args.append(nc.dram_tensor(f"in_{name}", a.shape, _mybir.dt.from_np(a.dtype), kind="ExternalInput").ap())
    for name in ("W1", "W2"):
        a = _np.ascontiguousarray(arrays[f"in_L0_gnn_{name}"].transpose(0, 2, 1))
        arrays[f"in_{name}t"] = a
        args.append(nc.dram_tensor(f"in_{name}t", a.shape, F32, kind="ExternalInput").ap())
    out = nc.dram_tensor("out_x", (N, D), F32, kind="ExternalOutput").ap()
    build(nc, *args, out)
    r = _run(nc, [arrays], core_ids=[0])
    return r.results[0]["out_x"]
```
